# Optimizing a Trainium2 kernel written in Bass

```python
import numpy as np
import jax
import jax.numpy as jnp

def _softmax(x, axis=-1):
    return jax.nn.softmax(x, axis=axis)

def _gelu(x):
    return jax.nn.gelu(x, approximate=True)

def _silu(x):
    return jax.nn.silu(x)

def _sigmoid(x):
    return jax.nn.sigmoid(x)

def _layernorm(x, axis=-1, eps=1e-05):
    m = jnp.mean(x, axis=axis, keepdims=True)
    v = jnp.var(x, axis=axis, keepdims=True)
    return (x - m) / jnp.sqrt(v + eps)

def _scatter_add(tgt, idx, src, axis=0):
    return tgt.at[idx].add(src)

def _segment_sum(src, seg, n):
    return jax.ops.segment_sum(src, seg, n)
kernel_name = 'mk_flamingo_gated_d2_seqx_r4_75753f'

def setup_inputs(seed: int=0):
    np.random.seed(seed)
    _w = jnp.asarray

    def _rec_inputs():
        import jax
        import jax.numpy as jnp
        _rk = jax.random.key(seed)
        x = -0.0003929 + 0.9999 * jax.random.normal(jax.random.fold_in(_rk, 1), (4, 512, 256), jnp.float32)
        _lenS = 512 - jax.random.randint(jax.random.fold_in(_rk, 7), (4,), 0, max(1, 512 // 4) + 1, jnp.int32)
        _lenS2 = 64 - jax.random.randint(jax.random.fold_in(_rk, 8), (4,), 0, max(1, 64 // 4) + 1, jnp.int32)
        _ctx_768P = jax.random.normal(jax.random.fold_in(_rk, 11), (4, 16, 192), jnp.float32)
        _ctx_768c = jax.random.dirichlet(jax.random.fold_in(_rk, 511), 0.3 * jnp.ones((16,), jnp.float32), (4, 64))
        _ctx_768t = jnp.einsum('bsk,bkd->bsd', _ctx_768c, _ctx_768P)
        _ctx_768t = _ctx_768t * jax.lax.rsqrt(jnp.mean(jnp.square(_ctx_768t)) + 1e-12) * 0.953939
        ctx_768 = -0.00055796 + 0.999787 * (_ctx_768t + 0.3 * jax.random.normal(jax.random.fold_in(_rk, 611), (4, 64, 192), jnp.float32))
        _g = jax.random.normal(jax.random.fold_in(_rk, 9001), (2, 2), jnp.float32)
        _g = jnp.sign(_g) * jnp.maximum(jnp.abs(_g), 1.0) + (_g == 0) * 1.0
        g_xattn = _g[0]
        g_ffn = _g[1]
        return (x, ctx_768, g_xattn, g_ffn)
    x, ctx_768, g_xattn, g_ffn = _rec_inputs()

    def _L0_xattn_setup():
        import jax, jax.numpy as jnp
        import numpy as np
        IMAGE_DIM = 256
        TEXT_DIM = 192
        NUM_HEADS = 16
        HEAD_DIM = IMAGE_DIM // NUM_HEADS
        key = jax.random.key(seed)
        ks = jax.random.split(key, 14)
        B, N, M = (4, 1024, 128)
        s_img = 1.0 / np.sqrt(IMAGE_DIM)
        s_txt = 1.0 / np.sqrt(TEXT_DIM)
        s_ff = 1.0 / np.sqrt(2 * IMAGE_DIM)
        return {'x': jax.random.normal(ks[0], (B, N, IMAGE_DIM), jnp.float32), 'y': jax.random.normal(ks[1], (B, M, TEXT_DIM), jnp.float32), 'Wq': jax.random.normal(ks[2], (IMAGE_DIM, IMAGE_DIM), jnp.float32) * s_img, 'bq': jax.random.normal(ks[3], (IMAGE_DIM,), jnp.float32) * s_img, 'Wk': jax.random.normal(ks[4], (TEXT_DIM, IMAGE_DIM), jnp.float32) * s_txt, 'bk': jax.random.normal(ks[5], (IMAGE_DIM,), jnp.float32) * s_txt, 'Wv': jax.random.normal(ks[6], (TEXT_DIM, IMAGE_DIM), jnp.float32) * s_txt, 'bv': jax.random.normal(ks[7], (IMAGE_DIM,), jnp.float32) * s_txt, 'W1': jax.random.normal(ks[8], (IMAGE_DIM, 2 * IMAGE_DIM), jnp.float32) * s_img, 'b1': jax.random.normal(ks[9], (2 * IMAGE_DIM,), jnp.float32) * s_img, 'W2': jax.random.normal(ks[10], (2 * IMAGE_DIM, IMAGE_DIM), jnp.float32) * s_ff, 'b2': jax.random.normal(ks[11], (IMAGE_DIM,), jnp.float32) * s_ff}
    _L0_xattn_all = _L0_xattn_setup()
    _L0_xattn_in = {k: v for k, v in _L0_xattn_all.items() if k in ('Wq', 'bq', 'Wk', 'bk', 'Wv', 'bv', 'W1', 'b1', 'W2', 'b2')}
    del _L0_xattn_all

    def _L0_ffn_setup():
        import jax, jax.numpy as jnp
        import numpy as np
        B, S, DIM, FFN, E = (4, 512, 256, 1024, 8)
        key = jax.random.key(seed)
        k0, k1, k2, k3 = jax.random.split(key, 4)
        scale = 0.02
        return {'hidden_states': jax.random.normal(k0, (B, S, DIM), jnp.float32), 'router_w': jax.random.normal(k1, (DIM, E), jnp.float32) * scale, 'router_b': jnp.zeros((E,), jnp.float32), 'w1': jax.random.normal(k2, (E, DIM, 2 * FFN), jnp.float32) * scale, 'w2': jax.random.normal(k3, (E, FFN, DIM), jnp.float32) * scale}
    _L0_ffn_all = _L0_ffn_setup()
    _L0_ffn_in = {k: v for k, v in _L0_ffn_all.items() if k in ('router_w', 'router_b', 'w1', 'w2')}
    del _L0_ffn_all

    def _L1_xattn_setup():
        import jax, jax.numpy as jnp
        import numpy as np
        QUERY_DIM = 256
        KEY_DIM = 192
        NUM_HEADS = 16
        HEAD_DIM = QUERY_DIM // NUM_HEADS
        SCALE = HEAD_DIM ** (-0.5)
        key = jax.random.key(seed)
        ks = jax.random.split(key, 11)
        B, Nq, Nk = (4, 1024, 256)
        s_q = QUERY_DIM ** (-0.5)
        s_k = KEY_DIM ** (-0.5)
        return {'query': jax.random.normal(ks[0], (B, Nq, QUERY_DIM), jnp.float32), 'key': jax.random.normal(ks[1], (B, Nk, KEY_DIM), jnp.float32), 'value': jax.random.normal(ks[2], (B, Nk, KEY_DIM), jnp.float32), 'Wq': jax.random.normal(ks[3], (QUERY_DIM, QUERY_DIM), jnp.float32) * s_q, 'bq': jnp.zeros((QUERY_DIM,), jnp.float32), 'Wk': jax.random.normal(ks[4], (KEY_DIM, QUERY_DIM), jnp.float32) * s_k, 'bk': jnp.zeros((QUERY_DIM,), jnp.float32), 'Wv': jax.random.normal(ks[5], (KEY_DIM, QUERY_DIM), jnp.float32) * s_k, 'bv': jnp.zeros((QUERY_DIM,), jnp.float32), 'Wo': jax.random.normal(ks[6], (QUERY_DIM, QUERY_DIM), jnp.float32) * s_q, 'bo': jnp.zeros((QUERY_DIM,), jnp.float32)}
    _L1_xattn_all = _L1_xattn_setup()
    _L1_xattn_in = {k: v for k, v in _L1_xattn_all.items() if k in ('Wq', 'bq', 'Wk', 'bk', 'Wv', 'bv', 'Wo', 'bo')}
    del _L1_xattn_all

    def _L1_ffn_setup():
        import jax, jax.numpy as jnp
        import numpy as np
        HIDDEN = 256
        INNER = 1024

        def _weight_quant(w):
            scale = 1.0 / jnp.clip(jnp.mean(jnp.abs(w)), 1e-05)
            wq = jnp.clip(jnp.round(w * scale), -1.0, 1.0) / scale
            return w + jax.lax.stop_gradient(wq - w)

        def _act_quant(x):
            scale = 127.0 / jnp.clip(jnp.max(jnp.abs(x), axis=-1, keepdims=True), 1e-05)
            xq = jnp.clip(jnp.round(x * scale), -128.0, 127.0) / scale
            return x + jax.lax.stop_gradient(xq - x)

        def _bitlinear(x, w):
            return jnp.einsum('bsi,oi->bso', _act_quant(x), _weight_quant(w))
        key = jax.random.key(seed)
        k0, k1, k2, k3 = jax.random.split(key, 4)
        x = jax.random.normal(k0, (4, 512, HIDDEN), dtype=jnp.float32)
        w_gate = jax.random.normal(k1, (INNER, HIDDEN), dtype=jnp.float32) / np.sqrt(HIDDEN)
        w_up = jax.random.normal(k2, (INNER, HIDDEN), dtype=jnp.float32) / np.sqrt(HIDDEN)
        w_down = jax.random.normal(k3, (HIDDEN, INNER), dtype=jnp.float32) / np.sqrt(INNER)
        return {'x': x, 'w_gate': w_gate, 'w_up': w_up, 'w_down': w_down}
    _L1_ffn_all = _L1_ffn_setup()
    _L1_ffn_in = {k: v for k, v in _L1_ffn_all.items() if k in ('w_gate', 'w_up', 'w_down')}
    del _L1_ffn_all
    return {'x': x, 'ctx_768': ctx_768, 'g_xattn': g_xattn, 'g_ffn': g_ffn, 'L0_xattn_Wq': _L0_xattn_in['Wq'], 'L0_xattn_bq': _L0_xattn_in['bq'], 'L0_xattn_Wk': _L0_xattn_in['Wk'], 'L0_xattn_bk': _L0_xattn_in['bk'], 'L0_xattn_Wv': _L0_xattn_in['Wv'], 'L0_xattn_bv': _L0_xattn_in['bv'], 'L0_xattn_W1': _L0_xattn_in['W1'], 'L0_xattn_b1': _L0_xattn_in['b1'], 'L0_xattn_W2': _L0_xattn_in['W2'], 'L0_xattn_b2': _L0_xattn_in['b2'], 'L0_ffn_router_w': _L0_ffn_in['router_w'], 'L0_ffn_router_b': _L0_ffn_in['router_b'], 'L0_ffn_w1': _L0_ffn_in['w1'], 'L0_ffn_w2': _L0_ffn_in['w2'], 'L1_xattn_Wq': _L1_xattn_in['Wq'], 'L1_xattn_bq': _L1_xattn_in['bq'], 'L1_xattn_Wk': _L1_xattn_in['Wk'], 'L1_xattn_bk': _L1_xattn_in['bk'], 'L1_xattn_Wv': _L1_xattn_in['Wv'], 'L1_xattn_bv': _L1_xattn_in['bv'], 'L1_xattn_Wo': _L1_xattn_in['Wo'], 'L1_xattn_bo': _L1_xattn_in['bo'], 'L1_ffn_w_gate': _L1_ffn_in['w_gate'], 'L1_ffn_w_up': _L1_ffn_in['w_up'], 'L1_ffn_w_down': _L1_ffn_in['w_down']}

def reference(x, ctx_768, g_xattn, g_ffn, L0_xattn_Wq, L0_xattn_bq, L0_xattn_Wk, L0_xattn_bk, L0_xattn_Wv, L0_xattn_bv, L0_xattn_W1, L0_xattn_b1, L0_xattn_W2, L0_xattn_b2, L0_ffn_router_w, L0_ffn_router_b, L0_ffn_w1, L0_ffn_w2, L1_xattn_Wq, L1_xattn_bq, L1_xattn_Wk, L1_xattn_bk, L1_xattn_Wv, L1_xattn_bv, L1_xattn_Wo, L1_xattn_bo, L1_ffn_w_gate, L1_ffn_w_up, L1_ffn_w_down):
    import jax
    import jax.numpy as jnp

    def _L0_xattn_ref(x, y, Wq, bq, Wk, bk, Wv, bv, W1, b1, W2, b2):
        import jax, jax.numpy as jnp
        import numpy as np
        IMAGE_DIM = 256
        TEXT_DIM = 192
        NUM_HEADS = 16
        HEAD_DIM = IMAGE_DIM // NUM_HEADS
        B, N, _ = x.shape
        M = y.shape[1]
        q = (x @ Wq + bq).reshape(B, N, NUM_HEADS, HEAD_DIM)
        k = (y @ Wk + bk).reshape(B, M, NUM_HEADS, HEAD_DIM)
        v = (y @ Wv + bv).reshape(B, M, NUM_HEADS, HEAD_DIM)
        scale = 1.0 / np.sqrt(HEAD_DIM)
        scores = jnp.einsum('bnhd,bmhd->bhnm', q, k) * scale
        attn = jax.nn.softmax(scores, axis=-1)
        out = jnp.einsum('bhnm,bmhd->bnhd', attn, v).reshape(B, N, IMAGE_DIM)
        h = jax.nn.relu(out @ W1 + b1)
        return h @ W2 + b2

    def _L0_ffn_ref(hidden_states, router_w, router_b, w1, w2):
        import jax, jax.numpy as jnp
        import numpy as np
        B, S, DIM, FFN, E = (4, 512, 256, 1024, 8)
        b, s, d = hidden_states.shape
        x = hidden_states.reshape(-1, d)
        logits = x @ router_w + router_b
        route = jax.nn.softmax(logits, axis=1)
        max_prob = jnp.max(route, axis=1, keepdims=True)
        max_ind = jnp.argmax(route, axis=1)
        out = jnp.zeros_like(x)
        num_experts = w1.shape[0]
        for e in range(num_experts):
            h = x @ w1[e]
            a, g = jnp.split(h, 2, axis=1)
            y = jax.nn.silu(a) * g @ w2[e]
            out = jnp.where((max_ind == e)[:, None], y, out)
        out = out * max_prob
        return out.reshape(b, s, d)

    def _L1_xattn_ref(query, key, value, Wq, bq, Wk, bk, Wv, bv, Wo, bo):
        import jax, jax.numpy as jnp
        import numpy as np
        QUERY_DIM = 256
        KEY_DIM = 192
        NUM_HEADS = 16
        HEAD_DIM = QUERY_DIM // NUM_HEADS
        SCALE = HEAD_DIM ** (-0.5)
        B, Nq, _ = query.shape
        Nk = key.shape[1]
        q = (query @ Wq + bq).reshape(B, Nq, NUM_HEADS, HEAD_DIM).transpose(0, 2, 1, 3)
        k = (key @ Wk + bk).reshape(B, Nk, NUM_HEADS, HEAD_DIM).transpose(0, 2, 1, 3)
        v = (value @ Wv + bv).reshape(B, Nk, NUM_HEADS, HEAD_DIM).transpose(0, 2, 1, 3)
        attn = jnp.einsum('bhqd,bhkd->bhqk', q, k) * SCALE
        attn = jax.nn.softmax(attn, axis=-1)
        out = jnp.einsum('bhqk,bhkd->bhqd', attn, v)
        out = out.transpose(0, 2, 1, 3).reshape(B, Nq, QUERY_DIM)
        return out @ Wo + bo

    def _L1_ffn_ref(x, w_gate, w_up, w_down):
        import jax, jax.numpy as jnp
        import numpy as np
        HIDDEN = 256
        INNER = 1024

        def _weight_quant(w):
            scale = 1.0 / jnp.clip(jnp.mean(jnp.abs(w)), 1e-05)
            wq = jnp.clip(jnp.round(w * scale), -1.0, 1.0) / scale
            return w + jax.lax.stop_gradient(wq - w)

        def _act_quant(x):
            scale = 127.0 / jnp.clip(jnp.max(jnp.abs(x), axis=-1, keepdims=True), 1e-05)
            xq = jnp.clip(jnp.round(x * scale), -128.0, 127.0) / scale
            return x + jax.lax.stop_gradient(xq - x)

        def _bitlinear(x, w):
            return jnp.einsum('bsi,oi->bso', _act_quant(x), _weight_quant(w))
        gate = jax.nn.silu(_bitlinear(x, w_gate))
        up = _bitlinear(x, w_up)
        return _bitlinear(gate * up, w_down)
    x = x + jnp.tanh(g_xattn[0]) * _L0_xattn_ref(_layernorm(x, axis=-1), ctx_768, L0_xattn_Wq, L0_xattn_bq, L0_xattn_Wk, L0_xattn_bk, L0_xattn_Wv, L0_xattn_bv, L0_xattn_W1, L0_xattn_b1, L0_xattn_W2, L0_xattn_b2)
    x = x + jnp.tanh(g_ffn[0]) * _L0_ffn_ref(_layernorm(x, axis=-1), L0_ffn_router_w, L0_ffn_router_b, L0_ffn_w1, L0_ffn_w2)
    x = x + jnp.tanh(g_xattn[1]) * _L1_xattn_ref(_layernorm(x, axis=-1), ctx_768, ctx_768, L1_xattn_Wq, L1_xattn_bq, L1_xattn_Wk, L1_xattn_bk, L1_xattn_Wv, L1_xattn_bv, L1_xattn_Wo, L1_xattn_bo)
    x = x + jnp.tanh(g_ffn[1]) * _L1_ffn_ref(_layernorm(x, axis=-1), L1_ffn_w_gate, L1_ffn_w_up, L1_ffn_w_down)
    return x

_drawn_inputs = setup_inputs


def setup_inputs(seed=0):
    import zlib

    import numpy as np

    out = dict(_drawn_inputs(seed))
    spreads = {'g_ffn': (-1.0, 0.6),
     'L0_ffn_router_b': (0.0, 0.8),
     'L1_xattn_bq': (0.0, 2.0),
     'L1_xattn_bk': (0.0, 2.0),
     'L1_xattn_bv': (0.0, 0.8),
     'L1_xattn_bo': (0.0, 0.8)}
    factors = {'L0_xattn_bq': 8.0,
     'L0_xattn_bk': 64.0,
     'L0_ffn_router_w': 8.0,
     'L0_ffn_w1': 8.0,
     'L0_ffn_w2': 8.0,
     'L1_xattn_Wq': 2.906,
     'L1_xattn_Wk': 2.797,
     'L1_ffn_w_gate': 4.623,
     'L1_ffn_w_up': 4.439,
     'L1_ffn_w_down': 4.457}
    for name, (base, spread) in spreads.items():
        noise = np.random.default_rng([zlib.crc32(name.encode()), seed]).standard_normal(out[name].shape)
        drawn = base * np.exp(spread * noise) if base else spread * noise
        out[name] = jnp.asarray(drawn.astype(out[name].dtype))
    for name, factor in factors.items():
        out[name] = (out[name] * factor).astype(out[name].dtype)
    return out
```

```python
from contextlib import ExitStack

import numpy as np
import concourse.bass as bass
from concourse import mybir

F32 = mybir.dt.float32
BF16 = mybir.dt.bfloat16
I32 = mybir.dt.int32
U32 = mybir.dt.uint32
ALU = mybir.AluOpType
ACT = mybir.ActivationFunctionType
AX = mybir.AxisListType.X

P = 128
B, N, D = 4, 512, 256
M, C = 64, 192
H, HD = 16, 16
TB = N // P
NT = B * TB
DK = D // P
HC = P // HD
PAIRS = H // 2
PW = 2 * HD + 2
F1 = 2 * D
FK = F1 // P
E, FE = 8, 1024
EK = FE // P
SLOT_TILES = NT + E - 1
SLOTS = SLOT_TILES * P
INNER = 1024
IK = INNER // P
EPS = 1e-5
QSCALE = float(HD) ** -0.5
ROUND = 1.5 * 2.0 ** 23


def flamingo(nc, inp, out, slots_x, slots_y):
    with ExitStack() as ctx:
        def sb(name, shape, dt=F32):
            return ctx.enter_context(nc.sbuf_tensor(name, shape, dt))

        def sem(name):
            return ctx.enter_context(nc.semaphore(name))

        def flat(ap):
            return ap.rearrange("p a b -> p (a b)")

        bank = [ctx.enter_context(nc.psum_tensor(f"bank{i}", [P, 512], F32)) for i in range(8)]
        s_bank = [bank[0:2], bank[2:4]]
        t_bank = bank[4:6]
        x_bank = bank[6:8]

        ident = sb("ident", [P, P])
        ident_b = sb("ident_b", [P, P], BF16)
        ones = sb("ones", [P, P])
        before = sb("before", [P, P])
        head_mask = sb("head_mask", [P, HC])
        minus_half = sb("minus_half", [P, TB])
        eps = sb("eps", [P, TB])
        expert_no = sb("expert_no", [P, E])
        expert_no8 = sb("expert_no8", [P, E])
        tile_edge = sb("tile_edge", [P, NT])
        slot_tile_no = sb("slot_tile_no", [P, SLOT_TILES])
        zeros = sb("zeros", [P, D])

        x_res = sb("x_res", [P, NT + TB, D])
        xn_all = sb("xn_all", [P, NT, D])
        xn = sb("xn", [P, TB, D])
        xn_t = sb("xn_t", [P, DK, N])
        stats = sb("stats", [P, TB, 6])
        halves = sb("halves", [P, TB])
        mv = sb("mv", [P, TB, 2])
        var_eps = sb("var_eps", [P, TB])
        rstd = sb("rstd", [P, TB])

        ctx_rows = sb("ctx_rows", [P, 2, C])
        ctx_ta = sb("ctx_ta", [P, B, 2, M])
        ctx_tb = sb("ctx_tb", [C - P, B, 2, M])
        vec_rows = sb("vec_rows", [12, P])
        vecs = sb("vecs", [P, 12])
        bq_s = sb("bq_s", [P, 2, DK])
        gates = sb("gates", [P, 4])
        tg = sb("tg", [P, 4])
        wq = [sb(f"wq{l}", [P, DK, D]) for l in range(2)]
        wka = [sb(f"wka{l}", [P, D]) for l in range(2)]
        wkb = [sb(f"wkb{l}", [C - P, D]) for l in range(2)]
        wva = [sb(f"wva{l}", [P, D]) for l in range(2)]
        wvb = [sb(f"wvb{l}", [C - P, D]) for l in range(2)]
        bv = [sb(f"bv{l}", [P, D]) for l in range(2)]
        bo = [sb(f"bo{l}", [P, D]) for l in range(2)]
        w1 = sb("w1", [P, DK, F1])
        w2 = sb("w2", [P, FK, D])
        wo = sb("wo", [P, DK, D])
        rw = sb("rw", [P, DK, E])
        rb = sb("rb", [P, E])
        k_t = sb("k_t", [P, DK, B * M])
        k_bd = sb("k_bd", [P, DK, B, HC * M])
        v_bd = [sb(f"v_bd{l}", [P, B, PAIRS, PW]) for l in range(2)]

        q_t = sb("q_t", [P, DK, N])
        s_max = sb("s_max", [P, TB, H])
        probs = sb("probs", [P, 2, H * M])
        probs_t = sb("probs_t", [P, 2, PAIRS, P])
        o_rcp = sb("o_rcp", [P, TB, H])
        o_n = sb("o_n", [P, 2, D])
        o_t = sb("o_t", [P, DK, N])
        h1_t = sb("h1_t", [P, FK, N])

        ew1 = sb("ew1", [P, 2, DK, 2 * FE])
        ew2 = sb("ew2", [P, 2, EK, D])
        xs = sb("xs", [P, 2, D])
        xs_t = q_t[:, 0, :].rearrange("p (s k t) -> p s k t", s=2, k=DK)
        sil = probs[:, :, 0:512]
        act_t = probs_t
        ys = o_n

        logits = sb("logits", [P, NT, E])
        l_max = sb("l_max", [P, NT])
        l_exp = sb("l_exp", [P, NT, E])
        l_sum = sb("l_sum", [P, NT])
        weight = sb("weight", [P, NT])
        onehot = sb("onehot", [P, NT, E])
        first = sb("first", [P, NT])
        r_tmp = sb("r_tmp", [P, NT, E])
        count = sb("count", [P, NT, E])
        upto = sb("upto", [P, E, NT])
        more = sb("more", [P, E, NT])
        tiles_of = sb("tiles_of", [P, E])
        tile_end = sb("tile_end", [P, E])
        slot_base = sb("slot_base", [P, E])
        pos_f = sb("pos_f", [P, NT])
        pos = sb("pos", [P, NT], U32)
        past = sb("past", [P, SLOT_TILES, E])
        expert_f = sb("expert_f", [P, SLOT_TILES])
        expert_of = sb("expert_of", [P, SLOT_TILES], I32)

        bit_raw = ew1[:, 0, :, :].rearrange("p k f -> p (k f)")[:, 0:2 * IK * D].rearrange(
            "p (w a) -> p w a", w=2)
        bit_down = ew2[:, 0, :, :].rearrange("p k f -> p (k f)")
        bit_q = ew1[:, 1, 0, 0:IK * D // 2].bitcast(BF16)
        w_sum = sb("w_sum", [P, 3])
        w_mean = sb("w_mean", [P, 3])
        w_inv = sb("w_inv", [P, 3])
        gate_t = sb("gate_t", [P, DK, INNER], BF16)
        up_t = sb("up_t", [P, DK, INNER], BF16)
        down_t = sb("down_t", [P, IK, D], BF16)
        wd_g = sb("wd_g", [P, 1])

        x_q = xs[:, 0, :].bitcast(BF16).rearrange("p (s d) -> p s d", s=2)
        x_qt = xs[:, 1, :].bitcast(BF16).rearrange("p (s k t) -> p s k t", s=2, k=DK)
        sil_g = probs
        h_f = probs_t[:, :, :, :].rearrange("p s k t -> p s (k t)")
        h_q = flat(h1_t[:, 0:2, :]).bitcast(BF16).rearrange("p (s k) -> p s k", s=2)
        h_qt = flat(h1_t[:, 2:4, :]).bitcast(BF16).rearrange("p (s k t) -> p s k t", s=2, k=IK)
        q_small = sb("q_small", [P, 2, 8])

        d_ctx, d_kv0, d_vec, d_x, d_q0, d_mlp, d_rout, d_l1, d_bit = (
            sem(n) for n in ("d_ctx", "d_kv0", "d_vec", "d_x", "d_q0", "d_mlp", "d_rout", "d_l1", "d_bit"))
        d_zero = sem("d_zero")
        p_mem, p_const, p_gate = sem("p_mem"), sem("p_const"), sem("p_gate")
        v_zero = sem("v_zero")
        a_tanh, v_bq, v_bo = sem("a_tanh"), sem("v_bq"), sem("v_bo")
        t_vec, v_vec, t_ctx, v_ctx = sem("t_vec"), sem("v_vec"), sem("t_ctx"), sem("v_ctx")
        t_k, a_k, p_kbd, t_v, v_vbd = sem("t_k"), sem("a_k"), sem("p_kbd"), sem("t_v"), sem("v_vbd")
        a_abs, t_abs, v_wm = sem("a_abs"), sem("t_abs"), sem("v_wm")
        p_tern, p_terq, t_bit, a_bit = sem("p_tern"), sem("p_terq"), sem("t_bit"), sem("a_bit")

        def ln_sems(ph):
            return {k: sem(f"ln_{k}_{ph}") for k in ("stats", "aggr", "eps", "rstd", "xn")}

        ln = {ph: ln_sems(ph) for ph in ("l0", "rt", "l1", "ff")}
        att = [{k: sem(f"{k}_l{l}") for k in (
            "t_xt", "a_xt", "t_q", "a_q", "t_s", "v_max", "v_sub", "a_exp", "t_pt", "v_pt", "a_pt",
            "t_o", "v_rcp", "v_o", "t_ot", "v_ot", "t_h", "a_h", "t_y", "v_y", "p_xb")} for l in range(2)]
        r_t, r_e, r_l, r_lg = sem("r_t"), sem("r_e"), sem("r_l"), sem("r_lg")
        p_keep = sem("p_keep")
        r_v, r_exp, r_cnt = sem("r_v"), sem("r_exp"), sem("r_cnt")
        r_hot, r_pos, r_exps = sem("r_hot"), sem("r_pos"), sem("r_exps")
        p_scat = sem("p_scat")
        m_w1 = [sem(f"m_w1_{i}") for i in range(2)]
        m_w2 = [sem(f"m_w2_{i}") for i in range(2)]
        m_x = [sem(f"m_x_{i}") for i in range(2)]
        m_st = [sem(f"m_st_{i}") for i in range(2)]
        m_t, m_xt, m_up, m_sil, m_act, m_dn, m_y = (
            sem(n) for n in ("m_t", "m_xt", "m_up", "m_sil", "m_act", "m_dn", "m_y"))
        g_y = [sem(f"g_y{i}") for i in range(B)]
        g_x = sem("g_x")
        f = {k: sem(f"f_{k}") for k in (
            "unit", "dunit", "max", "clip", "inv", "mul", "rnd", "xq", "t_x", "a_x", "t_gu", "a_sil", "v_h", "hmax", "hclip", "hinv",
            "hmul", "hrnd", "hq", "t_h", "a_h", "t_y", "v_y")}
        d_out = sem("d_out")

        block = ctx.enter_context(nc.Block())

        def batch_of(ap, b):
            return ap[:, bass.ds(b * TB, TB), :]

        @block.sync
        def _(sp):
            sp.dma_start(ctx_rows[:], inp["ctx_768"].rearrange("(t a) s c -> (a s) t c", t=2)).then_inc(d_ctx, 16)
            for l, s in ((0, d_kv0),):
                sp.dma_start(wka[l][:], inp[f"L{l}_xattn_Wk"][0:P, :]).then_inc(s, 16)
                sp.dma_start(wkb[l][:], inp[f"L{l}_xattn_Wk"][P:C, :]).then_inc(s, 16)
                sp.dma_start(wva[l][:], inp[f"L{l}_xattn_Wv"][0:P, :]).then_inc(s, 16)
                sp.dma_start(wvb[l][:], inp[f"L{l}_xattn_Wv"][P:C, :]).then_inc(s, 16)
            at = 0
            for name, rows in (("L0_xattn_bq", 2), ("L0_xattn_bk", 2), ("L0_xattn_b1", 4), ("L1_xattn_bq", 2),
                               ("L1_xattn_bk", 2)):
                sp.dma_start(vec_rows[at:at + rows, :], inp[name].rearrange("(m p) -> m p", p=P)).then_inc(d_vec, 16)
                at += rows
            for b in range(B):
                sp.dma_start(x_res[:, TB * b:TB * b + TB, :],
                             inp["x"][b].rearrange("(j p) d -> p j d", p=P)).then_inc(d_x, 16)
            sp.dma_start(wq[0][:], inp["L0_xattn_Wq"].rearrange("(k p) n -> p k n", p=P)).then_inc(d_q0, 16)
            sp.dma_start(gates[:, 0:2], inp["g_xattn"].partition_broadcast(P)).then_inc(d_rout, 16)
            sp.dma_start(gates[:, 2:4], inp["g_ffn"].partition_broadcast(P)).then_inc(d_rout, 16)
            sp.dma_start(bv[0][:], inp["L0_xattn_bv"].partition_broadcast(P)).then_inc(d_rout, 16)
            sp.dma_start(bv[1][:], inp["L1_xattn_bv"].partition_broadcast(P)).then_inc(d_rout, 16)
            sp.dma_start(bo[0][:], inp["L0_xattn_b2"].partition_broadcast(P)).then_inc(d_rout, 16)
            sp.dma_start(bo[1][:], inp["L1_xattn_bo"].partition_broadcast(P)).then_inc(d_rout, 16)
            sp.dma_start(rb[:], inp["L0_ffn_router_b"].partition_broadcast(P)).then_inc(d_rout, 16)
            sp.dma_start(rw[:], inp["L0_ffn_router_w"].rearrange("(k p) e -> p k e", p=P)).then_inc(d_rout, 16)
            sp.dma_start(w1[:], inp["L0_xattn_W1"].rearrange("(k p) n -> p k n", p=P)).then_inc(d_mlp, 16)
            sp.dma_start(w2[:], inp["L0_xattn_W2"].rearrange("(k p) n -> p k n", p=P)).then_inc(d_mlp, 16)
            for l, s in ((1, d_l1),):
                sp.dma_start(wka[l][:], inp[f"L{l}_xattn_Wk"][0:P, :]).then_inc(s, 16)
                sp.dma_start(wkb[l][:], inp[f"L{l}_xattn_Wk"][P:C, :]).then_inc(s, 16)
                sp.dma_start(wva[l][:], inp[f"L{l}_xattn_Wv"][0:P, :]).then_inc(s, 16)
                sp.dma_start(wvb[l][:], inp[f"L{l}_xattn_Wv"][P:C, :]).then_inc(s, 16)
            sp.dma_start(wq[1][:], inp["L1_xattn_Wq"].rearrange("(k p) n -> p k n", p=P)).then_inc(d_l1, 16)
            sp.dma_start(wo[:], inp["L1_xattn_Wo"].rearrange("(k p) n -> p k n", p=P)).then_inc(d_l1, 16)
            sp.dma_start(bit_raw[:, 0, :].rearrange("p (a i) -> p a i", a=IK),
                         inp["L1_ffn_w_gate"].rearrange("(a p) i -> p a i", p=P)).then_inc(d_bit, 16)
            sp.dma_start(bit_raw[:, 1, :].rearrange("p (a i) -> p a i", a=IK),
                         inp["L1_ffn_w_up"].rearrange("(a p) i -> p a i", p=P)).then_inc(d_bit, 16)
            sp.dma_start(bit_down.rearrange("p (a i) -> p a i", a=DK),
                         inp["L1_ffn_w_down"].rearrange("(a p) i -> p a i", p=P)).then_inc(d_bit, 16)
            sp.wait_ge(v_zero, 2)
            zero_tiles = SLOT_TILES
            sp.dma_start(slots_x.rearrange("(t p) d -> p t d", p=P),
                         zeros[:].unsqueeze(1).to_broadcast([P, zero_tiles, D])).then_inc(d_zero, 16)

            def expert_tile(t, par, again):
                e = sp.value_load(expert_of[0:1, bass.ds(t, 1)], min_val=0, max_val=E - 1)
                if again:
                    sp.wait_ge(m_up, 2 * t - 2)
                sp.dma_start(ew1[:, par, :, :], inp["L0_ffn_w1"][bass.ds(e, 1)].rearrange(
                    "o (k p) f -> p (o k) f", p=P)).then_inc(m_w1[par], 16)
                if again:
                    sp.wait_ge(m_dn, t - 1)
                sp.dma_start(xs[:, par, :], slots_x[bass.ds(t * P, P), :]).then_inc(m_x[par], 16)
                sp.dma_start(ew2[:, par, :, :], inp["L0_ffn_w2"][bass.ds(e, 1)].rearrange(
                    "o (k p) d -> p (o k) d", p=P)).then_inc(m_w2[par], 16)

            sp.wait_ge(r_exps, 1)
            sp.wait_ge(a_bit, 12)
            sp.wait_ge(p_scat, 16 * NT)
            expert_tile(0, 0, False)
            expert_tile(1, 1, False)
            with sp.Fori(1, SLOT_TILES // 2) as i:
                expert_tile(2 * i, 0, True)
                expert_tile(2 * i + 1, 1, True)
            expert_tile(SLOT_TILES - 1, 0, True)

            with sp.Fori(0, B) as b:
                sp.wait_ge(f["v_y"], TB * b + TB)
                sp.dma_start(out[bass.ds(b, 1)].rearrange("o (j p) d -> p (o j) d", p=P),
                             batch_of(x_res, b)).then_inc(d_out, 16)
            sp.wait_ge(d_out, 16 * B)

        def layer_norm_rstd(pool, s, n):
            pool.wait_ge(s["aggr"], n)
            nc.gpsimd.tensor_tensor(var_eps[:], mv[:, :, 1], eps[:], ALU.add).then_inc(s["eps"], 1)
            pool.wait_ge(s["eps"], n)
            nc.gpsimd.tensor_tensor(rstd[:], var_eps[:], minus_half[:], ALU.pow).then_inc(s["rstd"], 1)

        @block.gpsimd
        def _(pool):
            nc.gpsimd.memset(ident[:], 0.0).then_inc(p_mem, 1)
            nc.gpsimd.memset(ident_b[:], 0.0).then_inc(p_mem, 1)
            nc.gpsimd.memset(ones[:], 1.0).then_inc(p_mem, 1)
            nc.gpsimd.memset(before[:], 1.0).then_inc(p_mem, 1)
            nc.gpsimd.memset(head_mask[:], 1.0).then_inc(p_mem, 1)
            nc.gpsimd.memset(minus_half[:], -0.5).then_inc(p_mem, 1)
            nc.gpsimd.memset(eps[:], EPS).then_inc(p_mem, 1)
            nc.gpsimd.iota(expert_no[:], [[1, E]], base=0, channel_multiplier=0,
                           allow_small_or_imprecise_dtypes=True).then_inc(p_mem, 1)
            nc.gpsimd.iota(expert_no8[:], [[1, E]], base=E, channel_multiplier=0,
                           allow_small_or_imprecise_dtypes=True).then_inc(p_mem, 1)
            nc.gpsimd.iota(tile_edge[:], [[P, NT]], base=0, channel_multiplier=0,
                           allow_small_or_imprecise_dtypes=True).then_inc(p_mem, 1)
            nc.gpsimd.iota(slot_tile_no[:], [[1, SLOT_TILES]], base=0, channel_multiplier=0,
                           allow_small_or_imprecise_dtypes=True).then_inc(p_mem, 1)
            pool.wait_ge(p_mem, 11)
            nc.gpsimd.affine_select(out=ident[:], in_=ident[:], compare_op=ALU.not_equal, fill=1.0, base=0,
                                    pattern=[[-1, P]], channel_multiplier=1).then_inc(p_const, 1)
            nc.gpsimd.affine_select(out=ident_b[:], in_=ident_b[:], compare_op=ALU.not_equal, fill=1.0, base=0,
                                    pattern=[[-1, P]], channel_multiplier=1).then_inc(p_const, 1)
            nc.gpsimd.affine_select(out=before[:], in_=before[:], compare_op=ALU.is_gt, fill=0.0, base=0,
                                    pattern=[[1, P]], channel_multiplier=-1).then_inc(p_const, 1)
            nc.gpsimd.affine_select(out=head_mask[:], in_=head_mask[:], compare_op=ALU.is_ge, fill=0.0, base=0,
                                    pattern=[[-HD, HC]], channel_multiplier=1).then_inc(p_const, 1)
            pool.wait_ge(p_const, 4)
            nc.gpsimd.affine_select(out=head_mask[:], in_=head_mask[:], compare_op=ALU.is_ge, fill=0.0, base=HD - 1,
                                    pattern=[[HD, HC]], channel_multiplier=-1).then_inc(p_const, 1)
            pool.wait_ge(p_const, 5)
            layer_norm_rstd(pool, ln["l0"], 1)
            def spread_keys(l):
                for m in range(DK):
                    pool.wait_ge(a_k, DK * l + m + 1)
                    for b in range(B):
                        nc.gpsimd.tensor_tensor(
                            k_bd[:, m, b, :].rearrange("p (h s) -> p h s", h=HC),
                            k_t[:, m, b * M:b * M + M].unsqueeze(1).to_broadcast([P, HC, M]),
                            head_mask[:].unsqueeze(2).to_broadcast([P, HC, M]), ALU.mult).then_inc(p_kbd, 1)

            spread_keys(0)

            def bias_rows(l, b):
                s = att[l]
                pool.wait_ge(v_bo, 2)
                pool.wait_ge(ln["l0" if l == 0 else "l1"]["stats"], b + 1)
                pool.wait_ge(ln["l0" if l == 0 else "l1"]["xn"], b + 1)
                nc.gpsimd.tensor_tensor(batch_of(x_res, b), batch_of(x_res, b),
                                        bo[l][:].unsqueeze(1).to_broadcast([P, TB, D]), ALU.add).then_inc(s["p_xb"], 1)

            with pool.Fori(0, B) as b:
                bias_rows(0, b)
                layer_norm_rstd(pool, ln["l0"], b + 2)

            pool.wait_ge(v_wm, 3)
            raws = (bit_raw[:, 0, :], bit_raw[:, 1, :], bit_down)
            for w in range(3):
                nc.gpsimd.tensor_scalar(raws[w], raws[w], w_inv[:, w:w + 1], 1.0, ALU.mult, ALU.min).then_inc(p_tern, 1)
                pool.wait_ge(p_tern, 2 * w + 1)
                nc.gpsimd.tensor_scalar(raws[w], raws[w], -1.0, ROUND, ALU.max, ALU.add).then_inc(p_tern, 1)
                pool.wait_ge(p_tern, 2 * w + 2)
                if w >= 1:
                    pool.wait_ge(t_bit, 4 * w)
                nc.gpsimd.tensor_scalar(bit_q, raws[w], -ROUND, None, ALU.add).then_inc(p_terq, 1)

            with pool.Fori(0, B) as b:
                layer_norm_rstd(pool, ln["rt"], b + 1)
                pool.wait_ge(ln["rt"]["xn"], b + 1)
                nc.gpsimd.tensor_copy(batch_of(xn_all, b), xn[:]).then_inc(p_keep, 1)
            pool.wait_ge(p_keep, B)
            pool.wait_ge(d_zero, 16)
            pool.wait_ge(r_pos, 1)
            for t in range(NT):
                nc.gpsimd.indirect_dma_start(
                    out=slots_x[:, :], out_offset=bass.IndirectOffsetOnAxis(ap=pos[:, t:t + 1], axis=0),
                    in_=xn_all[:, t, :], in_offset=None).then_inc(p_scat, 16)

            pool.wait_ge(att[0]["t_s"], NT)
            spread_keys(1)

            pool.wait_ge(p_scat, 16 * NT)
            pool.wait_ge(m_st[0], 16 * ((SLOT_TILES + 1) // 2))
            pool.wait_ge(m_st[1], 16 * (SLOT_TILES // 2))
            for t in range(NT):
                nc.gpsimd.indirect_dma_start(
                    out=xn_all[:, t, :], out_offset=None, in_=slots_y[:, :],
                    in_offset=bass.IndirectOffsetOnAxis(ap=pos[:, t:t + 1], axis=0)).then_inc(g_y[t // TB], 16)

            layer_norm_rstd(pool, ln["l1"], 1)
            with pool.Fori(0, B) as b:
                bias_rows(1, b)
                layer_norm_rstd(pool, ln["l1"], b + 2)
            with pool.Fori(0, B) as b:
                layer_norm_rstd(pool, ln["ff"], b + 1)

        @block.tensor
        def _(pe):
            pe.wait_ge(p_const, 5)
            pe.wait_ge(d_vec, 16 * 5)
            nc.tensor.transpose(t_bank[0][:, 0:12], vec_rows[:], ident[0:12, 0:12]).then_inc(t_vec, 1)
            pe.wait_ge(d_ctx, 16)
            for t in range(2):
                nc.tensor.transpose(x_bank[0][:, P * t:P * t + P], ctx_rows[:, t, 0:P], ident[:])
            for t in range(2):
                last = nc.tensor.transpose(x_bank[1][0:C - P, P * t:P * t + P], ctx_rows[:, t, P:C], ident[:])
            last.then_inc(t_ctx, 1)
            pe.wait_ge(v_ctx, 4)
            for l in range(2):
                pe.wait_ge((d_kv0, d_l1)[l], (16 * 4, 16 * 6)[l])
                for m in range(DK):
                    if l:
                        pe.wait_ge(a_k, DK * l + m - 1)
                    nc.tensor.matmul(x_bank[m][:, 0:B * M], wka[l][:, m * P:m * P + P], ctx_ta[:, :, 0, :],
                                     start=True, stop=False)
                    nc.tensor.matmul(x_bank[m][:, 0:B * M], wkb[l][:, m * P:m * P + P], ctx_tb[:, :, 0, :],
                                     start=False, stop=True).then_inc(t_k, 1)
                for b in range(B):
                    o = s_bank[l][b // 2][:, (b % 2) * D:(b % 2) * D + D]
                    nc.tensor.matmul(o, flat(ctx_ta[:, b, :, :]), wva[l][:], start=True, stop=False)
                    last = nc.tensor.matmul(o, flat(ctx_tb[:, b, :, :]), wvb[l][:], start=False, stop=True)
                last.then_inc(t_v, 1)
            pe.wait_ge(a_abs, 3)
            pe.wait_ge(v_vec, 1)
            nc.tensor.matmul(t_bank[1][:, 0:3], ones[:], w_sum[:], start=True, stop=True).then_inc(t_abs, 1)
            pe.wait_ge(v_wm, 3)
            pe.wait_ge(v_vbd, 8)
            pe.wait_ge(a_k, 2 * DK)
            pe.wait_ge(p_kbd, DK * B)

            def attention(l, b):
                s = att[l]
                phase = ln["l0" if l == 0 else "l1"]
                pe.wait_ge(phase["xn"], b + 1)
                for k in range(DK):
                    for i in range(TB):
                        last = nc.tensor.transpose(x_bank[k][:, P * i:P * i + P], xn[:, i, k * P:k * P + P], ident[:])
                    last.then_inc(s["t_xt"], 1)
                pe.wait_ge(s["a_xt"], DK * b + DK)
                for m in range(DK):
                    for k in range(DK):
                        last = nc.tensor.matmul(x_bank[m][:], wq[l][:, k, m * P:m * P + P], xn_t[:, k, :],
                                                start=(k == 0), stop=(k == DK - 1))
                    last.then_inc(s["t_q"], 1)

                def scores(i):
                    if i == 0:
                        pe.wait_ge(s["a_q"], DK * b + DK)
                    if i >= 2:
                        pe.wait_ge(s["v_sub"], TB * b + i - 1)
                    for m in range(DK):
                        last = nc.tensor.matmul(s_bank[i % 2][m][:], q_t[:, m, P * i:P * i + P],
                                                flat(k_bd[:, m, bass.ds(b, 1), :]), start=True, stop=True)
                    last.then_inc(s["t_s"], 1)

                def turn(i):
                    pe.wait_ge(s["a_exp"], TB * b + i + 1)
                    for c in range(2):
                        for j in range(4):
                            last = nc.tensor.transpose(t_bank[c][:, P * j:P * j + P],
                                                       probs[:, i % 2, P * (4 * c + j):P * (4 * c + j + 1)], ident[:])
                        last.then_inc(s["t_pt"], 1)

                def values(i):
                    pe.wait_ge(s["v_pt"], TB * b + i + 1)
                    pe.wait_ge(s["a_pt"], TB * b + i + 1)
                    for j in range(PAIRS):
                        last = nc.tensor.matmul(x_bank[0][:, PW * j:PW * j + PW], probs_t[:, i % 2, j, :],
                                                flat(v_bd[l][:, bass.ds(b, 1), j, :]), start=True, stop=True)
                    last.then_inc(s["t_o"], 1)

                def turn_out(i):
                    pe.wait_ge(s["v_o"], TB * b + i + 1)
                    if i:
                        pe.wait_ge(s["v_ot"], TB * b + i)
                    for k in range(DK):
                        last = nc.tensor.transpose(x_bank[1][:, P * k:P * k + P], o_n[:, i % 2, k * P:k * P + P],
                                                   ident[:])
                    last.then_inc(s["t_ot"], 1)

                scores(0)
                scores(1)
                turn(0)
                scores(2)
                values(0)
                turn(1)
                scores(3)
                turn_out(0)
                values(1)
                turn(2)
                turn_out(1)
                values(2)
                turn(3)
                turn_out(2)
                values(3)
                turn_out(3)
                pe.wait_ge(s["v_ot"], TB * b + TB)
                if l == 0:
                    for m in range(FK):
                        if m >= 2:
                            pe.wait_ge(s["a_h"], FK * b + m - 1)
                        for k in range(DK):
                            last = nc.tensor.matmul(x_bank[m % 2][:], w1[:, k, m * P:m * P + P], o_t[:, k, :],
                                                    start=(k == 0), stop=(k == DK - 1))
                        last.then_inc(s["t_h"], 1)
                    pe.wait_ge(s["a_h"], FK * b + FK)
                src, w, kk = (h1_t, w2, FK) if l == 0 else (o_t, wo, DK)
                for i in range(TB):
                    if i >= 2:
                        pe.wait_ge(s["v_y"], TB * b + i - 1)
                    for k in range(kk):
                        last = nc.tensor.matmul(x_bank[i % 2][:, 0:D], src[:, k, P * i:P * i + P], w[:, k, :],
                                                start=(k == 0), stop=(k == kk - 1))
                    last.then_inc(s["t_y"], 1)
                pe.wait_ge(s["v_y"], TB * b + TB)

            pe.wait_ge(d_q0, 16)
            pe.wait_ge(d_mlp, 32)
            with pe.Fori(0, B) as b:
                attention(0, b)

            pe.wait_ge(att[0]["a_pt"], NT)
            pe.wait_ge(att[0]["v_pt"], NT)
            n = 0
            for w in range(3):
                pe.wait_ge(p_terq, w + 1)
                src = bit_q.rearrange("p (a i) -> p a i", a=(IK, IK, DK)[w])
                for c in range(4):
                    if n >= 2:
                        pe.wait_ge(a_bit, n - 1)
                    o = t_bank[n % 2][:, 0:256].bitcast(BF16)
                    for j in range(4):
                        q = 4 * c + j
                        a, i = (q % IK, q // IK) if w < 2 else (q % DK, q // DK)
                        last = nc.tensor.transpose(o[:, P * j:P * j + P], src[:, a, i * P:i * P + P], ident_b[:])
                    last.then_inc(t_bit, 1)
                    n += 1

            pe.wait_ge(d_rout, 16 * 8)
            pe.wait_ge(att[0]["v_y"], NT)
            with pe.Fori(0, B) as b:
                pe.wait_ge(ln["rt"]["xn"], b + 1)
                for k in range(DK):
                    for i in range(TB):
                        last = nc.tensor.transpose(x_bank[k][:, P * i:P * i + P], xn[:, i, k * P:k * P + P], ident[:])
                    last.then_inc(r_t, 1)
                pe.wait_ge(r_e, DK * b + DK)
                for i in range(TB):
                    for k in range(DK):
                        last = nc.tensor.matmul(s_bank[0][0][:, E * i:E * i + E], xn_t[:, k, P * i:P * i + P],
                                                rw[:, k, :], start=(k == 0), stop=(k == DK - 1))
                last.then_inc(r_l, 1)
            pe.wait_ge(r_hot, 1)
            nc.tensor.matmul(s_bank[1][0][:, 0:NT * E], before[:], flat(onehot[:]), start=True, stop=True)
            nc.tensor.matmul(s_bank[1][1][:, 0:NT * E], ones[:], flat(onehot[:]), start=True,
                             stop=True).then_inc(r_cnt, 1)
            pe.wait_ge(r_pos, 1)

            a_bank, g_bank, y_bank, r_bank = bank[0:2], bank[2:4], bank[4:6], bank[6:8]

            def rows_in(t, par, n):
                pe.wait_ge(m_x[par], 16 * (n + 1))
                for k in range(DK):
                    last = nc.tensor.transpose(r_bank[par][:, P * k:P * k + P], xs[:, par, k * P:k * P + P], ident[:])
                last.then_inc(m_t, 1)

            def expand(t, par, n, q):
                if q == 0:
                    pe.wait_ge(m_xt, t + 1)
                    pe.wait_ge(m_w1[par], 16 * (n + 1))
                if t is not 0:
                    pe.wait_ge(m_act, 2 * t - 1 + q)
                for o, base in ((a_bank[q], 0), (g_bank[q], FE)):
                    for j in range(4):
                        c0 = base + (4 * q + j) * P
                        for k in range(DK):
                            last = nc.tensor.matmul(o[:, P * j:P * j + P], ew1[:, par, k, c0:c0 + P],
                                                    xs_t[:, par, k, :], start=(k == 0), stop=(k == DK - 1))
                last.then_inc(m_up, 1)

            def contract(t, par, n, q):
                pe.wait_ge(m_act, 2 * t + q + 1)
                if q == 0:
                    pe.wait_ge(m_w2[par], 16 * (n + 1))
                    if n is not 0:
                        pe.wait_ge(m_y, t - 1)
                for j in range(4):
                    c = 4 * q + j
                    last = nc.tensor.matmul(y_bank[par][:, 0:D], act_t[:, par, c, :], ew2[:, par, c, :],
                                            start=(c == 0), stop=(c == EK - 1))
                if q == 1:
                    last.then_inc(m_dn, 1)

            def expert_tile(t, par, n, first_tile, last_tile):
                expand(t, par, n, 0)
                if not first_tile:
                    contract(t - 1, 1 - par, n if par else n - 1, 1)
                if not last_tile:
                    rows_in(t + 1, 1 - par, n + 1 if par else n)
                expand(t, par, n, 1)
                contract(t, par, n, 0)

            rows_in(0, 0, 0)
            expert_tile(0, 0, 0, True, False)
            expert_tile(1, 1, 0, False, False)
            with pe.Fori(1, SLOT_TILES // 2) as i:
                expert_tile(2 * i, 0, i, False, False)
                expert_tile(2 * i + 1, 1, i, False, False)
            expert_tile(SLOT_TILES - 1, 0, SLOT_TILES // 2, False, True)
            contract(SLOT_TILES - 1, 0, SLOT_TILES // 2, 1)

            pe.wait_ge(m_y, SLOT_TILES)
            pe.wait_ge(p_kbd, 2 * DK * B)
            with pe.Fori(0, B) as b:
                attention(1, b)

            pe.wait_ge(att[1]["v_y"], NT)

            def ff_tile(t, par):
                pe.wait_ge(f["xq"], t + 1)
                o = t_bank[0][:, 0:P].bitcast(BF16)
                for k in range(DK):
                    last = nc.tensor.transpose(o[:, P * k:P * k + P], x_q[:, par, k * P:k * P + P], ident_b[:])
                last.then_inc(f["t_x"], 1)
                pe.wait_ge(f["a_x"], t + 1)
                for c in range(2):
                    for o, w in ((bank[c], gate_t), (bank[2 + c], up_t)):
                        for k in range(DK):
                            last = nc.tensor.matmul(o[:], x_qt[:, par, k, :], w[:, k, 512 * c:512 * c + 512],
                                                    start=(k == 0), stop=(k == DK - 1))
                last.then_inc(f["t_gu"], 1)

            def ff_down(t, par):
                pe.wait_ge(f["hq"], t + 1)
                o = t_bank[1][:].bitcast(BF16)
                for k in range(IK):
                    last = nc.tensor.transpose(o[:, P * k:P * k + P], h_q[:, par, k * P:k * P + P], ident_b[:])
                last.then_inc(f["t_h"], 1)
                pe.wait_ge(f["a_h"], t + 1)
                for k in range(IK):
                    last = nc.tensor.matmul(x_bank[0][:, 0:D], h_qt[:, par, k, :], down_t[:, k, :],
                                            start=(k == 0), stop=(k == IK - 1))
                last.then_inc(f["t_y"], 1)

            with pe.Fori(0, B) as b:
                for i in range(TB):
                    ff_tile(TB * b + i, i % 2)
                    ff_down(TB * b + i, i % 2)

        @block.scalar
        def _(act):
            for l in range(2):
                act.wait_ge(v_vec, 1)
                for m in range(DK):
                    act.wait_ge(t_k, DK * l + m + 1)
                    if l:
                        act.wait_ge(p_kbd, DK * B)
                    nc.scalar.activation(k_t[:, m, :], x_bank[m][:, 0:B * M], ACT.Identity,
                                         bias=vecs[:, (2, 10)[l] + m:(2, 10)[l] + m + 1]).then_inc(a_k, 1)
                if l == 0:
                    act.wait_ge(d_rout, 16 * 8)
                    nc.scalar.activation(tg[:], gates[:], ACT.Tanh).then_inc(a_tanh, 1)
            act.wait_ge(d_bit, 48)
            for w, raw in enumerate((bit_raw[:, 0, :], bit_raw[:, 1, :], bit_down)):
                nc.scalar.activation(flat(probs[:, :, :]), raw, ACT.Abs, accum_out=w_sum[:, w:w + 1]).then_inc(a_abs, 1)
                act.wait_ge(a_abs, w + 1)

            def attention(l, b):
                s = att[l]
                for k in range(DK):
                    act.wait_ge(s["t_xt"], DK * b + k + 1)
                    nc.scalar.copy(xn_t[:, k, :], x_bank[k][:]).then_inc(s["a_xt"], 1)
                for m in range(DK):
                    act.wait_ge(s["t_q"], DK * b + m + 1)
                    nc.scalar.activation(q_t[:, m, :], x_bank[m][:], ACT.Identity, bias=bq_s[:, l, m:m + 1],
                                         scale=QSCALE).then_inc(s["a_q"], 1)

                def exps(i):
                    act.wait_ge(s["v_sub"], TB * b + i + 1)
                    nc.scalar.activation(probs[:, i % 2, :], probs[:, i % 2, :], ACT.Exp).then_inc(s["a_exp"], 1)

                def turned(i):
                    act.wait_ge(s["t_pt"], 2 * (TB * b + i) + 2)
                    nc.scalar.copy(flat(probs_t[:, i % 2, 4:8, :]), t_bank[1][:]).then_inc(s["a_pt"], 1)

                exps(0)
                exps(1)
                turned(0)
                exps(2)
                turned(1)
                exps(3)
                turned(2)
                turned(3)
                if l == 0:
                    for m in range(FK):
                        act.wait_ge(s["t_h"], FK * b + m + 1)
                        nc.scalar.activation(h1_t[:, m, :], x_bank[m % 2][:], ACT.Relu,
                                             bias=vecs[:, 4 + m:5 + m]).then_inc(s["a_h"], 1)

            act.wait_ge(v_bq, 2)
            with act.Fori(0, B) as b:
                attention(0, b)

            n = 0
            for w, dst in enumerate((gate_t, up_t, down_t)):
                flat_dst = flat(dst[:])
                for c in range(4):
                    act.wait_ge(t_bit, n + 1)
                    nc.scalar.copy(flat_dst[:, 512 * c:512 * c + 512],
                                   t_bank[n % 2][:, 0:256].bitcast(BF16)).then_inc(a_bit, 1)
                    n += 1

            with act.Fori(0, B) as b:
                for k in range(DK):
                    act.wait_ge(r_t, DK * b + k + 1)
                    nc.scalar.copy(xn_t[:, k, :], x_bank[k][:]).then_inc(r_e, 1)
            act.wait_ge(r_v, 2)
            nc.scalar.activation(l_exp[:], r_tmp[:], ACT.Exp).then_inc(r_exp, 1)

            def expert_rows(t, par):
                act.wait_ge(m_t, t + 1)
                nc.scalar.copy(flat(xs_t[:, par, :, :]), bank[6 + par][:, 0:D]).then_inc(m_xt, 1)

            def expert_gate(t, q):
                act.wait_ge(m_up, 2 * t + q + 1)
                if not (t is 0):
                    act.wait_ge(m_act, 2 * t + q - 1)
                nc.scalar.activation(sil[:, q, :], bank[q][:], ACT.Silu).then_inc(m_sil, 1)

            def expert_out(t, par, n, stored):
                act.wait_ge(m_dn, t + 1)
                if stored:
                    act.wait_ge(m_st[par], 16 * n)
                nc.scalar.copy(ys[:, par, :], bank[4 + par][:, 0:D]).then_inc(m_y, 1)
                act.wait_ge(m_y, t + 1)
                act.dma_start(slots_y[bass.ds(t * P, P), :], ys[:, par, :]).then_inc(m_st[par], 16)

            def expert_tile(t, par, n, first_tile, last_tile):
                expert_gate(t, 0)
                if not first_tile:
                    m = n if par else n - 1
                    expert_out(t - 1, 1 - par, m, not (m is 0))
                if not last_tile:
                    expert_rows(t + 1, 1 - par)
                expert_gate(t, 1)

            expert_rows(0, 0)
            expert_tile(0, 0, 0, True, False)
            expert_tile(1, 1, 0, False, False)
            with act.Fori(1, SLOT_TILES // 2) as i:
                expert_tile(2 * i, 0, i, False, False)
                expert_tile(2 * i + 1, 1, i, False, False)
            expert_tile(SLOT_TILES - 1, 0, SLOT_TILES // 2, False, True)
            expert_out(SLOT_TILES - 1, 0, SLOT_TILES // 2, True)

            with act.Fori(0, B) as b:
                attention(1, b)

            def ff_tile(t, par):
                act.wait_ge(f["t_x"], t + 1)
                nc.scalar.copy(flat(x_qt[:, par, :, :]), t_bank[0][:, 0:P].bitcast(BF16)).then_inc(f["a_x"], 1)
                act.wait_ge(f["unit"], t + 1)
                act.wait_ge(f["t_gu"], t + 1)
                for c in range(2):
                    nc.scalar.activation(sil_g[:, par, 512 * c:512 * c + 512], bank[c][:], ACT.Silu,
                                         scale=q_small[:, par, 3:4]).then_inc(f["a_sil"], 1)

            def ff_down(t, par):
                act.wait_ge(f["t_h"], t + 1)
                nc.scalar.copy(flat(h_qt[:, par, :, :]), t_bank[1][:].bitcast(BF16)).then_inc(f["a_h"], 1)

            with act.Fori(0, B) as b:
                for i in range(TB):
                    ff_tile(TB * b + i, i % 2)
                    ff_down(TB * b + i, i % 2)

        @block.vector
        def _(dve):
            nc.vector.memset(zeros[:], 0.0).then_inc(v_zero, 1)
            nc.vector.memset(x_res[:, NT:NT + TB, :], 0.0).then_inc(v_zero, 1)
            for l in range(2):
                nc.vector.memset(v_bd[l][:], 0.0).then_inc(v_zero, 1)
            dve.wait_ge(v_zero, 4)
            for l in range(2):
                nc.vector.memset(v_bd[l][0:M, :, :, 2 * HD:2 * HD + 1], 1.0).then_inc(v_zero, 1)
                nc.vector.memset(v_bd[l][M:P, :, :, 2 * HD + 1:PW], 1.0).then_inc(v_zero, 1)

            def layer_norm(s, n, b):
                for i in range(TB):
                    last = nc.vector.bn_stats(stats[:, i, :], x_res[:, bass.ds(b * TB + i, 1), :].rearrange(
                        "p o d -> p (o d)"))
                last.then_inc(s["stats"], 1)
                dve.wait_ge(s["stats"], n)
                nc.vector.tensor_copy(halves[:], stats[:, :, 0])
                for i in range(TB):
                    last = nc.vector.bn_aggr(mv[:, i, :], stats[:, i, :])
                last.then_inc(s["aggr"], 1)
                dve.wait_ge(s["aggr"], n)
                dve.wait_ge(s["rstd"], n)
                for i in range(TB):
                    last = nc.vector.tensor_scalar(
                        xn[:, i, :], x_res[:, bass.ds(b * TB + i, 1), :].rearrange("p o d -> p (o d)"),
                        mv[:, i, 0:1], rstd[:, i:i + 1], ALU.subtract, ALU.mult)
                last.then_inc(s["xn"], 1)

            dve.wait_ge(t_vec, 1)
            nc.vector.tensor_copy(vecs[:], t_bank[0][:, 0:12]).then_inc(v_vec, 1)
            dve.wait_ge(t_ctx, 1)
            for c, (dst, src) in enumerate(((ctx_ta, x_bank[0]), (ctx_tb, x_bank[1]))):
                rows = (P, C - P)[c]
                for twice in range(2):
                    nc.vector.tensor_copy(dst[:, :, twice, :], src[0:rows, 0:B * M].rearrange(
                        "p (b s) -> p b s", b=B)).then_inc(v_ctx, 1)
            dve.wait_ge(v_vec, 1)
            for l in range(2):
                nc.vector.tensor_scalar(bq_s[:, l, :], vecs[:, 8 * l:8 * l + 2], QSCALE, None, ALU.mult).then_inc(v_bq, 1)
            dve.wait_ge(d_x, 16 * B)
            layer_norm(ln["l0"], 1, 0)
            dve.wait_ge(d_rout, 16 * 8)
            dve.wait_ge(a_tanh, 1)
            for l in range(2):
                nc.vector.tensor_scalar(bo[l][:], bo[l][:], tg[:, l:l + 1], None, ALU.mult).then_inc(v_bo, 1)
            for l in range(2):
                dve.wait_ge(t_v, l + 1)
                dve.wait_ge(v_zero, 8)
                for half in range(2):
                    lo = half * M
                    for c in range(2):
                        src = s_bank[l][c][lo:lo + M, :].rearrange("p (b j a) -> p b j a", b=2, j=PAIRS)
                        bias = bv[l][lo:lo + M, :].rearrange("p (j a) -> p j a", j=PAIRS)
                        for b in range(2):
                            last = nc.vector.tensor_tensor(
                                v_bd[l][lo:lo + M, 2 * c + b, :, half * HD:half * HD + HD],
                                src[:, b, :, half * HD:half * HD + HD], bias[:, :, half * HD:half * HD + HD], ALU.add)
                        last.then_inc(v_vbd, 1)
            dve.wait_ge(t_abs, 1)
            nc.vector.tensor_scalar(w_mean[:], t_bank[1][:, 0:3], 1.0 / (INNER * D), EPS, ALU.mult,
                                    ALU.max).then_inc(v_wm, 1)
            dve.wait_ge(v_wm, 1)
            nc.vector.reciprocal(w_inv[:], w_mean[:]).then_inc(v_wm, 1)
            nc.vector.tensor_scalar(wd_g[:], w_mean[:, 2:3], tg[:, 3:4], 1.0 / 127.0, ALU.mult, ALU.mult).then_inc(v_wm, 1)

            def attention(l, b):
                s = att[l]
                phase = ln["l0" if l == 0 else "l1"]

                def scores(i):
                    g = TB * b + i
                    dve.wait_ge(s["t_s"], g + 1)
                    for m in range(DK):
                        last = nc.vector.tensor_reduce(s_max[:, i, HC * m:HC * m + HC],
                                                       s_bank[i % 2][m][:].rearrange("p (h s) -> p h s", h=HC),
                                                       AX, ALU.max)
                    last.then_inc(s["v_max"], 1)
                    dve.wait_ge(s["v_max"], g + 1)
                    if i >= 2:
                        dve.wait_ge(s["t_pt"], 2 * g - 2)
                    for m in range(DK):
                        last = nc.vector.tensor_tensor(
                            probs[:, i % 2, 512 * m:512 * m + 512].rearrange("p (h s) -> p h s", h=HC),
                            s_bank[i % 2][m][:].rearrange("p (h s) -> p h s", h=HC),
                            s_max[:, i, HC * m:HC * m + HC].unsqueeze(2).to_broadcast([P, HC, M]), ALU.subtract)
                    last.then_inc(s["v_sub"], 1)

                def turned(i):
                    dve.wait_ge(s["t_pt"], 2 * (TB * b + i) + 1)
                    nc.vector.tensor_copy(flat(probs_t[:, i % 2, 0:4, :]), t_bank[0][:]).then_inc(s["v_pt"], 1)

                def normalise(i):
                    g = TB * b + i
                    dve.wait_ge(s["t_o"], g + 1)
                    o = x_bank[0][:, 0:PAIRS * PW].rearrange("p (j a) -> p j a", j=PAIRS)
                    nc.vector.reciprocal(o_rcp[:, i, :].rearrange("p (j a) -> p j a", j=PAIRS),
                                         o[:, :, 2 * HD:PW]).then_inc(s["v_rcp"], 1)
                    dve.wait_ge(s["v_rcp"], g + 1)
                    for a in range(2):
                        last = nc.vector.tensor_tensor(
                            o_n[:, i % 2, :].rearrange("p (j a d) -> p j a d", j=PAIRS, a=2)[:, :, a, :],
                            o[:, :, HD * a:HD * a + HD],
                            o_rcp[:, i, :].rearrange("p (j a) -> p j a", j=PAIRS)[:, :, a:a + 1].to_broadcast(
                                [P, PAIRS, HD]), ALU.mult)
                    last.then_inc(s["v_o"], 1)

                def turned_out(i):
                    dve.wait_ge(s["t_ot"], TB * b + i + 1)
                    nc.vector.tensor_copy(o_t[:, :, P * i:P * i + P], x_bank[1][:, 0:D].rearrange(
                        "p (k t) -> p k t", k=DK)).then_inc(s["v_ot"], 1)

                scores(0)
                scores(1)
                turned(0)
                scores(2)
                normalise(0)
                turned(1)
                scores(3)
                turned_out(0)
                normalise(1)
                turned(2)
                turned_out(1)
                normalise(2)
                turned(3)
                turned_out(2)
                normalise(3)
                turned_out(3)
                layer_norm(phase, b + 2, b + 1)
                dve.wait_ge(s["p_xb"], b + 1)
                for i in range(TB):
                    g = TB * b + i
                    dve.wait_ge(s["t_y"], g + 1)
                    row = x_res[:, bass.ds(g, 1), :].rearrange("p o d -> p (o d)")
                    nc.vector.scalar_tensor_tensor(row, x_bank[i % 2][:, 0:D], tg[:, l:l + 1], row, ALU.mult,
                                                   ALU.add).then_inc(s["v_y"], 1)

            with dve.Fori(0, B) as b:
                attention(0, b)

            dve.wait_ge(att[0]["v_y"], NT)
            with dve.Fori(0, B) as b:
                layer_norm(ln["rt"], b + 1, b)
                dve.wait_ge(r_l, b + 1)
                nc.vector.tensor_tensor(logits[:, bass.ds(b * TB, TB), :],
                                        s_bank[0][0][:, 0:TB * E].rearrange("p (t e) -> p t e", t=TB),
                                        rb[:].unsqueeze(1).to_broadcast([P, TB, E]), ALU.add).then_inc(r_lg, 1)
            dve.wait_ge(r_lg, B)
            nc.vector.tensor_reduce(l_max[:], logits[:], AX, ALU.max).then_inc(r_v, 1)
            dve.wait_ge(r_v, 1)
            nc.vector.tensor_tensor(r_tmp[:], logits[:], l_max[:].unsqueeze(2).to_broadcast([P, NT, E]),
                                    ALU.subtract).then_inc(r_v, 1)
            nc.vector.tensor_tensor(onehot[:], logits[:], l_max[:].unsqueeze(2).to_broadcast([P, NT, E]),
                                    ALU.is_equal).then_inc(r_v, 1)
            dve.wait_ge(r_v, 3)
            nc.vector.scalar_tensor_tensor(count[:], onehot[:], -float(E),
                                           expert_no8[:].unsqueeze(1).to_broadcast([P, NT, E]), ALU.mult,
                                           ALU.add).then_inc(r_v, 1)
            dve.wait_ge(r_v, 4)
            nc.vector.tensor_reduce(first[:], count[:], AX, ALU.min).then_inc(r_v, 1)
            dve.wait_ge(r_v, 5)
            nc.vector.tensor_tensor(onehot[:], expert_no[:].unsqueeze(1).to_broadcast([P, NT, E]),
                                    first[:].unsqueeze(2).to_broadcast([P, NT, E]), ALU.is_equal).then_inc(r_hot, 1)
            dve.wait_ge(r_exp, 1)
            nc.vector.tensor_reduce(l_sum[:], l_exp[:], AX, ALU.add).then_inc(r_v, 1)
            dve.wait_ge(r_v, 6)
            nc.vector.reciprocal(l_sum[:], l_sum[:]).then_inc(r_v, 1)
            dve.wait_ge(r_v, 7)
            nc.vector.tensor_scalar(weight[:], l_sum[:], tg[:, 2:3], None, ALU.mult).then_inc(r_v, 1)
            dve.wait_ge(r_cnt, 1)
            nc.vector.tensor_copy(count[:], s_bank[1][1][:, 0:NT * E].rearrange("p (t e) -> p t e", t=NT)).then_inc(r_v, 1)
            dve.wait_ge(r_v, 9)
            for e in range(E):
                last = nc.vector.tensor_tensor_scan(upto[:, e, :], count[:, :, e], zeros[:, 0:NT], 0.0, ALU.add, ALU.add)
            last.then_inc(r_v, 1)
            dve.wait_ge(r_v, 10)
            nc.vector.tensor_tensor(more[:], upto[:, :, NT - 1:NT].to_broadcast([P, E, NT]),
                                    tile_edge[:].unsqueeze(1).to_broadcast([P, E, NT]), ALU.is_gt).then_inc(r_v, 1)
            dve.wait_ge(r_v, 11)
            nc.vector.tensor_reduce(tiles_of[:], more[:], AX, ALU.add).then_inc(r_v, 1)
            dve.wait_ge(r_v, 12)
            nc.vector.tensor_scalar(tiles_of[:], tiles_of[:], 1.0, None, ALU.max).then_inc(r_v, 1)
            dve.wait_ge(r_v, 13)
            nc.vector.tensor_tensor_scan(tile_end[:], tiles_of[:], zeros[:, 0:E], 0.0, ALU.add, ALU.add).then_inc(r_v, 1)
            dve.wait_ge(r_v, 14)
            nc.vector.tensor_tensor(past[:], tile_end[:].unsqueeze(1).to_broadcast([P, SLOT_TILES, E]),
                                    slot_tile_no[:].unsqueeze(2).to_broadcast([P, SLOT_TILES, E]), ALU.is_le).then_inc(r_v, 1)
            nc.vector.tensor_tensor(slot_base[:], tile_end[:], tiles_of[:], ALU.subtract).then_inc(r_v, 1)
            dve.wait_ge(r_v, 16)
            nc.vector.tensor_reduce(expert_f[:], past[:], AX, ALU.add).then_inc(r_v, 1)
            dve.wait_ge(r_v, 17)
            nc.vector.tensor_scalar(expert_of[:], expert_f[:], float(E - 1), None, ALU.min).then_inc(r_exps, 1)
            nc.vector.tensor_tensor(r_tmp[:], upto[:].rearrange("p e t -> p t e"), count[:], ALU.subtract).then_inc(r_v, 1)
            dve.wait_ge(r_v, 18)
            nc.vector.tensor_tensor(r_tmp[:], s_bank[1][0][:, 0:NT * E].rearrange("p (t e) -> p t e", t=NT), r_tmp[:],
                                    ALU.add).then_inc(r_v, 1)
            dve.wait_ge(r_v, 19)
            nc.vector.scalar_tensor_tensor(r_tmp[:], slot_base[:].unsqueeze(1).to_broadcast([P, NT, E]), float(P),
                                           r_tmp[:], ALU.mult, ALU.add).then_inc(r_v, 1)
            dve.wait_ge(r_v, 20)
            nc.vector.tensor_tensor(r_tmp[:], r_tmp[:], onehot[:], ALU.mult).then_inc(r_v, 1)
            dve.wait_ge(r_v, 21)
            nc.vector.tensor_reduce(pos_f[:], r_tmp[:], AX, ALU.add).then_inc(r_v, 1)
            dve.wait_ge(r_v, 22)
            nc.vector.tensor_copy(pos[:], pos_f[:]).then_inc(r_pos, 1)

            def expert_tile(t, par):
                for q in range(2):
                    dve.wait_ge(m_sil, 2 * t + q + 1)
                    nc.vector.tensor_tensor(flat(act_t[:, par, 4 * q:4 * q + 4, :]), bank[2 + q][:], sil[:, q, :],
                                            ALU.mult).then_inc(m_act, 1)

            expert_tile(0, 0)
            expert_tile(1, 1)
            with dve.Fori(1, SLOT_TILES // 2) as i:
                expert_tile(2 * i, 0)
                expert_tile(2 * i + 1, 1)
            expert_tile(SLOT_TILES - 1, 0)

            for b in range(B):
                dve.wait_ge(g_y[b], 16 * TB)
                for t in range(TB * b, TB * b + TB):
                    nc.vector.scalar_tensor_tensor(x_res[:, t, :], xn_all[:, t, :], weight[:, t:t + 1], x_res[:, t, :],
                                                   ALU.mult, ALU.add).then_inc(g_x, 1)
                if b == 0:
                    dve.wait_ge(g_x, TB)
                    layer_norm(ln["l1"], 1, 0)
            dve.wait_ge(g_x, NT)
            with dve.Fori(0, B) as b:
                attention(1, b)

            def quantise(src, dst, small, t, absmax, clip, inv, mul, rnd, done):
                nc.vector.tensor_reduce(small[:, 0:1], src, AX, ALU.max, apply_absolute_value=True).then_inc(absmax, 1)
                dve.wait_ge(absmax, t + 1)
                nc.vector.tensor_scalar(small[:, 0:1], small[:, 0:1], EPS, None, ALU.max).then_inc(clip, 1)
                dve.wait_ge(clip, t + 1)
                nc.vector.reciprocal(small[:, 1:2], small[:, 0:1]).then_inc(inv, 1)
                dve.wait_ge(inv, t + 1)
                nc.vector.tensor_scalar(small[:, 2:3], small[:, 1:2], 127.0, None, ALU.mult).then_inc(mul, 1)
                dve.wait_ge(mul, t + 1)
                nc.vector.tensor_scalar(src, src, small[:, 2:3], ROUND, ALU.mult, ALU.add).then_inc(rnd, 1)
                dve.wait_ge(rnd, t + 1)
                nc.vector.tensor_scalar(dst, src, ROUND, 127.0, ALU.subtract, ALU.min).then_inc(done, 1)

            def ff_rows(t, i, par):
                small = q_small[:, par, :]
                quantise(xn[:, i, :], x_q[:, par, :], small, t, f["max"], f["clip"], f["inv"], f["mul"], f["rnd"], f["xq"])

            with dve.Fori(0, B) as b:
                dve.wait_ge(att[1]["v_y"], NT)
                layer_norm(ln["ff"], b + 1, b)
                dve.wait_ge(ln["ff"]["xn"], b + 1)
                for i in range(TB):
                    t = TB * b + i
                    par = i % 2
                    small = q_small[:, par, :]
                    hs = h_f[:, par, :]
                    ff_rows(t, i, par)
                    nc.vector.tensor_scalar(small[:, 3:5], w_mean[:, 0:2], small[:, 0:1], 1.0 / 127.0, ALU.mult,
                                            ALU.mult).then_inc(f["unit"], 1)
                    dve.wait_ge(f["unit"], t + 1)
                    dve.wait_ge(f["a_sil"], 2 * t + 2)
                    for c in range(2):
                        last = nc.vector.scalar_tensor_tensor(hs[:, 512 * c:512 * c + 512], bank[2 + c][:], small[:, 4:5],
                                                              sil_g[:, par, 512 * c:512 * c + 512], ALU.mult, ALU.mult)
                    last.then_inc(f["v_h"], 1)
                    dve.wait_ge(f["v_h"], t + 1)
                    quantise(hs, h_q[:, par, :], small, t, f["hmax"], f["hclip"], f["hinv"], f["hmul"], f["hrnd"], f["hq"])
                    nc.vector.tensor_scalar(small[:, 5:6], small[:, 0:1], wd_g[:, 0:1], None, ALU.mult).then_inc(f["dunit"], 1)
                    dve.wait_ge(f["dunit"], t + 1)
                    dve.wait_ge(f["t_y"], t + 1)
                    row = x_res[:, bass.ds(t, 1), :].rearrange("p o d -> p (o d)")
                    nc.vector.scalar_tensor_tensor(row, x_bank[0][:, 0:D], small[:, 5:6], row, ALU.mult,
                                                   ALU.add).then_inc(f["v_y"], 1)


_INS = ["x", "ctx_768", "g_xattn", "g_ffn", "L0_xattn_Wq", "L0_xattn_bq", "L0_xattn_Wk", "L0_xattn_bk", "L0_xattn_Wv",
        "L0_xattn_bv", "L0_xattn_W1", "L0_xattn_b1", "L0_xattn_W2", "L0_xattn_b2", "L0_ffn_router_w",
        "L0_ffn_router_b", "L0_ffn_w1", "L0_ffn_w2", "L1_xattn_Wq", "L1_xattn_bq", "L1_xattn_Wk", "L1_xattn_bk",
        "L1_xattn_Wv", "L1_xattn_bv", "L1_xattn_Wo", "L1_xattn_bo", "L1_ffn_w_gate", "L1_ffn_w_up", "L1_ffn_w_down"]


def kernel(**inputs):
    import concourse.bacc as bacc
    from concourse.bass_utils import run_bass_kernel_spmd

    nc = bacc.Bacc("TRN2", target_bir_lowering=False, num_devices=1)
    arrays, inp = {}, {}
    for name in _INS:
        a = np.ascontiguousarray(inputs[name])
        arrays[f"in_{name}"] = a
        inp[name] = nc.dram_tensor(f"in_{name}", a.shape, mybir.dt.from_np(a.dtype), kind="ExternalInput").ap()
    out = nc.dram_tensor("out_rows", (B, N, D), F32, kind="ExternalOutput").ap()
    slots_x = nc.dram_tensor("slots_x", (SLOTS, D), F32, kind="Internal").ap()
    slots_y = nc.dram_tensor("slots_y", (SLOTS, D), F32, kind="Internal").ap()
    flamingo(nc, inp, out, slots_x, slots_y)
    r = run_bass_kernel_spmd(nc, [arrays], core_ids=[0])
    return r.results[0]["out_rows"]
```

```python
from contextlib import ExitStack

import numpy as np
import concourse.bass as bass
from concourse import mybir

F32 = mybir.dt.float32
BF16 = mybir.dt.bfloat16
I32 = mybir.dt.int32
U32 = mybir.dt.uint32
ALU = mybir.AluOpType
ACT = mybir.ActivationFunctionType
AX = mybir.AxisListType.X

P = 128
B, N, D = 4, 512, 256
M, C = 64, 192
H, HD = 16, 16
TB = N // P
NT = B * TB
DK = D // P
HC = P // HD
PAIRS = H // 2
PW = 2 * HD + 2
F1 = 2 * D
FK = F1 // P
E, FE = 8, 1024
EK = FE // P
SLOT_TILES = NT + E - 1
SLOTS = SLOT_TILES * P
INNER = 1024
IK = INNER // P
EPS = 1e-5
QSCALE = float(HD) ** -0.5
ROUND = 1.5 * 2.0 ** 23


def flamingo(nc, inp, out, slots_x, slots_y):
    with ExitStack() as ctx:
        def sb(name, shape, dt=F32):
            return ctx.enter_context(nc.sbuf_tensor(name, shape, dt))

        def sem(name):
            return ctx.enter_context(nc.semaphore(name))

        def flat(ap):
            return ap.rearrange("p a b -> p (a b)")

        bank = [ctx.enter_context(nc.psum_tensor(f"bank{i}", [P, 512], F32)) for i in range(8)]
        s_bank = [bank[0:2], bank[2:4]]
        t_bank = bank[4:6]
        x_bank = bank[6:8]

        ident = sb("ident", [P, P])
        ident_b = sb("ident_b", [P, P], BF16)
        ones = sb("ones", [P, P])
        before = sb("before", [P, P])
        head_mask = sb("head_mask", [P, HC])
        minus_half = sb("minus_half", [P, TB])
        eps = sb("eps", [P, TB])
        expert_no = sb("expert_no", [P, E])
        expert_no8 = sb("expert_no8", [P, E])
        tile_edge = sb("tile_edge", [P, NT])
        slot_tile_no = sb("slot_tile_no", [P, SLOT_TILES])
        zeros = sb("zeros", [P, D])

        x_res = sb("x_res", [P, NT + TB, D])
        xn_all = sb("xn_all", [P, NT, D])
        xn = sb("xn", [P, TB, D])
        xn_t = sb("xn_t", [P, DK, N])
        stats = sb("stats", [P, TB, 6])
        carried = sb("carried", [P, 7])
        mv = sb("mv", [P, TB, 2])
        var_eps = sb("var_eps", [P, TB])
        rstd = sb("rstd", [P, TB])

        ctx_rows = sb("ctx_rows", [P, 2, C])
        ctx_ta = sb("ctx_ta", [P, B, 2, M])
        ctx_tb = sb("ctx_tb", [C - P, B, 2, M])
        vec_rows = sb("vec_rows", [12, P])
        vecs = sb("vecs", [P, 12])
        bq_s = sb("bq_s", [P, 2, DK])
        gates = sb("gates", [P, 4])
        tg = sb("tg", [P, 4])
        wq = [sb(f"wq{l}", [P, DK, D]) for l in range(2)]
        wka = [sb(f"wka{l}", [P, D]) for l in range(2)]
        wkb = [sb(f"wkb{l}", [C - P, D]) for l in range(2)]
        wva = [sb(f"wva{l}", [P, D]) for l in range(2)]
        wvb = [sb(f"wvb{l}", [C - P, D]) for l in range(2)]
        bv = [sb(f"bv{l}", [P, D]) for l in range(2)]
        bo = [sb(f"bo{l}", [P, D]) for l in range(2)]
        w1 = sb("w1", [P, DK, F1])
        w2 = sb("w2", [P, FK, D])
        wo = sb("wo", [P, DK, D])
        rw = sb("rw", [P, DK, E])
        rb = sb("rb", [P, E])
        k_t = sb("k_t", [P, DK, B * M])
        k_bd = sb("k_bd", [P, DK, B, HC * M])
        v_bd = [sb(f"v_bd{l}", [P, B, PAIRS, PW]) for l in range(2)]

        q_t = sb("q_t", [P, DK, N])
        s_max = sb("s_max", [P, TB, H])
        probs = sb("probs", [P, 2, H * M])
        probs_t = sb("probs_t", [P, 2, PAIRS, P])
        o_rcp = sb("o_rcp", [P, TB, H])
        o_n = sb("o_n", [P, 2, D])
        o_t = sb("o_t", [P, DK, N])
        h1_t = sb("h1_t", [P, FK, N])

        ew1 = sb("ew1", [P, 2, DK, 2 * FE])
        ew2 = sb("ew2", [P, 2, EK, D])
        xs = sb("xs", [P, 2, D])
        xs_t = q_t[:, 0, :].rearrange("p (s k t) -> p s k t", s=2, k=DK)
        sil = probs[:, :, 0:512]
        act_t = probs_t
        ys = o_n

        logits = sb("logits", [P, NT, E])
        l_max = sb("l_max", [P, NT])
        l_exp = sb("l_exp", [P, NT, E])
        l_sum = sb("l_sum", [P, NT])
        weight = sb("weight", [P, NT])
        onehot = sb("onehot", [P, NT, E])
        first = sb("first", [P, NT])
        r_tmp = sb("r_tmp", [P, NT, E])
        count = sb("count", [P, NT, E])
        upto = sb("upto", [P, E, NT])
        more = sb("more", [P, E, NT])
        tiles_of = sb("tiles_of", [P, E])
        tile_end = sb("tile_end", [P, E])
        slot_base = sb("slot_base", [P, E])
        pos_f = sb("pos_f", [P, NT])
        pos = sb("pos", [P, NT], U32)
        past = sb("past", [P, SLOT_TILES, E])
        expert_f = sb("expert_f", [P, SLOT_TILES])
        expert_of = sb("expert_of", [P, SLOT_TILES], I32)

        bit_raw = ew1[:, 0, :, :].rearrange("p k f -> p (k f)")[:, 0:2 * IK * D].rearrange(
            "p (w a) -> p w a", w=2)
        bit_down = ew2[:, 0, :, :].rearrange("p k f -> p (k f)")
        bit_q = flat(ew1[:, 1, :, :])[:, 0:3 * IK * D // 2].bitcast(BF16).rearrange("p (w a) -> p w a", w=3)
        xn2 = ew2[:, 1, 0:TB, :]
        w_sum = sb("w_sum", [P, 3])
        w_mean = sb("w_mean", [P, 3])
        w_inv = sb("w_inv", [P, 3])
        gate_t = sb("gate_t", [P, DK, INNER], BF16)
        up_t = sb("up_t", [P, DK, INNER], BF16)
        down_t = sb("down_t", [P, IK, D], BF16)
        wd_g = sb("wd_g", [P, 1])

        x_q = flat(xs[:]).bitcast(BF16).rearrange("p (s d) -> p s d", s=TB)
        x_qt = q_t[:, 0, 0:D].bitcast(BF16).rearrange("p (s k t) -> p s k t", s=2, k=DK)
        sil_g = probs
        h_f = probs_t[:, :, :, :].rearrange("p s k t -> p s (k t)")
        h_q = flat(h1_t[:, 0:2, :]).bitcast(BF16).rearrange("p (s k) -> p s k", s=2)
        h_qt = flat(h1_t[:, 2:4, :]).bitcast(BF16).rearrange("p (s k t) -> p s k t", s=2, k=IK)
        x_abs = sb("x_abs", [P, TB])
        x_inv = sb("x_inv", [P, TB])
        x_scale = sb("x_scale", [P, TB])
        x_unit = sb("x_unit", [P, 2, TB])
        h_abs = sb("h_abs", [P, 2])
        h_inv = sb("h_inv", [P, 2])
        h_scale = sb("h_scale", [P, 2])
        h_unit = sb("h_unit", [P, TB])

        d_ctx, d_kv0, d_vec, d_x0, d_x, d_q0, d_mlp, d_rout, d_l1, d_bit, d_bv = (
            sem(n) for n in ("d_ctx", "d_kv0", "d_vec", "d_x0", "d_x", "d_q0", "d_mlp", "d_rout", "d_l1", "d_bit", "d_bv"))
        d_zero = sem("d_zero")
        p_mem, p_const, p_gate = sem("p_mem"), sem("p_const"), sem("p_gate")
        v_zero = sem("v_zero")
        a_tanh, v_bq, v_bo = sem("a_tanh"), sem("v_bq"), sem("v_bo")
        t_vec, v_vec, t_ctx, v_ctx = sem("t_vec"), sem("v_vec"), sem("t_ctx"), sem("v_ctx")
        t_k, a_k, p_kbd, t_v, v_vbd = sem("t_k"), sem("a_k"), sem("p_kbd"), sem("t_v"), sem("v_vbd")
        a_abs, t_abs, v_wm = sem("a_abs"), sem("t_abs"), sem("v_wm")
        p_tern, p_terq, t_bit, a_bit = sem("p_tern"), sem("p_terq"), sem("t_bit"), sem("a_bit")

        def ln_sems(ph):
            return {k: sem(f"ln_{k}_{ph}") for k in ("stats", "aggr", "eps", "rstd", "xn")}

        ln = {ph: ln_sems(ph) for ph in ("l0", "rt", "l1", "ff")}
        att = [{k: sem(f"{k}_l{l}") for k in (
            "t_xt", "a_xt", "t_q", "a_q", "t_s", "v_max", "v_sub", "a_exp", "t_pt", "v_pt", "a_pt",
            "t_o", "v_rcp", "v_o", "t_ot", "v_ot", "t_h", "a_h", "t_y", "v_y", "p_xb")} for l in range(2)]
        r_t, r_e, r_l, r_lg = sem("r_t"), sem("r_e"), sem("r_l"), sem("r_lg")
        p_keep = sem("p_keep")
        r_v, r_exp, r_cnt = sem("r_v"), sem("r_exp"), sem("r_cnt")
        r_hot, r_pos, r_exps = sem("r_hot"), sem("r_pos"), sem("r_exps")
        p_scat = sem("p_scat")
        m_w1 = [sem(f"m_w1_{i}") for i in range(2)]
        m_w2 = [sem(f"m_w2_{i}") for i in range(2)]
        m_x = [sem(f"m_x_{i}") for i in range(2)]
        m_st = [sem(f"m_st_{i}") for i in range(2)]
        m_t, m_xt, m_up, m_sil, m_act, m_dn, m_y = (
            sem(n) for n in ("m_t", "m_xt", "m_up", "m_sil", "m_act", "m_dn", "m_y"))
        g_y = [sem(f"g_y{i}") for i in range(B)]
        g_x = sem("g_x")
        f = {k: sem(f"f_{k}") for k in (
            "max", "clip", "inv", "mul", "unit", "rnd", "xq", "t_x", "a_x", "t_gu", "a_sil", "v_h", "hmax", "hclip",
            "hinv", "hmul", "hrnd", "hq", "hunit", "t_h", "a_h", "t_y", "v_y")}
        d_out = sem("d_out")

        block = ctx.enter_context(nc.Block())

        def batch_of(ap, b):
            return ap[:, bass.ds(b * TB, TB), :]

        @block.sync
        def _(sp):
            sp.dma_start(ctx_rows[:], inp["ctx_768"].rearrange("(t a) s c -> (a s) t c", t=2)).then_inc(d_ctx, 16)
            sp.dma_start(x_res[:, 0:TB, :], inp["x"][0].rearrange("(j p) d -> p j d", p=P)).then_inc(d_x0, 16)
            at = 0
            for name, rows in (("L0_xattn_bq", 2), ("L0_xattn_bk", 2), ("L0_xattn_b1", 4), ("L1_xattn_bq", 2),
                               ("L1_xattn_bk", 2)):
                sp.dma_start(vec_rows[at:at + rows, :], inp[name].rearrange("(m p) -> m p", p=P)).then_inc(d_vec, 16)
                at += rows

            def key_value_weights(l, s):
                sp.dma_start(wka[l][:], inp[f"L{l}_xattn_Wk"][0:P, :]).then_inc(s, 16)
                sp.dma_start(wkb[l][:], inp[f"L{l}_xattn_Wk"][P:C, :]).then_inc(s, 16)
                sp.dma_start(wva[l][:], inp[f"L{l}_xattn_Wv"][0:P, :]).then_inc(s, 16)
                sp.dma_start(wvb[l][:], inp[f"L{l}_xattn_Wv"][P:C, :]).then_inc(s, 16)

            key_value_weights(0, d_kv0)
            sp.dma_start(bv[0][:], inp["L0_xattn_bv"].partition_broadcast(P)).then_inc(d_bv, 16)
            sp.dma_start(wq[0][:], inp["L0_xattn_Wq"].rearrange("(k p) n -> p k n", p=P)).then_inc(d_q0, 16)
            for b in range(1, B):
                sp.dma_start(x_res[:, TB * b:TB * b + TB, :],
                             inp["x"][b].rearrange("(j p) d -> p j d", p=P)).then_inc(d_x, 16)
            sp.dma_start(gates[:, 0:2], inp["g_xattn"].partition_broadcast(P)).then_inc(d_rout, 16)
            sp.dma_start(gates[:, 2:4], inp["g_ffn"].partition_broadcast(P)).then_inc(d_rout, 16)
            sp.dma_start(bv[1][:], inp["L1_xattn_bv"].partition_broadcast(P)).then_inc(d_rout, 16)
            sp.dma_start(bo[0][:], inp["L0_xattn_b2"].partition_broadcast(P)).then_inc(d_rout, 16)
            sp.dma_start(bo[1][:], inp["L1_xattn_bo"].partition_broadcast(P)).then_inc(d_rout, 16)
            sp.dma_start(rb[:], inp["L0_ffn_router_b"].partition_broadcast(P)).then_inc(d_rout, 16)
            sp.dma_start(rw[:], inp["L0_ffn_router_w"].rearrange("(k p) e -> p k e", p=P)).then_inc(d_rout, 16)
            sp.dma_start(w1[:], inp["L0_xattn_W1"].rearrange("(k p) n -> p k n", p=P)).then_inc(d_mlp, 16)
            sp.dma_start(w2[:], inp["L0_xattn_W2"].rearrange("(k p) n -> p k n", p=P)).then_inc(d_mlp, 16)
            key_value_weights(1, d_l1)
            sp.dma_start(wq[1][:], inp["L1_xattn_Wq"].rearrange("(k p) n -> p k n", p=P)).then_inc(d_l1, 16)
            sp.dma_start(wo[:], inp["L1_xattn_Wo"].rearrange("(k p) n -> p k n", p=P)).then_inc(d_l1, 16)
            sp.dma_start(bit_raw[:, 0, :].rearrange("p (a i) -> p a i", a=IK),
                         inp["L1_ffn_w_gate"].rearrange("(a p) i -> p a i", p=P)).then_inc(d_bit, 16)
            sp.dma_start(bit_raw[:, 1, :].rearrange("p (a i) -> p a i", a=IK),
                         inp["L1_ffn_w_up"].rearrange("(a p) i -> p a i", p=P)).then_inc(d_bit, 16)
            sp.dma_start(bit_down.rearrange("p (a i) -> p a i", a=DK),
                         inp["L1_ffn_w_down"].rearrange("(a p) i -> p a i", p=P)).then_inc(d_bit, 16)
            sp.wait_ge(v_zero, 3)
            zero_tiles = SLOT_TILES
            sp.dma_start(slots_x.rearrange("(t p) d -> p t d", p=P),
                         zeros[:].unsqueeze(1).to_broadcast([P, zero_tiles, D])).then_inc(d_zero, 16)

            def expert_first(e, par):
                sp.dma_start(ew1[:, par, :, :], inp["L0_ffn_w1"][bass.ds(e, 1)].rearrange(
                    "o (k p) f -> p (o k) f", p=P)).then_inc(m_w1[par], 16)

            def expert_second(e, par):
                sp.dma_start(ew2[:, par, :, :], inp["L0_ffn_w2"][bass.ds(e, 1)].rearrange(
                    "o (k p) d -> p (o k) d", p=P)).then_inc(m_w2[par], 16)

            def slot_rows(t, par):
                sp.dma_start(xs[:, par, :], slots_x[bass.ds(t * P, P), :]).then_inc(m_x[par], 16)

            def expert_tile(t, par):
                e = sp.value_load(expert_of[0:1, bass.ds(t, 1)], min_val=0, max_val=E - 1)
                sp.wait_ge(m_up, 2 * t - 2)
                expert_first(e, par)
                slot_rows(t, par)
                sp.wait_ge(m_dn, t - 1)
                expert_second(e, par)

            sp.wait_ge(a_bit, 12)
            expert_first(0, 0)
            expert_second(0, 0)
            sp.wait_ge(r_exps, 1)
            sp.wait_ge(p_keep, B)
            e = sp.value_load(expert_of[0:1, 1:2], min_val=0, max_val=E - 1)
            expert_first(e, 1)
            expert_second(e, 1)
            sp.wait_ge(p_scat, 16 * NT)
            slot_rows(0, 0)
            slot_rows(1, 1)
            with sp.Fori(1, SLOT_TILES // 2) as i:
                expert_tile(2 * i, 0)
                expert_tile(2 * i + 1, 1)
            expert_tile(SLOT_TILES - 1, 0)

            with sp.Fori(0, B) as b:
                sp.wait_ge(f["v_y"], TB * b + TB)
                sp.dma_start(out[bass.ds(b, 1)].rearrange("o (j p) d -> p (o j) d", p=P),
                             batch_of(x_res, b)).then_inc(d_out, 16)
            sp.wait_ge(d_out, 16 * B)

        def layer_norm_rstd(pool, s, n, tiles=slice(0, TB)):
            pool.wait_ge(s["aggr"], n)
            nc.gpsimd.tensor_tensor(var_eps[:, tiles], mv[:, tiles, 1], eps[:, tiles], ALU.add).then_inc(s["eps"], 1)
            pool.wait_ge(s["eps"], n)
            nc.gpsimd.tensor_tensor(rstd[:, tiles], var_eps[:, tiles], minus_half[:, tiles], ALU.pow).then_inc(s["rstd"], 1)

        @block.gpsimd
        def _(pool):
            nc.gpsimd.memset(ident[:], 0.0).then_inc(p_mem, 1)
            nc.gpsimd.memset(ident_b[:], 0.0).then_inc(p_mem, 1)
            nc.gpsimd.memset(ones[:], 1.0).then_inc(p_mem, 1)
            nc.gpsimd.memset(before[:], 1.0).then_inc(p_mem, 1)
            nc.gpsimd.memset(head_mask[:], 1.0).then_inc(p_mem, 1)
            nc.gpsimd.memset(minus_half[:], -0.5).then_inc(p_mem, 1)
            nc.gpsimd.memset(carried[:, 2:3], 0.0).then_inc(p_mem, 1)
            nc.gpsimd.memset(eps[:], EPS).then_inc(p_mem, 1)
            nc.gpsimd.iota(expert_no[:], [[1, E]], base=0, channel_multiplier=0,
                           allow_small_or_imprecise_dtypes=True).then_inc(p_mem, 1)
            nc.gpsimd.iota(expert_no8[:], [[1, E]], base=E, channel_multiplier=0,
                           allow_small_or_imprecise_dtypes=True).then_inc(p_mem, 1)
            nc.gpsimd.iota(tile_edge[:], [[P, NT]], base=0, channel_multiplier=0,
                           allow_small_or_imprecise_dtypes=True).then_inc(p_mem, 1)
            nc.gpsimd.iota(slot_tile_no[:], [[1, SLOT_TILES]], base=0, channel_multiplier=0,
                           allow_small_or_imprecise_dtypes=True).then_inc(p_mem, 1)
            pool.wait_ge(p_mem, 12)
            nc.gpsimd.affine_select(out=ident[:], in_=ident[:], compare_op=ALU.not_equal, fill=1.0, base=0,
                                    pattern=[[-1, P]], channel_multiplier=1).then_inc(p_const, 1)
            nc.gpsimd.affine_select(out=ident_b[:], in_=ident_b[:], compare_op=ALU.not_equal, fill=1.0, base=0,
                                    pattern=[[-1, P]], channel_multiplier=1).then_inc(p_const, 1)
            nc.gpsimd.affine_select(out=before[:], in_=before[:], compare_op=ALU.is_gt, fill=0.0, base=0,
                                    pattern=[[1, P]], channel_multiplier=-1).then_inc(p_const, 1)
            nc.gpsimd.affine_select(out=head_mask[:], in_=head_mask[:], compare_op=ALU.is_ge, fill=0.0, base=0,
                                    pattern=[[-HD, HC]], channel_multiplier=1).then_inc(p_const, 1)
            pool.wait_ge(p_const, 4)
            nc.gpsimd.affine_select(out=head_mask[:], in_=head_mask[:], compare_op=ALU.is_ge, fill=0.0, base=HD - 1,
                                    pattern=[[HD, HC]], channel_multiplier=-1).then_inc(p_const, 1)
            pool.wait_ge(p_const, 5)
            layer_norm_rstd(pool, ln["l0"], 1)
            def spread_keys(l):
                for m in range(DK):
                    pool.wait_ge(a_k, DK * l + m + 1)
                    for b in range(B):
                        nc.gpsimd.tensor_tensor(
                            k_bd[:, m, b, :].rearrange("p (h s) -> p h s", h=HC),
                            k_t[:, m, b * M:b * M + M].unsqueeze(1).to_broadcast([P, HC, M]),
                            head_mask[:].unsqueeze(2).to_broadcast([P, HC, M]), ALU.mult).then_inc(p_kbd, 1)

            spread_keys(0)
            layer_norm_rstd(pool, ln["l0"], 2)
            pool.wait_ge(v_wm, 3)
            raws = (bit_raw[:, 0, :], bit_raw[:, 1, :], bit_down)
            for w in range(3):
                nc.gpsimd.tensor_scalar(raws[w], raws[w], w_inv[:, w:w + 1], 1.0, ALU.mult, ALU.min).then_inc(p_tern, 1)
                pool.wait_ge(p_tern, 2 * w + 1)
                nc.gpsimd.tensor_scalar(raws[w], raws[w], -1.0, ROUND, ALU.max, ALU.add).then_inc(p_tern, 1)
                pool.wait_ge(p_tern, 2 * w + 2)
                nc.gpsimd.tensor_scalar(bit_q[:, w, :], raws[w], -ROUND, 1.0, ALU.add, ALU.mult).then_inc(p_terq, 1)
            pool.wait_ge(v_bo, 2)

            def bias_rows(l, b):
                pool.wait_ge(ln["l0" if l == 0 else "l1"]["xn"], b + 1)
                nc.gpsimd.tensor_tensor(batch_of(x_res, b), batch_of(x_res, b),
                                        bo[l][:].unsqueeze(1).to_broadcast([P, TB, D]),
                                        ALU.add).then_inc(att[l]["p_xb"], 1)

            def batch(l, b, last):
                bias_rows(l, b)
                if not last:
                    layer_norm_rstd(pool, ln["l0" if l == 0 else "l1"], b + 3)
                if l == 0:
                    layer_norm_rstd(pool, ln["rt"], b + 1)
                    pool.wait_ge(ln["rt"]["xn"], b + 1)
                    nc.gpsimd.tensor_copy(batch_of(xn_all, b), xn2).then_inc(p_keep, 1)

            with pool.Fori(0, B - 1) as b:
                batch(0, b, False)
            batch(0, B - 1, True)

            pool.wait_ge(p_keep, B)
            pool.wait_ge(d_zero, 16)
            pool.wait_ge(r_pos, 1)
            for t in range(NT):
                nc.gpsimd.indirect_dma_start(
                    out=slots_x[:, :], out_offset=bass.IndirectOffsetOnAxis(ap=pos[:, t:t + 1], axis=0),
                    in_=xn_all[:, t, :], in_offset=None).then_inc(p_scat, 16)

            pool.wait_ge(att[0]["t_s"], NT)
            spread_keys(1)

            pool.wait_ge(p_scat, 16 * NT)
            pool.wait_ge(m_st[0], 16 * ((SLOT_TILES + 1) // 2))
            pool.wait_ge(m_st[1], 16 * (SLOT_TILES // 2))
            for t in range(NT):
                nc.gpsimd.indirect_dma_start(
                    out=xn_all[:, t, :], out_offset=None, in_=slots_y[:, :],
                    in_offset=bass.IndirectOffsetOnAxis(ap=pos[:, t:t + 1], axis=0)).then_inc(g_y[t // TB], 16)

            layer_norm_rstd(pool, ln["l1"], 1)
            layer_norm_rstd(pool, ln["l1"], 2)
            with pool.Fori(0, B - 1) as b:
                batch(1, b, False)
            batch(1, B - 1, True)

            def carry_wait(use):
                nc.gpsimd.tensor_tensor(carried[:, 3 + use:4 + use], carried[:, 2:3], carried[:, 2:3], ALU.add)

            def ff_rows(g, j):
                layer_norm_rstd(pool, ln["ff"], g + 1, slice(2 * j, 2 * j + 2))
                pool.wait_ge(f["mul"], g + 1)
                carry_wait(0)
                for i in range(2 * j, 2 * j + 2):
                    nc.gpsimd.tensor_scalar(xn[:, i, :], xn[:, i, :], x_scale[:, i:i + 1], ROUND, ALU.mult,
                                            ALU.add).then_inc(f["rnd"], 1)
                pool.wait_ge(f["rnd"], 2 * g + 2)
                carry_wait(1)
                for i in range(2 * j, 2 * j + 2):
                    nc.gpsimd.tensor_scalar(x_q[:, i, :], xn[:, i, :], -ROUND, 1.0, ALU.add, ALU.mult).then_inc(f["xq"], 1)

            def ff_hidden(t, par, first):
                pool.wait_ge(f["hmul"], t + 1)
                carry_wait(2)
                nc.gpsimd.tensor_scalar(h_f[:, par, :], h_f[:, par, :], h_scale[:, par:par + 1], ROUND, ALU.mult,
                                        ALU.add).then_inc(f["hrnd"], 1)
                if not first:
                    pool.wait_ge(f["t_h"], t - 1)
                pool.wait_ge(f["hrnd"], t + 1)
                carry_wait(3)
                nc.gpsimd.tensor_scalar(h_q[:, par, :], h_f[:, par, :], -ROUND, 1.0, ALU.add, ALU.mult).then_inc(f["hq"], 1)

            def ff_batch(b, first):
                for i in range(TB):
                    if i % 2 == 0:
                        ff_rows(2 * b + i // 2 + 1, (i // 2 + 1) % 2)
                    ff_hidden(TB * b + i, i % 2, first and i < 2)

            ff_rows(0, 0)
            ff_batch(0, True)
            with pool.Fori(1, B) as b:
                ff_batch(b, False)

        @block.tensor
        def _(pe):
            pe.wait_ge(p_const, 5)
            pe.wait_ge(d_vec, 16 * 5)
            nc.tensor.transpose(t_bank[0][:, 0:12], vec_rows[:], ident[0:12, 0:12]).then_inc(t_vec, 1)
            pe.wait_ge(d_ctx, 16)
            for t in range(2):
                nc.tensor.transpose(x_bank[0][:, P * t:P * t + P], ctx_rows[:, t, 0:P], ident[:])
            for t in range(2):
                last = nc.tensor.transpose(x_bank[1][0:C - P, P * t:P * t + P], ctx_rows[:, t, P:C], ident[:])
            last.then_inc(t_ctx, 1)
            pe.wait_ge(v_ctx, 4)

            def keys_values(l, kb, vb):
                for m in range(DK):
                    nc.tensor.matmul(kb[m][:, 0:B * M], wka[l][:, m * P:m * P + P], ctx_ta[:, :, 0, :],
                                     start=True, stop=False)
                    nc.tensor.matmul(kb[m][:, 0:B * M], wkb[l][:, m * P:m * P + P], ctx_tb[:, :, 0, :],
                                     start=False, stop=True).then_inc(t_k, 1)
                for b in range(B):
                    o = vb[b // 2][:, (b % 2) * D:(b % 2) * D + D]
                    nc.tensor.matmul(o, flat(ctx_ta[:, b, :, :]), wva[l][:], start=True, stop=False)
                    last = nc.tensor.matmul(o, flat(ctx_tb[:, b, :, :]), wvb[l][:], start=False, stop=True)
                last.then_inc(t_v, 1)

            pe.wait_ge(d_kv0, 16 * 4)
            keys_values(0, x_bank, s_bank[0])
            pe.wait_ge(v_vec, 1)
            pe.wait_ge(a_k, DK)

            def turn_rows(l, n):
                pe.wait_ge(ln["l0" if l == 0 else "l1"]["xn"], n + 1)
                for k in range(DK):
                    for i in range(TB):
                        last = nc.tensor.transpose(t_bank[k][:, P * i:P * i + P], xn[:, i, k * P:k * P + P], ident[:])
                    last.then_inc(att[l]["t_xt"], 1)

            def queries(l, n, after_tiles):
                s = att[l]
                pe.wait_ge(s["a_xt"], DK * n + DK)
                for m in range(DK):
                    if m == 1 and after_tiles:
                        pe.wait_ge(s["v_ot"], TB * n)
                    for k in range(DK):
                        last = nc.tensor.matmul(x_bank[m][:], wq[l][:, k, m * P:m * P + P], xn_t[:, k, :],
                                                start=(k == 0), stop=(k == DK - 1))
                    last.then_inc(s["t_q"], 1)

            def scores(l, n, i):
                s = att[l]
                if i == 0:
                    pe.wait_ge(s["a_q"], DK * n + DK)
                if i >= 2:
                    pe.wait_ge(s["v_sub"], TB * n + i - 1)
                for m in range(DK):
                    last = nc.tensor.matmul(s_bank[i % 2][m][:], q_t[:, m, P * i:P * i + P],
                                            flat(k_bd[:, m, bass.ds(n, 1), :]), start=True, stop=True)
                last.then_inc(s["t_s"], 1)

            def attention(l, b, last_batch):
                s = att[l]

                def turn(i):
                    pe.wait_ge(s["a_exp"], TB * b + i + 1)
                    for c in range(2):
                        for j in range(4):
                            last = nc.tensor.transpose(t_bank[c][:, P * j:P * j + P],
                                                       probs[:, i % 2, P * (4 * c + j):P * (4 * c + j + 1)], ident[:])
                        last.then_inc(s["t_pt"], 1)

                def values(i):
                    pe.wait_ge(s["v_pt"], TB * b + i + 1)
                    pe.wait_ge(s["a_pt"], TB * b + i + 1)
                    for j in range(PAIRS):
                        last = nc.tensor.matmul(x_bank[0][:, PW * j:PW * j + PW], probs_t[:, i % 2, j, :],
                                                flat(v_bd[l][:, bass.ds(b, 1), j, :]), start=True, stop=True)
                    last.then_inc(s["t_o"], 1)

                def turn_out(i):
                    pe.wait_ge(s["v_o"], TB * b + i + 1)
                    if i:
                        pe.wait_ge(s["v_ot"], TB * b + i)
                    for k in range(DK):
                        last = nc.tensor.transpose(x_bank[1][:, P * k:P * k + P], o_n[:, i % 2, k * P:k * P + P],
                                                   ident[:])
                    last.then_inc(s["t_ot"], 1)

                turn(0)
                scores(l, b, 2)
                values(0)
                turn(1)
                scores(l, b, 3)
                turn_out(0)
                values(1)
                turn(2)
                turn_out(1)
                values(2)
                turn(3)
                turn_out(2)
                values(3)
                if not last_batch:
                    turn_rows(l, b + 1)
                turn_out(3)
                if not last_batch:
                    queries(l, b + 1, True)
                if l == 1 and not last_batch:
                    scores(l, b + 1, 0)
                    scores(l, b + 1, 1)
                pe.wait_ge(s["v_ot"], TB * b + TB)
                out_bank = [*t_bank, *x_bank]
                if l == 0:
                    if last_batch:
                        ternary_weights()
                    for m in range(FK):
                        if m == 2 and not last_batch:
                            pe.wait_ge(s["a_q"], DK * b + 2 * DK)
                        for k in range(DK):
                            last = nc.tensor.matmul(out_bank[m][:], w1[:, k, m * P:m * P + P], o_t[:, k, :],
                                                    start=(k == 0), stop=(k == DK - 1))
                        last.then_inc(s["t_h"], 1)
                    pe.wait_ge(s["a_h"], FK * b + FK)
                src, w, kk = (h1_t, w2, FK) if l == 0 else (o_t, wo, DK)
                for i in range(TB):
                    for k in range(kk):
                        last = nc.tensor.matmul(out_bank[i][:, 0:D], src[:, k, P * i:P * i + P], w[:, k, :],
                                                start=(k == 0), stop=(k == kk - 1))
                    last.then_inc(s["t_y"], 1)
                if l == 0 and not last_batch:
                    scores(l, b + 1, 0)
                    scores(l, b + 1, 1)
                if l == 0:
                    router(b)
                else:
                    pe.wait_ge(s["v_y"], TB * b + TB)

            def ternary_weights():
                pe.wait_ge(p_terq, 3)
                pe.wait_ge(att[0]["v_sub"], NT)
                n = 0
                for w in range(3):
                    src = bit_q[:, w, :].rearrange("p (a i) -> p a i", a=(IK, IK, DK)[w])
                    for c in range(4):
                        if n >= 4:
                            pe.wait_ge(a_bit, n - 3)
                        o = bank[n % 4][:, 0:256].bitcast(BF16)
                        for j in range(4):
                            q = 4 * c + j
                            a, i = (q % IK, q // IK) if w < 2 else (q % DK, q // DK)
                            last = nc.tensor.transpose(o[:, P * j:P * j + P], src[:, a, i * P:i * P + P], ident_b[:])
                        last.then_inc(t_bit, 1)
                        n += 1

            def router(b):
                pe.wait_ge(ln["rt"]["xn"], b + 1)
                for k in range(DK):
                    for i in range(TB):
                        last = nc.tensor.transpose(t_bank[k][:, P * i:P * i + P], xn2[:, i, k * P:k * P + P], ident[:])
                    last.then_inc(r_t, 1)
                pe.wait_ge(r_e, DK * b + DK)
                for i in range(TB):
                    for k in range(DK):
                        last = nc.tensor.matmul(x_bank[0][:, E * i:E * i + E], xn_t[:, k, P * i:P * i + P],
                                                rw[:, k, :], start=(k == 0), stop=(k == DK - 1))
                last.then_inc(r_l, 1)
                pe.wait_ge(r_lg, b + 1)

            pe.wait_ge(d_q0, 16)
            turn_rows(0, 0)
            queries(0, 0, False)
            pe.wait_ge(v_vbd, 4)
            pe.wait_ge(p_kbd, DK * B)
            scores(0, 0, 0)
            scores(0, 0, 1)
            pe.wait_ge(a_abs, 3)
            nc.tensor.matmul(t_bank[1][:, 0:3], ones[:], w_sum[:], start=True, stop=True).then_inc(t_abs, 1)
            pe.wait_ge(v_wm, 3)
            pe.wait_ge(d_mlp, 32)
            pe.wait_ge(d_rout, 16 * 7)
            with pe.Fori(0, B - 1) as b:
                attention(0, b, False)
            attention(0, B - 1, True)

            pe.wait_ge(a_bit, 12)
            pe.wait_ge(r_hot, 1)
            nc.tensor.matmul(s_bank[1][0][:, 0:NT * E], before[:], flat(onehot[:]), start=True, stop=True)
            nc.tensor.matmul(s_bank[1][1][:, 0:NT * E], ones[:], flat(onehot[:]), start=True,
                             stop=True).then_inc(r_cnt, 1)
            pe.wait_ge(d_l1, 16 * 6)
            keys_values(1, t_bank, s_bank[0])
            pe.wait_ge(r_pos, 1)
            pe.wait_ge(a_k, 2 * DK)
            pe.wait_ge(v_vbd, 8)

            a_bank, g_bank, y_bank, r_bank = bank[0:2], bank[2:4], bank[4:6], bank[6:8]

            def rows_in(t, par, n):
                pe.wait_ge(m_x[par], 16 * (n + 1))
                for k in range(DK):
                    last = nc.tensor.transpose(r_bank[par][:, P * k:P * k + P], xs[:, par, k * P:k * P + P], ident[:])
                last.then_inc(m_t, 1)

            def expand(t, par, n, q):
                if q == 0:
                    pe.wait_ge(m_xt, t + 1)
                    pe.wait_ge(m_w1[par], 16 * (n + 1))
                if t is not 0:
                    pe.wait_ge(m_act, 2 * t - 1 + q)
                for o, base in ((a_bank[q], 0), (g_bank[q], FE)):
                    for j in range(4):
                        c0 = base + (4 * q + j) * P
                        for k in range(DK):
                            last = nc.tensor.matmul(o[:, P * j:P * j + P], ew1[:, par, k, c0:c0 + P],
                                                    xs_t[:, par, k, :], start=(k == 0), stop=(k == DK - 1))
                last.then_inc(m_up, 1)

            def contract(t, par, n, q):
                pe.wait_ge(m_act, 2 * t + q + 1)
                if q == 0:
                    pe.wait_ge(m_w2[par], 16 * (n + 1))
                    if n is not 0:
                        pe.wait_ge(m_y, t - 1)
                for j in range(4):
                    c = 4 * q + j
                    last = nc.tensor.matmul(y_bank[par][:, 0:D], act_t[:, par, c, :], ew2[:, par, c, :],
                                            start=(c == 0), stop=(c == EK - 1))
                if q == 1:
                    last.then_inc(m_dn, 1)

            def expert_tile(t, par, n, first_tile, last_tile):
                expand(t, par, n, 0)
                if not first_tile:
                    contract(t - 1, 1 - par, n if par else n - 1, 1)
                if not last_tile:
                    rows_in(t + 1, 1 - par, n + 1 if par else n)
                expand(t, par, n, 1)
                contract(t, par, n, 0)

            rows_in(0, 0, 0)
            expert_tile(0, 0, 0, True, False)
            expert_tile(1, 1, 0, False, False)
            with pe.Fori(1, SLOT_TILES // 2) as i:
                expert_tile(2 * i, 0, i, False, False)
                expert_tile(2 * i + 1, 1, i, False, False)
            expert_tile(SLOT_TILES - 1, 0, SLOT_TILES // 2, False, True)
            contract(SLOT_TILES - 1, 0, SLOT_TILES // 2, 1)

            pe.wait_ge(m_y, SLOT_TILES)
            turn_rows(1, 0)
            queries(1, 0, False)
            pe.wait_ge(p_kbd, 2 * DK * B)
            scores(1, 0, 0)
            scores(1, 0, 1)
            with pe.Fori(0, B - 1) as b:
                attention(1, b, False)
            attention(1, B - 1, True)

            def ff_turn(t, i):
                pe.wait_ge(f["xq"], t + 1)
                o = t_bank[0][:, 0:P].bitcast(BF16)
                for k in range(DK):
                    last = nc.tensor.transpose(o[:, P * k:P * k + P], x_q[:, i, k * P:k * P + P], ident_b[:])
                last.then_inc(f["t_x"], 1)

            def ff_up(t, par, first):
                pe.wait_ge(f["a_x"], t + 1)
                for c in range(2):
                    if not first:
                        pe.wait_ge(f["v_h"], 2 * t - 1 + c)
                    for o, w in ((bank[c], gate_t), (bank[2 + c], up_t)):
                        for k in range(DK):
                            last = nc.tensor.matmul(o[:], x_qt[:, par, k, :], w[:, k, 512 * c:512 * c + 512],
                                                    start=(k == 0), stop=(k == DK - 1))
                    last.then_inc(f["t_gu"], 1)

            def ff_down(t, par, first):
                pe.wait_ge(f["hq"], t + 1)
                o = t_bank[1][:].bitcast(BF16)
                for k in range(IK):
                    last = nc.tensor.transpose(o[:, P * k:P * k + P], h_q[:, par, k * P:k * P + P], ident_b[:])
                last.then_inc(f["t_h"], 1)
                pe.wait_ge(f["a_h"], t + 1)
                if not first:
                    pe.wait_ge(f["v_y"], t - 1)
                for k in range(IK):
                    last = nc.tensor.matmul(x_bank[par][:, 0:D], h_qt[:, par, k, :], down_t[:, k, :],
                                            start=(k == 0), stop=(k == IK - 1))
                last.then_inc(f["t_y"], 1)

            def ff_batch(b, first):
                for i in range(TB):
                    t = TB * b + i
                    ff_up(t, i % 2, first and i == 0)
                    ff_turn(t + 1, (i + 1) % TB)
                    if not (first and i < 2):
                        ff_down(t - 2, i % 2, first and i < 4)

            ff_turn(0, 0)
            ff_batch(0, True)
            with pe.Fori(1, B) as b:
                ff_batch(b, False)
            ff_down(NT - 2, 0, False)
            ff_down(NT - 1, 1, False)

        @block.scalar
        def _(act):
            def keys(l, kb):
                for m in range(DK):
                    act.wait_ge(t_k, DK * l + m + 1)
                    nc.scalar.activation(k_t[:, m, :], kb[m][:, 0:B * M], ACT.Identity,
                                         bias=vecs[:, (2, 10)[l] + m:(2, 10)[l] + m + 1]).then_inc(a_k, 1)

            act.wait_ge(v_vec, 1)
            keys(0, x_bank)

            def turned_rows(l, n):
                for k in range(DK):
                    act.wait_ge(att[l]["t_xt"], DK * n + k + 1)
                    nc.scalar.copy(xn_t[:, k, :], t_bank[k][:]).then_inc(att[l]["a_xt"], 1)

            def queries(l, n):
                for m in range(DK):
                    act.wait_ge(att[l]["t_q"], DK * n + m + 1)
                    nc.scalar.activation(q_t[:, m, :], x_bank[m][:], ACT.Identity, bias=bq_s[:, l, m:m + 1],
                                         scale=QSCALE).then_inc(att[l]["a_q"], 1)

            def exps(l, n, i):
                act.wait_ge(att[l]["v_sub"], TB * n + i + 1)
                nc.scalar.activation(probs[:, i % 2, :], probs[:, i % 2, :], ACT.Exp).then_inc(att[l]["a_exp"], 1)

            def router_rows(b):
                for k in range(DK):
                    act.wait_ge(r_t, DK * b + k + 1)
                    nc.scalar.copy(xn_t[:, k, :], t_bank[k][:]).then_inc(r_e, 1)

            def ternary_weights():
                n = 0
                for dst in (gate_t, up_t, down_t):
                    flat_dst = flat(dst[:])
                    for c in range(4):
                        act.wait_ge(t_bit, n + 1)
                        nc.scalar.copy(flat_dst[:, 512 * c:512 * c + 512],
                                       bank[n % 4][:, 0:256].bitcast(BF16)).then_inc(a_bit, 1)
                        n += 1

            def attention(l, b, last_batch):
                s = att[l]

                def turned(i):
                    act.wait_ge(s["t_pt"], 2 * (TB * b + i) + 2)
                    nc.scalar.copy(flat(probs_t[:, i % 2, 4:8, :]), t_bank[1][:]).then_inc(s["a_pt"], 1)

                turned(0)
                exps(l, b, 2)
                turned(1)
                exps(l, b, 3)
                turned(2)
                turned(3)
                if not last_batch:
                    turned_rows(l, b + 1)
                    queries(l, b + 1)
                if l == 0:
                    if last_batch:
                        ternary_weights()
                    out_bank = [*t_bank, *x_bank]
                    for m in range(FK):
                        act.wait_ge(s["t_h"], FK * b + m + 1)
                        nc.scalar.activation(h1_t[:, m, :], out_bank[m][:], ACT.Relu,
                                             bias=vecs[:, 4 + m:5 + m]).then_inc(s["a_h"], 1)
                if not last_batch:
                    exps(l, b + 1, 0)
                if l == 0:
                    router_rows(b)
                if not last_batch:
                    exps(l, b + 1, 1)

            turned_rows(0, 0)
            act.wait_ge(v_bq, 2)
            queries(0, 0)
            act.wait_ge(d_rout, 16 * 7)
            nc.scalar.activation(tg[:], gates[:], ACT.Tanh).then_inc(a_tanh, 1)
            act.wait_ge(d_bit, 48)
            for w, raw in enumerate((bit_raw[:, 0, :], bit_raw[:, 1, :], bit_down)):
                nc.scalar.activation(flat(h1_t[:, :, :]), raw, ACT.Abs, accum_out=w_sum[:, w:w + 1]).then_inc(a_abs, 1)
                act.wait_ge(a_abs, w + 1)
            exps(0, 0, 0)
            exps(0, 0, 1)
            with act.Fori(0, B - 1) as b:
                attention(0, b, False)
            attention(0, B - 1, True)

            act.wait_ge(r_v, 2)
            nc.scalar.activation(l_exp[:], r_tmp[:], ACT.Exp).then_inc(r_exp, 1)
            act.wait_ge(p_kbd, DK * B)
            keys(1, t_bank)

            def expert_rows(t, par):
                act.wait_ge(m_t, t + 1)
                nc.scalar.copy(flat(xs_t[:, par, :, :]), bank[6 + par][:, 0:D]).then_inc(m_xt, 1)

            def expert_gate(t, q):
                act.wait_ge(m_up, 2 * t + q + 1)
                if not (t is 0):
                    act.wait_ge(m_act, 2 * t + q - 1)
                nc.scalar.activation(sil[:, q, :], bank[q][:], ACT.Silu).then_inc(m_sil, 1)

            def expert_out(t, par, n, stored):
                act.wait_ge(m_dn, t + 1)
                if stored:
                    act.wait_ge(m_st[par], 16 * n)
                nc.scalar.copy(ys[:, par, :], bank[4 + par][:, 0:D]).then_inc(m_y, 1)
                act.wait_ge(m_y, t + 1)
                act.dma_start(slots_y[bass.ds(t * P, P), :], ys[:, par, :]).then_inc(m_st[par], 16)

            def expert_tile(t, par, n, first_tile, last_tile):
                expert_gate(t, 0)
                if not first_tile:
                    m = n if par else n - 1
                    expert_out(t - 1, 1 - par, m, not (m is 0))
                if not last_tile:
                    expert_rows(t + 1, 1 - par)
                expert_gate(t, 1)

            expert_rows(0, 0)
            expert_tile(0, 0, 0, True, False)
            expert_tile(1, 1, 0, False, False)
            with act.Fori(1, SLOT_TILES // 2) as i:
                expert_tile(2 * i, 0, i, False, False)
                expert_tile(2 * i + 1, 1, i, False, False)
            expert_tile(SLOT_TILES - 1, 0, SLOT_TILES // 2, False, True)
            expert_out(SLOT_TILES - 1, 0, SLOT_TILES // 2, True)

            turned_rows(1, 0)
            queries(1, 0)
            exps(1, 0, 0)
            exps(1, 0, 1)
            with act.Fori(0, B - 1) as b:
                attention(1, b, False)
            attention(1, B - 1, True)

            def ff_rows(t, par):
                act.wait_ge(f["t_x"], t + 1)
                nc.scalar.copy(flat(x_qt[:, par, :, :]), t_bank[0][:, 0:P].bitcast(BF16)).then_inc(f["a_x"], 1)

            def ff_batch(b, first):
                for i in range(TB):
                    t = TB * b + i
                    act.wait_ge(f["unit"], 2 * (2 * b + i // 2) + 2)
                    for c in range(2):
                        act.wait_ge(f["t_gu"], 2 * t + c + 1)
                        nc.scalar.activation(sil_g[:, i % 2, 512 * c:512 * c + 512], bank[c][:], ACT.Silu,
                                             scale=x_unit[:, 0, i:i + 1]).then_inc(f["a_sil"], 1)
                    ff_rows(t + 1, (i + 1) % 2)
                    if not (first and i < 2):
                        ff_hidden(t - 2, i % 2)

            def ff_hidden(t, par):
                act.wait_ge(f["t_h"], t + 1)
                nc.scalar.copy(flat(h_qt[:, par, :, :]), t_bank[1][:].bitcast(BF16)).then_inc(f["a_h"], 1)

            ff_rows(0, 0)
            ff_batch(0, True)
            with act.Fori(1, B) as b:
                ff_batch(b, False)
            ff_hidden(NT - 2, 0)
            ff_hidden(NT - 1, 1)

        @block.vector
        def _(dve):
            nc.vector.memset(carried[:, 0:1], 0.0).then_inc(v_zero, 1)
            nc.vector.memset(zeros[:], 0.0).then_inc(v_zero, 1)
            nc.vector.memset(x_res[:, NT:NT + TB, :], 0.0).then_inc(v_zero, 1)
            for l in range(2):
                nc.vector.memset(v_bd[l][:], 0.0).then_inc(v_zero, 1)
            dve.wait_ge(v_zero, 5)
            for l in range(2):
                nc.vector.memset(v_bd[l][0:M, :, :, 2 * HD:2 * HD + 1], 1.0).then_inc(v_zero, 1)
                nc.vector.memset(v_bd[l][M:P, :, :, 2 * HD + 1:PW], 1.0).then_inc(v_zero, 1)

            def carry_wait():
                nc.vector.tensor_copy(carried[:, 1:2], carried[:, 0:1])

            def layer_norm(s, n, t0, out, tiles=range(TB)):
                carry_wait()
                for i in tiles:
                    last = nc.vector.bn_stats(stats[:, i, :], x_res[:, bass.ds(t0 + (i - tiles[0]), 1), :].rearrange(
                        "p o d -> p (o d)"))
                last.then_inc(s["stats"], 1)
                dve.wait_ge(s["stats"], n)
                carry_wait()
                for i in tiles:
                    last = nc.vector.bn_aggr(mv[:, i, :], stats[:, i, :])
                last.then_inc(s["aggr"], 1)
                dve.wait_ge(s["aggr"], n)
                dve.wait_ge(s["rstd"], n)
                for i in tiles:
                    last = nc.vector.tensor_scalar(
                        out[:, i, :], x_res[:, bass.ds(t0 + (i - tiles[0]), 1), :].rearrange("p o d -> p (o d)"),
                        mv[:, i, 0:1], rstd[:, i:i + 1], ALU.subtract, ALU.mult)
                last.then_inc(s["xn"], 1)

            dve.wait_ge(t_vec, 1)
            nc.vector.tensor_copy(vecs[:], t_bank[0][:, 0:12]).then_inc(v_vec, 1)
            dve.wait_ge(t_ctx, 1)
            for c, (dst, src) in enumerate(((ctx_ta, x_bank[0]), (ctx_tb, x_bank[1]))):
                rows = (P, C - P)[c]
                for twice in range(2):
                    nc.vector.tensor_copy(dst[:, :, twice, :], src[0:rows, 0:B * M].rearrange(
                        "p (b s) -> p b s", b=B)).then_inc(v_ctx, 1)
            dve.wait_ge(v_vec, 1)
            for l in range(2):
                nc.vector.tensor_scalar(bq_s[:, l, :], vecs[:, 8 * l:8 * l + 2], QSCALE, None, ALU.mult).then_inc(v_bq, 1)
            dve.wait_ge(d_x0, 16)
            layer_norm(ln["l0"], 1, 0, xn)

            def spread_values(l):
                dve.wait_ge(t_v, l + 1)
                for half in range(2):
                    lo = half * M
                    for c in range(2):
                        src = s_bank[0][c][lo:lo + M, :].rearrange("p (b j a) -> p b j a", b=2, j=PAIRS)
                        bias = bv[l][lo:lo + M, :].rearrange("p (j a) -> p j a", j=PAIRS)
                        for b in range(2):
                            last = nc.vector.tensor_tensor(
                                v_bd[l][lo:lo + M, 2 * c + b, :, half * HD:half * HD + HD],
                                src[:, b, :, half * HD:half * HD + HD], bias[:, :, half * HD:half * HD + HD], ALU.add)
                        last.then_inc(v_vbd, 1)

            dve.wait_ge(v_zero, 9)
            dve.wait_ge(d_bv, 16)
            spread_values(0)

            def scores(l, n, i):
                s = att[l]
                g = TB * n + i
                dve.wait_ge(s["t_s"], g + 1)
                for m in range(DK):
                    last = nc.vector.tensor_reduce(s_max[:, i, HC * m:HC * m + HC],
                                                   s_bank[i % 2][m][:].rearrange("p (h s) -> p h s", h=HC),
                                                   AX, ALU.max)
                last.then_inc(s["v_max"], 1)
                dve.wait_ge(s["v_max"], g + 1)
                if i >= 2:
                    dve.wait_ge(s["t_pt"], 2 * g - 2)
                for m in range(DK):
                    last = nc.vector.tensor_tensor(
                        probs[:, i % 2, 512 * m:512 * m + 512].rearrange("p (h s) -> p h s", h=HC),
                        s_bank[i % 2][m][:].rearrange("p (h s) -> p h s", h=HC),
                        s_max[:, i, HC * m:HC * m + HC].unsqueeze(2).to_broadcast([P, HC, M]), ALU.subtract)
                last.then_inc(s["v_sub"], 1)

            scores(0, 0, 0)
            scores(0, 0, 1)
            dve.wait_ge(d_x, 16 * (B - 1))
            dve.wait_ge(att[0]["t_xt"], DK)
            layer_norm(ln["l0"], 2, TB, xn)
            dve.wait_ge(d_rout, 16 * 7)
            dve.wait_ge(a_tanh, 1)
            for l in range(2):
                nc.vector.tensor_scalar(bo[l][:], bo[l][:], tg[:, l:l + 1], None, ALU.mult).then_inc(v_bo, 1)
            dve.wait_ge(t_abs, 1)
            nc.vector.tensor_scalar(w_mean[:], t_bank[1][:, 0:3], 1.0 / (INNER * D), EPS, ALU.mult,
                                    ALU.max).then_inc(v_wm, 1)
            dve.wait_ge(v_wm, 1)
            nc.vector.reciprocal(w_inv[:], w_mean[:]).then_inc(v_wm, 1)
            nc.vector.tensor_scalar(wd_g[:], w_mean[:, 2:3], tg[:, 3:4], 1.0 / 127.0, ALU.mult, ALU.mult).then_inc(v_wm, 1)

            def attention(l, b, last_batch):
                s = att[l]
                phase = ln["l0" if l == 0 else "l1"]

                def turned(i):
                    dve.wait_ge(s["t_pt"], 2 * (TB * b + i) + 1)
                    nc.vector.tensor_copy(flat(probs_t[:, i % 2, 0:4, :]), t_bank[0][:]).then_inc(s["v_pt"], 1)

                def normalise(i):
                    g = TB * b + i
                    dve.wait_ge(s["t_o"], g + 1)
                    o = x_bank[0][:, 0:PAIRS * PW].rearrange("p (j a) -> p j a", j=PAIRS)
                    nc.vector.reciprocal(o_rcp[:, i, :].rearrange("p (j a) -> p j a", j=PAIRS),
                                         o[:, :, 2 * HD:PW]).then_inc(s["v_rcp"], 1)
                    dve.wait_ge(s["v_rcp"], g + 1)
                    for a in range(2):
                        last = nc.vector.tensor_tensor(
                            o_n[:, i % 2, :].rearrange("p (j a d) -> p j a d", j=PAIRS, a=2)[:, :, a, :],
                            o[:, :, HD * a:HD * a + HD],
                            o_rcp[:, i, :].rearrange("p (j a) -> p j a", j=PAIRS)[:, :, a:a + 1].to_broadcast(
                                [P, PAIRS, HD]), ALU.mult)
                    last.then_inc(s["v_o"], 1)

                def turned_out(i):
                    dve.wait_ge(s["t_ot"], TB * b + i + 1)
                    nc.vector.tensor_copy(o_t[:, :, P * i:P * i + P], x_bank[1][:, 0:D].rearrange(
                        "p (k t) -> p k t", k=DK)).then_inc(s["v_ot"], 1)

                turned(0)
                scores(l, b, 2)
                normalise(0)
                turned(1)
                scores(l, b, 3)
                turned_out(0)
                normalise(1)
                turned(2)
                turned_out(1)
                normalise(2)
                turned(3)
                turned_out(2)
                normalise(3)
                turned_out(3)
                if not last_batch:
                    dve.wait_ge(s["t_xt"], DK * b + 2 * DK)
                    layer_norm(phase, b + 3, TB * b + 2 * TB, xn)
                if l == 1 and not last_batch:
                    scores(l, b + 1, 0)
                    scores(l, b + 1, 1)
                dve.wait_ge(s["p_xb"], b + 1)
                out_bank = [*t_bank, *x_bank]
                for i in range(TB):
                    g = TB * b + i
                    dve.wait_ge(s["t_y"], g + 1)
                    row = x_res[:, bass.ds(g, 1), :].rearrange("p o d -> p (o d)")
                    nc.vector.scalar_tensor_tensor(row, out_bank[i][:, 0:D], tg[:, l:l + 1], row, ALU.mult,
                                                   ALU.add).then_inc(s["v_y"], 1)
                if l == 0:
                    dve.wait_ge(s["v_y"], TB * b + TB)
                    layer_norm(ln["rt"], b + 1, TB * b, xn2)
                    if not last_batch:
                        scores(l, b + 1, 0)
                        scores(l, b + 1, 1)
                    dve.wait_ge(r_l, b + 1)
                    nc.vector.tensor_tensor(logits[:, bass.ds(b * TB, TB), :],
                                            x_bank[0][:, 0:TB * E].rearrange("p (t e) -> p t e", t=TB),
                                            rb[:].unsqueeze(1).to_broadcast([P, TB, E]), ALU.add).then_inc(r_lg, 1)

            with dve.Fori(0, B - 1) as b:
                attention(0, b, False)
            attention(0, B - 1, True)

            dve.wait_ge(r_lg, B)
            nc.vector.tensor_reduce(l_max[:], logits[:], AX, ALU.max).then_inc(r_v, 1)
            dve.wait_ge(r_v, 1)
            nc.vector.tensor_tensor(r_tmp[:], logits[:], l_max[:].unsqueeze(2).to_broadcast([P, NT, E]),
                                    ALU.subtract).then_inc(r_v, 1)
            nc.vector.tensor_tensor(onehot[:], logits[:], l_max[:].unsqueeze(2).to_broadcast([P, NT, E]),
                                    ALU.is_equal).then_inc(r_v, 1)
            dve.wait_ge(r_v, 3)
            nc.vector.scalar_tensor_tensor(count[:], onehot[:], -float(E),
                                           expert_no8[:].unsqueeze(1).to_broadcast([P, NT, E]), ALU.mult,
                                           ALU.add).then_inc(r_v, 1)
            dve.wait_ge(r_v, 4)
            nc.vector.tensor_reduce(first[:], count[:], AX, ALU.min).then_inc(r_v, 1)
            dve.wait_ge(r_v, 5)
            nc.vector.tensor_tensor(onehot[:], expert_no[:].unsqueeze(1).to_broadcast([P, NT, E]),
                                    first[:].unsqueeze(2).to_broadcast([P, NT, E]), ALU.is_equal).then_inc(r_hot, 1)
            dve.wait_ge(r_exp, 1)
            nc.vector.tensor_reduce(l_sum[:], l_exp[:], AX, ALU.add).then_inc(r_v, 1)
            dve.wait_ge(r_v, 6)
            nc.vector.reciprocal(l_sum[:], l_sum[:]).then_inc(r_v, 1)
            dve.wait_ge(r_v, 7)
            nc.vector.tensor_scalar(weight[:], l_sum[:], tg[:, 2:3], None, ALU.mult).then_inc(r_v, 1)
            dve.wait_ge(r_cnt, 1)
            nc.vector.tensor_copy(count[:], s_bank[1][1][:, 0:NT * E].rearrange("p (t e) -> p t e", t=NT)).then_inc(r_v, 1)
            dve.wait_ge(r_v, 9)
            for e in range(E):
                last = nc.vector.tensor_tensor_scan(upto[:, e, :], count[:, :, e], zeros[:, 0:NT], 0.0, ALU.add, ALU.add)
            last.then_inc(r_v, 1)
            dve.wait_ge(r_v, 10)
            nc.vector.tensor_tensor(more[:], upto[:, :, NT - 1:NT].to_broadcast([P, E, NT]),
                                    tile_edge[:].unsqueeze(1).to_broadcast([P, E, NT]), ALU.is_gt).then_inc(r_v, 1)
            dve.wait_ge(r_v, 11)
            nc.vector.tensor_reduce(tiles_of[:], more[:], AX, ALU.add).then_inc(r_v, 1)
            dve.wait_ge(r_v, 12)
            nc.vector.tensor_scalar(tiles_of[:], tiles_of[:], 1.0, None, ALU.max).then_inc(r_v, 1)
            dve.wait_ge(r_v, 13)
            nc.vector.tensor_tensor_scan(tile_end[:], tiles_of[:], zeros[:, 0:E], 0.0, ALU.add, ALU.add).then_inc(r_v, 1)
            dve.wait_ge(r_v, 14)
            nc.vector.tensor_tensor(past[:], tile_end[:].unsqueeze(1).to_broadcast([P, SLOT_TILES, E]),
                                    slot_tile_no[:].unsqueeze(2).to_broadcast([P, SLOT_TILES, E]), ALU.is_le).then_inc(r_v, 1)
            nc.vector.tensor_tensor(slot_base[:], tile_end[:], tiles_of[:], ALU.subtract).then_inc(r_v, 1)
            dve.wait_ge(r_v, 16)
            nc.vector.tensor_reduce(expert_f[:], past[:], AX, ALU.add).then_inc(r_v, 1)
            dve.wait_ge(r_v, 17)
            nc.vector.tensor_scalar(expert_of[:], expert_f[:], float(E - 1), None, ALU.min).then_inc(r_exps, 1)
            nc.vector.tensor_tensor(r_tmp[:], upto[:].rearrange("p e t -> p t e"), count[:], ALU.subtract).then_inc(r_v, 1)
            dve.wait_ge(r_v, 18)
            nc.vector.tensor_tensor(r_tmp[:], s_bank[1][0][:, 0:NT * E].rearrange("p (t e) -> p t e", t=NT), r_tmp[:],
                                    ALU.add).then_inc(r_v, 1)
            dve.wait_ge(r_v, 19)
            nc.vector.scalar_tensor_tensor(r_tmp[:], slot_base[:].unsqueeze(1).to_broadcast([P, NT, E]), float(P),
                                           r_tmp[:], ALU.mult, ALU.add).then_inc(r_v, 1)
            dve.wait_ge(r_v, 20)
            nc.vector.tensor_tensor(r_tmp[:], r_tmp[:], onehot[:], ALU.mult).then_inc(r_v, 1)
            dve.wait_ge(r_v, 21)
            nc.vector.tensor_reduce(pos_f[:], r_tmp[:], AX, ALU.add).then_inc(r_v, 1)
            dve.wait_ge(r_v, 22)
            nc.vector.tensor_copy(pos[:], pos_f[:]).then_inc(r_pos, 1)

            spread_values(1)

            def expert_tile(t, par):
                for q in range(2):
                    dve.wait_ge(m_sil, 2 * t + q + 1)
                    nc.vector.tensor_tensor(flat(act_t[:, par, 4 * q:4 * q + 4, :]), bank[2 + q][:], sil[:, q, :],
                                            ALU.mult).then_inc(m_act, 1)

            expert_tile(0, 0)
            expert_tile(1, 1)
            with dve.Fori(1, SLOT_TILES // 2) as i:
                expert_tile(2 * i, 0)
                expert_tile(2 * i + 1, 1)
            expert_tile(SLOT_TILES - 1, 0)

            for b in range(B):
                dve.wait_ge(g_y[b], 16 * TB)
                for t in range(TB * b, TB * b + TB):
                    nc.vector.scalar_tensor_tensor(x_res[:, t, :], xn_all[:, t, :], weight[:, t:t + 1], x_res[:, t, :],
                                                   ALU.mult, ALU.add).then_inc(g_x, 1)
                if b < 2:
                    dve.wait_ge(g_x, TB * b + TB)
                    if b:
                        dve.wait_ge(att[1]["t_xt"], DK)
                    layer_norm(ln["l1"], b + 1, TB * b, xn)
            dve.wait_ge(g_x, NT)
            scores(1, 0, 0)
            scores(1, 0, 1)
            with dve.Fori(0, B - 1) as b:
                attention(1, b, False)
            attention(1, B - 1, True)

            def ff_rows(g, j):
                pair = slice(2 * j, 2 * j + 2)
                layer_norm(ln["ff"], g + 1, 2 * g, xn, range(2 * j, 2 * j + 2))
                dve.wait_ge(ln["ff"]["xn"], g + 1)
                nc.vector.tensor_reduce(x_abs[:, pair], xn[:, pair, :], AX, ALU.max,
                                        apply_absolute_value=True).then_inc(f["max"], 1)
                dve.wait_ge(f["max"], g + 1)
                nc.vector.tensor_scalar(x_abs[:, pair], x_abs[:, pair], EPS, None, ALU.max).then_inc(f["clip"], 1)
                dve.wait_ge(f["clip"], g + 1)
                nc.vector.reciprocal(x_inv[:, pair], x_abs[:, pair]).then_inc(f["inv"], 1)
                for w in range(2):
                    nc.vector.tensor_scalar(x_unit[:, w, pair], x_abs[:, pair], w_mean[:, w:w + 1], 1.0 / 127.0,
                                            ALU.mult, ALU.mult).then_inc(f["unit"], 1)
                dve.wait_ge(f["inv"], g + 1)
                nc.vector.tensor_scalar(x_scale[:, pair], x_inv[:, pair], 127.0, None, ALU.mult).then_inc(f["mul"], 1)

            def ff_hidden(t, i, first):
                par = i % 2
                one = slice(par, par + 1)
                if not first:
                    dve.wait_ge(f["hq"], t - 1)
                for c in range(2):
                    dve.wait_ge(f["a_sil"], 2 * t + c + 1)
                    nc.vector.scalar_tensor_tensor(h_f[:, par, 512 * c:512 * c + 512], bank[2 + c][:],
                                                   x_unit[:, 1, i:i + 1], sil_g[:, par, 512 * c:512 * c + 512],
                                                   ALU.mult, ALU.mult).then_inc(f["v_h"], 1)
                dve.wait_ge(f["v_h"], 2 * t + 2)
                nc.vector.tensor_reduce(h_abs[:, one], h_f[:, par, :], AX, ALU.max,
                                        apply_absolute_value=True).then_inc(f["hmax"], 1)
                dve.wait_ge(f["hmax"], t + 1)
                nc.vector.tensor_scalar(h_abs[:, one], h_abs[:, one], EPS, None, ALU.max).then_inc(f["hclip"], 1)
                dve.wait_ge(f["hclip"], t + 1)
                nc.vector.reciprocal(h_inv[:, one], h_abs[:, one]).then_inc(f["hinv"], 1)
                dve.wait_ge(f["hinv"], t + 1)
                nc.vector.tensor_scalar(h_scale[:, one], h_inv[:, one], 127.0, None, ALU.mult).then_inc(f["hmul"], 1)

            def ff_out(t, i):
                dve.wait_ge(f["t_y"], t + 1)
                dve.wait_ge(f["hunit"], t + 1)
                row = x_res[:, bass.ds(t, 1), :].rearrange("p o d -> p (o d)")
                nc.vector.scalar_tensor_tensor(row, x_bank[i % 2][:, 0:D], h_unit[:, i:i + 1], row, ALU.mult,
                                               ALU.add).then_inc(f["v_y"], 1)

            def ff_batch(b, first):
                for i in range(TB):
                    t = TB * b + i
                    ff_hidden(t, i, first and i < 2)
                    if not (first and i < 2):
                        ff_out(t - 2, (i - 2) % TB)
                    nc.vector.tensor_scalar(h_unit[:, i:i + 1], h_abs[:, i % 2:i % 2 + 1], wd_g[:, 0:1], None,
                                            ALU.mult).then_inc(f["hunit"], 1)
                    if i % 2 == 0:
                        ff_rows(2 * b + i // 2 + 1, (i // 2 + 1) % 2)

            dve.wait_ge(att[1]["v_y"], NT)
            ff_rows(0, 0)
            ff_batch(0, True)
            with dve.Fori(1, B) as b:
                ff_batch(b, False)
            ff_out(NT - 2, TB - 2)
            ff_out(NT - 1, TB - 1)


_INS = ["x", "ctx_768", "g_xattn", "g_ffn", "L0_xattn_Wq", "L0_xattn_bq", "L0_xattn_Wk", "L0_xattn_bk", "L0_xattn_Wv",
        "L0_xattn_bv", "L0_xattn_W1", "L0_xattn_b1", "L0_xattn_W2", "L0_xattn_b2", "L0_ffn_router_w",
        "L0_ffn_router_b", "L0_ffn_w1", "L0_ffn_w2", "L1_xattn_Wq", "L1_xattn_bq", "L1_xattn_Wk", "L1_xattn_bk",
        "L1_xattn_Wv", "L1_xattn_bv", "L1_xattn_Wo", "L1_xattn_bo", "L1_ffn_w_gate", "L1_ffn_w_up", "L1_ffn_w_down"]


def kernel(**inputs):
    import concourse.bacc as bacc
    from concourse.bass_utils import run_bass_kernel_spmd

    nc = bacc.Bacc("TRN2", target_bir_lowering=False, num_devices=1)
    arrays, inp = {}, {}
    for name in _INS:
        a = np.ascontiguousarray(inputs[name])
        arrays[f"in_{name}"] = a
        inp[name] = nc.dram_tensor(f"in_{name}", a.shape, mybir.dt.from_np(a.dtype), kind="ExternalInput").ap()
    out = nc.dram_tensor("out_rows", (B, N, D), F32, kind="ExternalOutput").ap()
    slots_x = nc.dram_tensor("slots_x", (SLOTS, D), F32, kind="Internal").ap()
    slots_y = nc.dram_tensor("slots_y", (SLOTS, D), F32, kind="Internal").ap()
    flamingo(nc, inp, out, slots_x, slots_y)
    r = run_bass_kernel_spmd(nc, [arrays], core_ids=[0])
    return r.results[0]["out_rows"]
```

```python
from contextlib import ExitStack

import numpy as np
import concourse.bass as bass
from concourse import mybir

F32 = mybir.dt.float32
F32R = mybir.dt.float32r
BF16 = mybir.dt.bfloat16
I32 = mybir.dt.int32
U32 = mybir.dt.uint32
ALU = mybir.AluOpType
ACT = mybir.ActivationFunctionType
AX = mybir.AxisListType.X

P = 128
B, N, D = 4, 512, 256
M, C = 64, 192
H, HD = 16, 16
TB = N // P
NT = B * TB
DK = D // P
HC = P // HD
PAIRS = H // 2
F1 = 2 * D
FK = F1 // P
E, FE = 8, 1024
EK = FE // P
SLOT_PAIRS = (NT + E) // 2
SLOT_TILES = 2 * SLOT_PAIRS
READ_TILES = SLOT_TILES + 1
INNER = 1024
GATHERS = (range(0, TB // 2), range(TB // 2, TB), range(TB, 2 * TB), range(2 * TB, NT))
IK = INNER // P
EPS = 1e-5
QSCALE = float(HD) ** -0.5
ROUND = 1.5 * 2.0 ** 23


def flamingo(nc, inp, out, token_rows, slots_y):
    with ExitStack() as ctx:
        def sb(name, shape, dt=F32):
            return ctx.enter_context(nc.sbuf_tensor(name, shape, dt))

        def under(name, tensor, shape, at=0):
            size = int(np.prod(tensor.shape[1:])) * 4
            return nc.alloc_sbuf_tensor_at(name, shape, F32R, offset=nc.sbuf_base - size + at)

        def sem(name):
            return ctx.enter_context(nc.semaphore(name))

        def flat(ap):
            return ap.rearrange("p a b -> p (a b)")

        bank = [ctx.enter_context(nc.psum_tensor(f"bank{i}", [P, 512], F32)) for i in range(8)]
        s_bank = [bank[0:2], bank[2:4]]
        t_bank = bank[4:6]
        x_bank = bank[6:8]
        logit_out = x_bank[1][:, 2 * P:2 * P + TB * E]
        sum_out = x_bank[1][:, 2 * P + TB * E:2 * P + TB * E + 1]
        out_bank = [[*t_bank, *x_bank], [*reversed(t_bank), *x_bank]]

        ident = sb("ident", [P, P])
        ident_b = sb("ident_b", [P, P], BF16)
        ones = sb("ones", [P, P])
        before = sb("before", [P, P])
        head_mask = sb("head_mask", [P, HC])
        minus_half = sb("minus_half", [P, TB])
        eps = sb("eps", [P, TB])
        expert_no = sb("expert_no", [P, E])
        expert_no8 = sb("expert_no8", [P, E])
        tile_edge = sb("tile_edge", [P, NT])
        slot_tile_no = sb("slot_tile_no", [P, SLOT_TILES])
        slot_edge = sb("slot_edge", [P, READ_TILES + 1])
        slot_no = sb("slot_no", [P, P])
        row_no = sb("row_no", [P, 1])

        x_res = sb("x_res", [P, NT + TB, D])
        xn_all = sb("xn_all", [P, NT, D])
        ew2_hi = under("ew2_hi", xn_all, [P, 2, EK, D])
        w1_hi = under("w1_hi", xn_all, [P, DK, F1])
        w2_hi = under("w2_hi", xn_all, [P, FK, D], DK * F1 * 4)
        h1_hi = under("h1_hi", xn_all, [P, FK, N], (DK * F1 + FK * D) * 4)
        zeros = x_res[:, NT, :]
        xn = sb("xn", [P, TB, D])
        xn_t = sb("xn_t", [P, DK, N])
        stats = sb("stats", [P, TB, 6])
        carried = sb("carried", [P, 11 + 2 * TB])
        mv = sb("mv", [P, TB, 2])
        var_eps = sb("var_eps", [P, TB])
        rstd = sb("rstd", [P, TB])

        ctx_rows = sb("ctx_rows", [P, 2, C])
        ctx_ta = sb("ctx_ta", [P, B, 2, M])
        ctx_tb = sb("ctx_tb", [C - P, B, 2, M])
        vec_rows = sb("vec_rows", [12, P])
        vecs = sb("vecs", [P, 12])
        bq_s = sb("bq_s", [P, 2, DK])
        gates = sb("gates", [P, 4])
        tg = sb("tg", [P, 4])
        wq = [sb(f"wq{l}", [P, DK, D]) for l in range(2)]
        wka = [sb(f"wka{l}", [P, D]) for l in range(2)]
        wkb = [sb(f"wkb{l}", [C - P, D]) for l in range(2)]
        wva = [sb(f"wva{l}", [P, D]) for l in range(2)]
        wvb = [sb(f"wvb{l}", [C - P, D]) for l in range(2)]
        bv = [sb(f"bv{l}", [P, D]) for l in range(2)]
        bo = [sb(f"bo{l}", [P, D]) for l in range(2)]
        w1 = sb("w1", [P, DK, F1])
        w1_lo = under("w1_lo", w1, [P, DK, F1])
        w2 = sb("w2", [P, FK, D])
        w2_lo = under("w2_lo", w2, [P, FK, D])
        wo = sb("wo", [P, DK, D])
        rw = sb("rw", [P, DK, E])
        rb = sb("rb", [P, E])
        k_t = sb("k_t", [P, DK, B * M])
        k_bd = sb("k_bd", [P, DK, B, HC * M])
        v_pair = [sb(f"v_pair{l}", [P, B, PAIRS, HD]) for l in range(2)]
        v_bd = sb("v_bd", [P, DK * 512 + P])

        q_t = sb("q_t", [P, DK, N])
        s_max = sb("s_max", [P, TB, H])
        probs = sb("probs", [P, 2, H * M])
        probs_t = sb("probs_t", [P, 2, PAIRS, P])
        act_lo = under("act_lo", probs_t, [P, 2, EK, P])
        p_sum = sb("p_sum", [P, TB, H])
        p_rcp = sb("p_rcp", [P, TB, H])
        o_t = sb("o_t", [P, DK, N])
        o_hi = under("o_hi", o_t, [P, DK, N])
        h1_t = sb("h1_t", [P, FK, N])
        h1_lo = under("h1_lo", h1_t, [P, FK, N])
        act_hi = under("act_hi", h1_t, [P, 2, EK, P])

        ew1 = sb("ew1", [P, 2, DK, 2 * FE])
        o_lo = under("o_lo", ew1, [P, DK, N], 3 * IK * D * 4)
        ew2 = sb("ew2", [P, 2, EK, D])
        ew2_lo = under("ew2_lo", ew2, [P, 2, EK, D])
        xs = sb("xs", [P, 2, D])
        xs_t = q_t[:, 0, :].rearrange("p (s k t) -> p s k t", s=2, k=DK)
        sil = probs[:, :, 0:512]
        act_t = probs_t
        ys = xn[:, 0:2, :]

        logits = sb("logits", [P, NT, E])
        l_max = sb("l_max", [P, NT])
        l_exp = sb("l_exp", [P, NT, E])
        l_sum = sb("l_sum", [P, NT])
        weight = sb("weight", [P, NT])
        onehot = sb("onehot", [P, NT, E])
        first = sb("first", [P, NT])
        r_tmp = sb("r_tmp", [P, NT, E])
        count = sb("count", [P, NT, E])
        upto = sb("upto", [P, E, NT])
        more = sb("more", [P, E, NT])
        tiles_of = sb("tiles_of", [P, E])
        tile_end = sb("tile_end", [P, E])
        slot_base = sb("slot_base", [P, E])
        pos_f = sb("pos_f", [P, NT])
        pos = sb("pos", [P, NT], U32)
        above = flat(xn[:])[:, 0:NT * (READ_TILES + 1)].rearrange("p (t k) -> p t k", t=NT)
        in_tile = flat(xn[:])[:, NT * (READ_TILES + 1):NT * (2 * READ_TILES + 1)].rearrange("p (t k) -> p t k", t=NT)
        in_slot = flat(h1_t[:, 0:2, :]).bitcast(BF16).rearrange("p (t s) -> p t s", t=NT)
        ids = flat(h1_t[:, 2:4, :]).bitcast(BF16)[:, 0:2 * NT * READ_TILES].rearrange("p (t w k) -> p t w k", t=NT, w=2)
        token_f = flat(xn[:])[:, 0:READ_TILES]
        n_above = sb("n_above", [P, NT])
        pos_lo = sb("pos_lo", [P, NT])
        token_of = sb("token_of", [P, READ_TILES], U32)
        token_now = sb("token_now", [P, 2], U32)
        past = sb("past", [P, SLOT_TILES, E])
        expert_f = sb("expert_f", [P, SLOT_TILES])
        end_of = sb("end_of", [P, E], I32)
        expert_of = sb("expert_of", [P, SLOT_TILES], I32)

        bit_raw = ew1[:].rearrange("p s k f -> p (s k f)")[:, 0:3 * IK * D].rearrange(
            "p (w a) -> p w a", w=3)
        ew2_flat = ew2[:].rearrange("p s k f -> p (s k f)")
        bit_q = ew2_flat[:, 0:3 * IK * D // 2].bitcast(BF16).rearrange("p (w a) -> p w a", w=3)
        xn2 = ew2_flat[:, 3 * IK * D // 2:3 * IK * D // 2 + TB * D].rearrange("p (i d) -> p i d", i=TB)
        w_sum = sb("w_sum", [P, 3])
        w_mean = sb("w_mean", [P, 3])
        w_inv = sb("w_inv", [P, 3])
        gate_t = sb("gate_t", [P, DK, INNER], BF16)
        up_t = sb("up_t", [P, DK, INNER], BF16)
        down_t = sb("down_t", [P, IK, D], BF16)
        wd_g = sb("wd_g", [P, 1])

        x_q = flat(xs[:]).bitcast(BF16).rearrange("p (s d) -> p s d", s=TB)
        x_qt = flat(ew1[:, 0, :, :])[:, 0:NT * D // 2].bitcast(BF16).rearrange("p (t k i) -> p t k i", t=NT, k=DK)
        sil_g = probs
        h_f = probs_t[:, :, :, :].rearrange("p s k t -> p s (k t)")
        h_q = flat(h1_t[:, 0:2, :]).bitcast(BF16).rearrange("p (s k) -> p s k", s=2)
        h_qt = flat(h1_t[:, 2:4, :]).bitcast(BF16).rearrange("p (s k t) -> p s k t", s=2, k=IK)
        y_f = xn[:, 0:2, :]
        x_abs = sb("x_abs", [P, TB])
        x_scale = sb("x_scale", [P, TB])
        x_unit = flat(past[:])[:, 0:2 * NT].rearrange("p (w t) -> p w t", w=2)
        h_abs = sb("h_abs", [P, 2])
        h_scale = sb("h_scale", [P, 2])
        h_unit = sb("h_unit", [P, TB])

        d_ctx, d_kv0, d_vec, d_x0, d_x, d_q0, d_mlp, d_rout, d_l1, d_bit, d_bv = (
            sem(n) for n in ("d_ctx", "d_kv0", "d_vec", "d_x0", "d_x", "d_q0", "d_mlp", "d_rout", "d_l1", "d_bit",
                              "d_bv"))
        d_zero = sem("d_zero")
        p_const = sem("p_const")
        v_zero = sem("v_zero")
        a_tanh, v_bq, v_bo = sem("a_tanh"), sem("v_bq"), sem("v_bo")
        t_ctx, v_ctx = sem("t_ctx"), sem("v_ctx")
        t_k, a_k, p_kbd, t_v, v_vbd = sem("t_k"), sem("a_k"), sem("p_kbd"), sem("t_v"), sem("v_vbd")
        a_abs, t_abs, v_wm, v_wd = sem("a_abs"), sem("t_abs"), sem("v_wm"), sem("v_wd")
        v_tern, p_terq, t_bit, a_bit = sem("v_tern"), sem("p_terq"), sem("t_bit"), sem("a_bit")

        def ln_sems(ph):
            return {k: sem(f"ln_{k}_{ph}") for k in ("stats", "aggr", "eps", "rstd", "xn")}

        ln = {ph: ln_sems(ph) for ph in ("l0", "rt", "l1", "ff")}
        att = [{k: sem(f"{k}_l{l}") for k in (
            "t_xt", "a_xt", "t_q", "a_q", "t_s", "v_max", "v_sub", "a_exp", "t_pt", "a_pt",
            "t_o", "v_sum", "v_rcp", "p_norm", "v_bd", "a_o", "t_y", "v_y", "p_xb",
            *(("t_h", "a_h") if l == 0 else ()))}
            for l in range(2)]
        r_t, r_e, r_l, r_lg = sem("r_t"), sem("r_e"), sem("r_l"), sem("r_lg")
        d_rows = sem("d_rows")
        r_v, r_exp, r_cnt = sem("r_v"), sem("r_exp"), sem("r_cnt")
        r_hot, r_pos, r_exps = sem("r_hot"), sem("r_pos"), sem("r_exps")
        r_slot, r_id, r_inv, r_tok, p_tok = sem("r_slot"), sem("r_id"), sem("r_inv"), sem("r_tok"), sem("p_tok")
        p_xm = sem("p_xm")
        m_w1 = [sem(f"m_w1_{i}") for i in range(2)]
        m_w2 = [sem(f"m_w2_{i}") for i in range(2)]
        m_x = [sem(f"m_x_{i}") for i in range(2)]
        m_st = [sem(f"m_st_{i}") for i in range(2)]
        p_wlo, v_olo, v_hlo = sem("p_wlo"), sem("v_olo"), sem("v_hlo")
        m_hi, m_lo, a_w2, v_w2 = sem("m_hi"), sem("m_lo"), sem("a_w2"), sem("v_w2")
        m_t, m_xt, m_up, m_sil, m_act, m_dn, m_y = (
            sem(n) for n in ("m_t", "m_xt", "m_up", "m_sil", "m_act", "m_dn", "m_y"))
        g_y = [sem(f"g_y{i}") for i in range(len(GATHERS))]
        g_x = sem("g_x")
        f = {k: sem(f"f_{k}") for k in (
            "abs", "inv", "unit", "rnd", "xq", "t_x", "a_x", "t_gu", "a_sil", "v_h", "habs",
            "hinv", "hrnd", "hq", "hunit", "t_h", "a_h", "t_y", "a_y", "p_y")}
        d_out = sem("d_out")

        block = ctx.enter_context(nc.Block())

        def batch_of(ap, b):
            return ap[:, bass.ds(b * TB, TB), :]

        def slot_pairs(engine):
            engine.wait_ge(r_exps, 2)
            return (engine.value_load(end_of[0:1, E - 1:E], min_val=NT, max_val=SLOT_TILES - 1) + 1) // 2

        def next_expert(engine, t, prepare):
            e, before = (engine.value_load(expert_of[0:1, bass.ds(n, 1)], min_val=0, max_val=E - 1) for n in (t, t - 1))
            with engine.If(e != before):
                with engine.If(e < E - 1):
                    with engine.If(e % 2 == 0):
                        prepare(e + 1, 1)
                    with engine.Else():
                        prepare(e + 1, 0)

        @block.sync
        def _(sp):
            sp.dma_start(ctx_rows[:], inp["ctx_768"].rearrange("(t a) s c -> (a s) t c", t=2)).then_inc(d_ctx, 16)
            sp.dma_start(x_res[:, 0:TB, :], inp["x"][0].rearrange("(j p) d -> p j d", p=P)).then_inc(d_x0, 16)
            at = 0
            for name, rows in (("L0_xattn_bq", 2), ("L0_xattn_bk", 2), ("L0_xattn_b1", 4), ("L1_xattn_bq", 2),
                               ("L1_xattn_bk", 2)):
                sp.dma_start(vec_rows[at:at + rows, :], inp[name].rearrange("(m p) -> m p", p=P)).then_inc(d_vec, 16)
                at += rows

            def key_value_weights(l, s):
                sp.dma_start(wka[l][:], inp[f"L{l}_xattn_Wk"][0:P, :]).then_inc(s, 16)
                sp.dma_start(wkb[l][:], inp[f"L{l}_xattn_Wk"][P:C, :]).then_inc(s, 16)
                sp.dma_start(wva[l][:], inp[f"L{l}_xattn_Wv"][0:P, :]).then_inc(s, 16)
                sp.dma_start(wvb[l][:], inp[f"L{l}_xattn_Wv"][P:C, :]).then_inc(s, 16)

            key_value_weights(0, d_kv0)
            sp.dma_start(bv[0][:], inp["L0_xattn_bv"].partition_broadcast(P)).then_inc(d_bv, 16)
            sp.dma_start(wq[0][:], inp["L0_xattn_Wq"].rearrange("(k p) n -> p k n", p=P)).then_inc(d_q0, 16)
            for b in range(1, B):
                sp.dma_start(x_res[:, TB * b:TB * b + TB, :],
                             inp["x"][b].rearrange("(j p) d -> p j d", p=P)).then_inc(d_x, 16)
            sp.dma_start(gates[:, 0:2], inp["g_xattn"].partition_broadcast(P)).then_inc(d_rout, 16)
            sp.dma_start(gates[:, 2:4], inp["g_ffn"].partition_broadcast(P)).then_inc(d_rout, 16)
            sp.dma_start(bv[1][:], inp["L1_xattn_bv"].partition_broadcast(P)).then_inc(d_rout, 16)
            sp.dma_start(bo[0][:], inp["L0_xattn_b2"].partition_broadcast(P)).then_inc(d_rout, 16)
            sp.dma_start(bo[1][:], inp["L1_xattn_bo"].partition_broadcast(P)).then_inc(d_rout, 16)
            sp.dma_start(rb[:], inp["L0_ffn_router_b"].partition_broadcast(P)).then_inc(d_rout, 16)
            sp.dma_start(rw[:], inp["L0_ffn_router_w"].rearrange("(k p) e -> p k e", p=P)).then_inc(d_rout, 16)
            sp.dma_start(w1[:], inp["L0_xattn_W1"].rearrange("(k p) n -> p k n", p=P)).then_inc(d_mlp, 16)
            sp.dma_start(w2[:], inp["L0_xattn_W2"].rearrange("(k p) n -> p k n", p=P)).then_inc(d_mlp, 16)
            key_value_weights(1, d_l1)
            sp.dma_start(wq[1][:], inp["L1_xattn_Wq"].rearrange("(k p) n -> p k n", p=P)).then_inc(d_l1, 16)
            sp.dma_start(wo[:], inp["L1_xattn_Wo"].rearrange("(k p) n -> p k n", p=P)).then_inc(d_l1, 16)
            sp.dma_start(bit_raw[:, 0, :].rearrange("p (a i) -> p a i", a=IK),
                         inp["L1_ffn_w_gate"].rearrange("(a p) i -> p a i", p=P)).then_inc(d_bit, 16)
            sp.dma_start(bit_raw[:, 1, :].rearrange("p (a i) -> p a i", a=IK),
                         inp["L1_ffn_w_up"].rearrange("(a p) i -> p a i", p=P)).then_inc(d_bit, 16)
            sp.dma_start(bit_raw[:, 2, :].rearrange("p (a i) -> p a i", a=DK),
                         inp["L1_ffn_w_down"].rearrange("(a p) i -> p a i", p=P)).then_inc(d_bit, 16)
            sp.wait_ge(v_zero, 2)
            sp.dma_start(slots_y[NT * P:SLOT_TILES * P, :].rearrange("(t p) d -> p t d", p=P),
                         zeros.unsqueeze(1).to_broadcast([P, SLOT_TILES - NT, D])).then_inc(d_zero, 16)

            def expert_first(e, s):
                sp.dma_start(ew1[:, s, :, :], inp["L0_ffn_w1"][bass.ds(e, 1)].rearrange(
                    "o (k p) f -> p (o k) f", p=P)).then_inc(m_w1[s], 16)

            def expert_second(e, s):
                sp.dma_start(ew2[:, s, :, :], inp["L0_ffn_w2"][bass.ds(e, 1)].rearrange(
                    "o (k p) d -> p (o k) d", p=P)).then_inc(m_w2[s], 16)

            def store_rows(b):
                sp.wait_ge(ln["rt"]["xn"], b + 1)
                sp.dma_start(token_rows[bass.ds(b * N, N), :].rearrange("(i p) d -> p i d", p=P),
                             xn2).then_inc(d_rows, 16)

            with sp.Fori(0, B - 1) as b:
                store_rows(b)
            sp.wait_ge(a_bit, 6)
            expert_first(0, 0)
            expert_second(0, 0)
            store_rows(B - 1)
            expert_first(1, 1)
            sp.wait_ge(r_l, B)
            sp.wait_ge(d_rows, 16 * B)
            expert_second(1, 1)
            sp.wait_ge(r_exps, 2)
            with sp.Fori(1, E // 2) as j:
                for s in range(2):
                    e = 2 * j + s
                    end = sp.value_load(end_of[0:1, bass.ds(e - 2, 1)], min_val=1, max_val=SLOT_TILES - 1)
                    sp.wait_ge(m_up, 2 * end)
                    expert_first(e, s)
                    sp.wait_ge(m_dn, end)
                    expert_second(e, s)

            with sp.Fori(0, B - 1) as b:
                sp.wait_ge(f["p_y"], TB * b + TB)
                sp.dma_start(out[bass.ds(b, 1)].rearrange("o (j p) d -> p (o j) d", p=P),
                             batch_of(x_res, b)).then_inc(d_out, 16)
            last_rows = out[B - 1].rearrange("(j p) d -> p j d", p=P)
            for lo, hi in ((0, TB - 1), (TB - 1, TB)):
                sp.wait_ge(f["p_y"], NT - TB + hi)
                sp.dma_start(last_rows[:, lo:hi, :], x_res[:, NT - TB + lo:NT - TB + hi, :]).then_inc(d_out, 16)
            sp.wait_ge(d_out, 16 * (B + 1))

        def layer_norm_rstd(pool, s, n, tiles=slice(0, TB)):
            pool.wait_ge(s["aggr"], n)
            nc.gpsimd.tensor_tensor(var_eps[:, tiles], mv[:, tiles, 1], eps[:, tiles], ALU.add).then_inc(s["eps"], 1)
            pool.wait_ge(s["eps"], n)
            nc.gpsimd.tensor_tensor(rstd[:, tiles], var_eps[:, tiles], minus_half[:, tiles],
                                    ALU.pow).then_inc(s["rstd"], 1)

        @block.gpsimd
        def _(pool):
            nc.gpsimd.memset(ident[:], 0.0).then_inc(p_const, 1)
            nc.gpsimd.memset(ident_b[:], 0.0).then_inc(p_const, 1)
            nc.gpsimd.memset(ones[:], 1.0).then_inc(p_const, 1)
            nc.gpsimd.memset(before[:], 1.0).then_inc(p_const, 1)
            nc.gpsimd.memset(head_mask[:], 1.0).then_inc(p_const, 1)
            nc.gpsimd.memset(minus_half[:], -0.5).then_inc(p_const, 1)
            nc.gpsimd.memset(carried[:, 2:3], 0.0).then_inc(p_const, 1)
            nc.gpsimd.memset(eps[:], EPS).then_inc(p_const, 1)
            nc.gpsimd.iota(expert_no[:], [[1, E]], base=0, channel_multiplier=0,
                           allow_small_or_imprecise_dtypes=True).then_inc(p_const, 1)
            nc.gpsimd.iota(expert_no8[:], [[1, E]], base=E, channel_multiplier=0,
                           allow_small_or_imprecise_dtypes=True).then_inc(p_const, 1)
            nc.gpsimd.iota(tile_edge[:], [[P, NT]], base=0, channel_multiplier=0,
                           allow_small_or_imprecise_dtypes=True).then_inc(p_const, 1)
            nc.gpsimd.iota(slot_tile_no[:], [[1, SLOT_TILES]], base=0, channel_multiplier=0,
                           allow_small_or_imprecise_dtypes=True).then_inc(p_const, 1)
            nc.gpsimd.iota(slot_edge[:], [[P, READ_TILES + 1]], base=0, channel_multiplier=0,
                           allow_small_or_imprecise_dtypes=True).then_inc(p_const, 1)
            nc.gpsimd.iota(slot_no[:], [[1, P]], base=-P, channel_multiplier=0,
                           allow_small_or_imprecise_dtypes=True).then_inc(p_const, 1)
            nc.gpsimd.iota(row_no[:], [[1, 1]], base=0, channel_multiplier=1,
                           allow_small_or_imprecise_dtypes=True).then_inc(p_const, 1)
            pool.wait_ge(p_const, 15)
            nc.gpsimd.affine_select(out=ident[:], in_=ident[:], compare_op=ALU.not_equal, fill=1.0, base=0,
                                    pattern=[[-1, P]], channel_multiplier=1).then_inc(p_const, 1)
            nc.gpsimd.affine_select(out=ident_b[:], in_=ident_b[:], compare_op=ALU.not_equal, fill=1.0, base=0,
                                    pattern=[[-1, P]], channel_multiplier=1).then_inc(p_const, 1)
            nc.gpsimd.affine_select(out=before[:], in_=before[:], compare_op=ALU.is_gt, fill=0.0, base=0,
                                    pattern=[[1, P]], channel_multiplier=-1).then_inc(p_const, 1)
            nc.gpsimd.affine_select(out=head_mask[:], in_=head_mask[:], compare_op=ALU.is_ge, fill=0.0, base=0,
                                    pattern=[[-HD, HC]], channel_multiplier=1).then_inc(p_const, 1)
            pool.wait_ge(p_const, 19)
            nc.gpsimd.affine_select(out=head_mask[:], in_=head_mask[:], compare_op=ALU.is_ge, fill=0.0, base=HD - 1,
                                    pattern=[[HD, HC]], channel_multiplier=-1).then_inc(p_const, 1)
            pool.wait_ge(p_const, 20)
            layer_norm_rstd(pool, ln["l0"], 1)
            def spread_keys(l):
                pool.wait_ge(a_k, DK * l + DK)
                for b in range(B):
                    for m in range(DK):
                        nc.gpsimd.tensor_tensor(
                            k_bd[:, m, b, :].rearrange("p (h s) -> p h s", h=HC),
                            k_t[:, m, b * M:b * M + M].unsqueeze(1).to_broadcast([P, HC, M]),
                            head_mask[:].unsqueeze(2).to_broadcast([P, HC, M]), ALU.mult).then_inc(p_kbd, 1)

            spread_keys(0)
            pool.wait_ge(d_mlp, 32)
            nc.gpsimd.tensor_copy(w1_hi[:], w1[:]).then_inc(p_wlo, 1)
            nc.gpsimd.tensor_copy(w2_hi[:], w2[:]).then_inc(p_wlo, 1)
            def bias_rows(l, b):
                pool.wait_ge(ln["l0" if l == 0 else "l1"]["xn"], b + 1)
                nc.gpsimd.tensor_tensor(batch_of(x_res, b), batch_of(x_res, b),
                                        bo[l][:].unsqueeze(1).to_broadcast([P, TB, D]),
                                        ALU.add).then_inc(att[l]["p_xb"], 1)

            def carry_wait(use):
                nc.gpsimd.tensor_tensor(carried[:, 3 + use:4 + use], carried[:, 2:3], carried[:, 2:3], ALU.add)

            def ternary(w):
                pool.wait_ge(v_tern, 3 * w + 3)
                nc.gpsimd.tensor_scalar(bit_q[:, w, :], bit_raw[:, w, :], -ROUND, 1.0, ALU.add,
                                        ALU.mult).then_inc(p_terq, 1)

            def ff_rows(b):
                pool.wait_ge(f["inv"], b + 1)
                carry_wait(0)
                for i in range(TB):
                    nc.gpsimd.tensor_scalar(xn2[:, i, :], xn2[:, i, :], x_scale[:, i:i + 1], ROUND, ALU.mult,
                                            ALU.add).then_inc(f["rnd"], 1)
                pool.wait_ge(f["rnd"], TB * b + TB)
                carry_wait(1)
                for i in range(TB):
                    last = nc.gpsimd.tensor_scalar(x_q[:, i, :], xn2[:, i, :], -ROUND, 1.0, ALU.add, ALU.mult)
                last.then_inc(f["xq"], 1)

            def normalise(l, b, i):
                s = att[l]
                pool.wait_ge(s["v_rcp"], TB * b + i + 1)
                p = probs[:, i % 2, :].rearrange("p (h s) -> p h s", h=H)
                nc.gpsimd.tensor_tensor(p, p, p_rcp[:, i, :].unsqueeze(2).to_broadcast([P, H, M]),
                                        ALU.mult).then_inc(s["p_norm"], 1)

            def centre_rows(b):
                pool.wait_ge(att[1]["t_xt"], DK * b)
                nc.gpsimd.tensor_tensor(xn[:], batch_of(x_res, b), mv[:, :, 0:1].to_broadcast([P, TB, D]),
                                        ALU.subtract).then_inc(p_xm, 1)

            def scale_rows(b):
                pool.wait_ge(ln["l1"]["rstd"], b + 1)
                pool.wait_ge(p_xm, b - 1)
                nc.gpsimd.tensor_tensor(xn[:], xn[:], rstd[:].unsqueeze(2).to_broadcast([P, TB, D]),
                                        ALU.mult).then_inc(ln["l1"]["xn"], 1)

            def batch(l, b, first, last):
                if last:
                    bias_rows(l, b)
                normalise(l, b, 2)
                if l == 1 and not last:
                    bias_rows(l, b)
                normalise(l, b, 3)
                if not last:
                    layer_norm_rstd(pool, ln["l0" if l == 0 else "l1"], b + 3)
                if l == 1 and not first:
                    ff_rows(b - 1)
                if l == 0 and not last:
                    bias_rows(l, b)
                if not last:
                    normalise(l, b + 1, 0)
                    if l == 1:
                        centre_rows(b + 2)
                    normalise(l, b + 1, 1)
                    if l == 1:
                        scale_rows(b + 2)
                    if l == 0:
                        ternary(b)
                layer_norm_rstd(pool, ln["rt" if l == 0 else "ff"], b + 1)

            normalise(0, 0, 0)
            normalise(0, 0, 1)
            layer_norm_rstd(pool, ln["l0"], 2)
            pool.wait_ge(p_wlo, 2)
            nc.gpsimd.tensor_tensor(w1_lo[:], w1[:], w1_hi[:].bitcast(F32), ALU.subtract).then_inc(p_wlo, 1)
            nc.gpsimd.tensor_tensor(w2_lo[:], w2[:], w2_hi[:].bitcast(F32), ALU.subtract).then_inc(p_wlo, 1)
            pool.wait_ge(v_bo, 2)
            for b in range(B):
                batch(0, b, b == 0, b == B - 1)

            def gather_rows(tokens, par):
                nc.gpsimd.indirect_dma_start(
                    out=xs[:, par, :], out_offset=None, in_=token_rows[:, :],
                    in_offset=bass.IndirectOffsetOnAxis(ap=tokens, axis=0)).then_inc(m_x[par], 16)

            def slot_rows(t, par):
                pool.wait_ge(m_t, t - 1)
                nc.gpsimd.tensor_tensor(token_now[:, par:par + 1], token_of[:, bass.ds(t, 1)],
                                        carried[:, 2:3].bitcast(U32),
                                        ALU.add).then_inc(p_tok, 1)
                pool.wait_ge(p_tok, t)
                carry_wait(par)
                gather_rows(token_now[:, par:par + 1], par)

            pool.wait_ge(r_v, 25)
            nc.gpsimd.tensor_tensor(ids[:, :, 1, :], in_tile, row_no[:].unsqueeze(2).to_broadcast([P, NT, READ_TILES]),
                                    ALU.mult).then_inc(p_tok, 1)

            pool.wait_ge(d_rows, 16 * B)
            pool.wait_ge(r_tok, 1)
            for t in range(2):
                gather_rows(token_of[:, t:t + 1], t)
            pool.wait_ge(att[0]["t_s"], NT)
            spread_keys(1)
            slot_rows(2, 0)
            pairs = slot_pairs(pool)
            with pool.Fori(1, SLOT_PAIRS) as i:
                with pool.If(i < pairs):
                    for par in (1, 0):
                        t = 2 * i + 2 - par
                        slot_rows(t, par)

            pool.wait_ge(r_pos, 1)
            for par in range(2):
                pool.wait_ge(m_st[par], 16 * pairs)
                carry_wait(5 + par)
            for g, tiles in enumerate(GATHERS):
                for t in tiles:
                    nc.gpsimd.indirect_dma_start(
                        out=xn_all[:, t, :], out_offset=None, in_=slots_y[:, :],
                        in_offset=bass.IndirectOffsetOnAxis(ap=pos[:, t:t + 1], axis=0)).then_inc(g_y[g], 16)
                if g >= 2:
                    layer_norm_rstd(pool, ln["l1"], g - 1)

            normalise(1, 0, 0)
            normalise(1, 0, 1)
            batch(1, 0, True, False)
            with pool.Fori(1, B - 1) as b:
                batch(1, b, False, False)
            batch(1, B - 1, False, True)

            def ff_hidden(t, par, first):
                pool.wait_ge(f["hinv"], t + 1)
                carry_wait(3)
                nc.gpsimd.tensor_scalar(h_f[:, par, :], h_f[:, par, :], h_scale[:, par:par + 1], ROUND, ALU.mult,
                                        ALU.add).then_inc(f["hrnd"], 1)
                if not first:
                    pool.wait_ge(f["t_h"], t - 1)
                pool.wait_ge(f["hrnd"], t + 1)
                carry_wait(4)
                nc.gpsimd.tensor_scalar(h_q[:, par, :], h_f[:, par, :], -ROUND, 1.0, ALU.add,
                                        ALU.mult).then_inc(f["hq"], 1)

            def ff_out(t, par):
                pool.wait_ge(f["a_y"], t + 1)
                row = x_res[:, bass.ds(t, 1), :].rearrange("p o d -> p (o d)")
                nc.gpsimd.tensor_tensor(row, row, y_f[:, par, :], ALU.add).then_inc(f["p_y"], 1)

            def ff_batch(b, first):
                for i in range(TB):
                    t = TB * b + i
                    ff_hidden(t, i % 2, first and i < 2)
                    if first and i == 0:
                        ff_rows(B - 1)
                    if not (first and i < 3):
                        ff_out(t - 3, (i + 1) % 2)

            ff_batch(0, True)
            with pool.Fori(1, B) as b:
                ff_batch(b, False)
            for t in range(NT - 3, NT):
                ff_out(t, t % 2)

        @block.tensor
        def _(pe):
            pe.wait_ge(p_const, 20)
            pe.wait_ge(d_vec, 16 * 5)
            nc.tensor.transpose(t_bank[0][:, 0:12], vec_rows[:], ident[0:12, 0:12]).then_inc(t_ctx, 1)
            pe.wait_ge(d_ctx, 16)
            for t in range(2):
                nc.tensor.transpose(x_bank[0][:, P * t:P * t + P], ctx_rows[:, t, 0:P], ident[:])
            for t in range(2):
                last = nc.tensor.transpose(x_bank[1][0:C - P, P * t:P * t + P], ctx_rows[:, t, P:C], ident[:])
            last.then_inc(t_ctx, 1)
            pe.wait_ge(v_ctx, 5)

            def keys(l, kb):
                for m in range(DK):
                    nc.tensor.matmul(kb[m][:, 0:B * M], wka[l][:, m * P:m * P + P], ctx_ta[:, :, 0, :],
                                     start=True, stop=False)
                    nc.tensor.matmul(kb[m][:, 0:B * M], wkb[l][:, m * P:m * P + P], ctx_tb[:, :, 0, :],
                                     start=False, stop=True).then_inc(t_k, 1)

            def values_of(l, b, vb):
                o = vb[:, (b % 2) * D:(b % 2) * D + D]
                nc.tensor.matmul(o, flat(ctx_ta[:, b, :, :]), wva[l][:], start=True, stop=False)
                last = nc.tensor.matmul(o, flat(ctx_tb[:, b, :, :]), wvb[l][:], start=False, stop=True)
                if b % 2:
                    last.then_inc(t_v, 1)

            pe.wait_ge(d_kv0, 16 * 4)
            keys(0, x_bank)
            pe.wait_ge(v_ctx, 1)
            pe.wait_ge(a_k, DK)

            def turn_rows(l, n):
                pe.wait_ge(ln["l0" if l == 0 else "l1"]["xn"], n + 1)
                for k in range(DK):
                    for i in range(TB):
                        last = nc.tensor.transpose(t_bank[k][:, P * i:P * i + P], xn[:, i, k * P:k * P + P], ident[:])
                    last.then_inc(att[l]["t_xt"], 1)

            def queries(l, n, first, start):
                s = att[l]
                pe.wait_ge(s["a_xt"], DK * n + DK)
                for m in range(DK):
                    if l == 0 and m == 1 and not start:
                        pe.wait_ge(v_wm, n)
                        if not first:
                            pe.wait_ge(r_lg, n - 1)
                    if not start:
                        left = v_olo if l == 0 else s["a_o"]
                        pe.wait_ge(left, 2 * DK * n - 2 * DK + m + 1)
                    for k in range(DK):
                        last = nc.tensor.matmul(x_bank[m][:], wq[l][:, k, m * P:m * P + P], xn_t[:, k, :],
                                                start=(k == 0), stop=(k == DK - 1))
                    last.then_inc(s["t_q"], 1)

            def scores(l, n, i, chunks=range(DK)):
                s = att[l]
                if i == 0:
                    pe.wait_ge(s["a_q"], DK * n + DK)
                if i >= 2 and 0 in chunks:
                    pe.wait_ge(s["v_sub"], TB * n + i - 1)
                for m in chunks:
                    last = nc.tensor.matmul(s_bank[i % 2][m][:], q_t[:, m, P * i:P * i + P],
                                            flat(k_bd[:, m, bass.ds(n, 1), :]), start=True, stop=True)
                if DK - 1 in chunks:
                    last.then_inc(s["t_s"], 1)

            def attention(l, b, first_batch, last_batch):
                s = att[l]

                def turn(i):
                    pe.wait_ge(s["p_norm"], TB * b + i + 1)
                    if i % 2:
                        pe.wait_ge(s["a_pt"], TB * b + i)
                    for c in range(2):
                        for j in range(4):
                            last = nc.tensor.transpose(t_bank[c][:, P * j:P * j + P],
                                                       probs[:, i % 2, P * (4 * c + j):P * (4 * c + j + 1)], ident[:])
                        last.then_inc(s["t_pt"], 1)

                def values(half):
                    pe.wait_ge(s["a_pt"], TB * b + 2 * half + 2)
                    pe.wait_ge(s["v_bd"], b + 1)
                    if half == 0 and not first_batch:
                        pe.wait_ge(s["v_y"], TB * b)
                    if half and l == 0 and last_batch:
                        pe.wait_ge(v_olo, 2 * DK * b + DK)
                    if half and not last_batch:
                        pe.wait_ge(s["a_q"], DK * b + 2 * DK)
                    for k in range(DK):
                        if half == 0 and k:
                            between()
                        if half and k and l == 1 and not last_batch:
                            scores(l, b + 1, 1, (1,))
                        for j in range(4):
                            last = nc.tensor.matmul(x_bank[k][:, 0:2 * P], v_bd[:, 512 * k + P * j:512 * k + P * j + P],
                                                    probs_t[:, :, 4 * k + j, :], start=(j == 0), stop=(j == 3))
                        last.then_inc(s["t_o"], 1)

                def between():
                    if l == 0 and not first_batch:
                        router_products(b - 1)
                    if l == 0 and not last_batch:
                        weight_sum(b)
                    if not last_batch:
                        turn_rows(l, b + 1)

                turn(0)
                scores(l, b, 2)
                turn(1)
                scores(l, b, 3)
                pe.wait_ge(s["a_pt"], TB * b + 2)
                if l == 0 and not first_batch:
                    router_turn(b - 1)
                values(0)
                if not last_batch:
                    queries(l, b + 1, first_batch, False)
                if l == 0 and last_batch:
                    ternary_chunk(0)
                    ternary_chunk(1)
                turn(2)
                if l == 0 and last_batch:
                    ternary_chunk(2)
                    ternary_chunk(3)
                if not last_batch:
                    scores(l, b + 1, 0)
                turn(3)
                if not last_batch:
                    pe.wait_ge(s["v_sub"], TB * b + TB)
                    scores(l, b + 1, 1, (0,))
                if l == 0 and last_batch:
                    ternary_chunk(4)
                    ternary_chunk(5)
                    pe.wait_ge(r_lg, B - 1)
                values(1)
                if l == 0 and not last_batch:
                    scores(l, b + 1, 1, (1,))
                if l == 1 and not first_batch:
                    ff_turn(b - 1)
                if l == 0:
                    if first_batch:
                        pe.wait_ge(p_wlo, 4)
                    pe.wait_ge(v_olo, 2 * DK * b + 2 * DK)
                    for m in range(FK):
                        for k in range(DK):
                            for n, (w, o) in enumerate(((w1_hi, o_hi), (w1_hi, o_lo), (w1_lo, o_hi))):
                                last = nc.tensor.matmul(out_bank[0][m][:], w[:, k, m * P:m * P + P], o[:, k, :],
                                                        start=(k == 0 and n == 0), stop=(k == DK - 1 and n == 2))
                        last.then_inc(s["t_h"], 1)
                    for i, k in (*((i, 0) for i in range(TB)), *((i, k) for i in range(TB) for k in range(1, FK))):
                        if k == 0:
                            pe.wait_ge(s["a_h"], 2 * FK * b + 2 * i + 1)
                        if i == 0:
                            pe.wait_ge(v_hlo, FK * b + k + 1)
                        for n, (h, w) in enumerate(((h1_hi, w2_hi), (h1_hi, w2_lo), (h1_lo, w2_hi))):
                            last = nc.tensor.matmul(out_bank[0][i][:, 0:D], h[:, k, P * i:P * i + P], w[:, k, :],
                                                    start=(k == 0 and n == 0), stop=(k == FK - 1 and n == 2))
                        if k == FK - 1:
                            last.then_inc(s["t_y"], 1)
                else:
                    pe.wait_ge(s["a_o"], 2 * DK * b + 2 * DK)
                    for i in range(TB):
                        if i == 1 and not first_batch:
                            pe.wait_ge(f["a_x"], b)
                        for k in range(DK):
                            last = nc.tensor.matmul(out_bank[1][i][:, 0:D], o_t[:, k, P * i:P * i + P], wo[:, k, :],
                                                    start=(k == 0), stop=(k == DK - 1))
                        last.then_inc(s["t_y"], 1)
                pe.wait_ge(s["v_y"], TB * b + 2)

            def weight_sum(w):
                pe.wait_ge(a_abs, w + 1)
                nc.tensor.matmul(sum_out, ones[:], w_sum[:, bass.ds(w, 1)], start=True,
                                 stop=True).then_inc(t_abs, 1)

            def ternary_chunk(n):
                w, c = n // 2, n % 2
                if n == 0:
                    pe.wait_ge(p_terq, 3)
                    pe.wait_ge(att[0]["v_sub"], NT - 1)
                if n >= 2:
                    pe.wait_ge(a_bit, n - 1)
                src = bit_q[:, w, :].rearrange("p (a i) -> p a i", a=(IK, IK, DK)[w])
                o = s_bank[0][c][:].bitcast(BF16)
                for j in range(8):
                    q = 8 * c + j
                    a, i = (q % IK, q // IK) if w < 2 else (q % DK, q // DK)
                    last = nc.tensor.transpose(o[:, P * j:P * j + P], src[:, a, i * P:i * P + P], ident_b[:])
                last.then_inc(t_bit, 1)

            def router_turn(b):
                pe.wait_ge(ln["rt"]["xn"], b + 1)
                for k in range(DK):
                    for i in range(TB):
                        last = nc.tensor.transpose(t_bank[k][:, P * i:P * i + P], xn2[:, i, k * P:k * P + P], ident[:])
                    last.then_inc(r_t, 1)

            def router_products(b):
                pe.wait_ge(r_e, DK * b + DK)
                for i in range(TB):
                    for k in range(DK):
                        last = nc.tensor.matmul(logit_out[:, E * i:E * i + E], xn_t[:, k, P * i:P * i + P],
                                                rw[:, k, :], start=(k == 0), stop=(k == DK - 1))
                last.then_inc(r_l, 1)

            def ff_turn(b):
                pe.wait_ge(f["xq"], b + 1)
                o = t_bank[0][:].bitcast(BF16)
                for i in range(TB):
                    for k in range(DK):
                        c = DK * i + k
                        last = nc.tensor.transpose(o[:, P * c:P * c + P], x_q[:, i, k * P:k * P + P], ident_b[:])
                last.then_inc(f["t_x"], 1)

            pe.wait_ge(d_q0, 16)
            values_of(0, 0, s_bank[1][1])
            turn_rows(0, 0)
            values_of(0, 1, s_bank[1][1])
            queries(0, 0, True, True)
            pe.wait_ge(p_kbd, DK)
            scores(0, 0, 0)
            pe.wait_ge(v_vbd, 2)
            scores(0, 0, 1)
            for b in range(2, B):
                values_of(0, b, t_bank[1])
            pe.wait_ge(p_kbd, DK * B)
            pe.wait_ge(v_vbd, 4)
            pe.wait_ge(d_rout, 16 * 7)
            attention(0, 0, True, False)
            with pe.Fori(1, B - 1) as b:
                attention(0, b, False, False)
            attention(0, B - 1, False, True)
            pe.wait_ge(att[0]["v_y"], NT)
            router_turn(B - 1)
            router_products(B - 1)

            pe.wait_ge(a_bit, 6)
            pe.wait_ge(r_hot, 1)
            nc.tensor.matmul(s_bank[1][0][:, 0:NT * E], before[:], flat(onehot[:]), start=True, stop=True)
            nc.tensor.matmul(s_bank[1][1][:, 0:NT * E], ones[:], flat(onehot[:]), start=True,
                             stop=True).then_inc(r_cnt, 1)
            pe.wait_ge(d_l1, 16 * 6)
            keys(1, t_bank)
            for t in range(NT):
                if t % TB == 0:
                    pe.wait_ge(r_slot, t // TB + 1)
                if t == 0:
                    pe.wait_ge(r_id, 1)
                    pe.wait_ge(p_tok, 1)
                last = nc.tensor.matmul(x_bank[0][:, 0:2 * READ_TILES], in_slot[:, t, :],
                                        ids[:, t, :, :].rearrange("p w k -> p (w k)"), start=(t == 0),
                                        stop=(t == NT - 1))
            last.then_inc(r_inv, 1)
            pe.wait_ge(a_k, 2 * DK)

            a_bank, g_bank, y_bank, r_bank = bank[0:2], bank[2:4], bank[4:6], bank[6:8]

            def rows_in(t, par, n):
                pe.wait_ge(m_x[par], 16 * (n + 1))
                for k in range(DK):
                    last = nc.tensor.transpose(r_bank[par][:, P * k:P * k + P], xs[:, par, k * P:k * P + P], ident[:])
                last.then_inc(m_t, 1)

            def expand(t, par, s, loads, q, first_tile):
                if q == 0:
                    pe.wait_ge(m_xt, t + 1)
                    pe.wait_ge(m_w1[s], loads)
                if not first_tile:
                    pe.wait_ge(m_act, 2 * t - 1 + q)
                for o, base in ((a_bank[q], 0), (g_bank[q], FE)):
                    for j in range(4):
                        c0 = base + (4 * q + j) * P
                        for k in range(DK):
                            last = nc.tensor.matmul(o[:, P * j:P * j + P], ew1[:, s, k, c0:c0 + P],
                                                    xs_t[:, par, k, :], start=(k == 0), stop=(k == DK - 1))
                last.then_inc(m_up, 1)

            def contract(t, par, s, q):
                pe.wait_ge(m_lo, 2 * t + q + 1)
                for j in range(4):
                    c = 4 * q + j
                    w_hi, w_lo = (w[:, bass.ds(s, 1), c, :].rearrange("p o d -> p (o d)") for w in (ew2_hi, ew2_lo))
                    u_hi, u_lo = act_hi[:, par, c, :], act_lo[:, par, c, :]
                    for n, (u, w) in enumerate(((u_hi, w_hi), (u_hi, w_lo), (u_lo, w_hi))):
                        last = nc.tensor.matmul(y_bank[par][:, 0:D], u, w, start=(c == 0 and n == 0),
                                                stop=(c == EK - 1 and n == 2))
                if q == 1:
                    last.then_inc(m_dn, 1)

            def expert(t):
                return pe.value_load(expert_of[0:1, bass.ds(t, 1)], min_val=0, max_val=E - 1)

            def expert_tile(t, par, n, e, s, first_tile, first_pair):
                loads = 8 * e + 16 - 8 * s
                expand(t, par, s, loads, 0, first_tile)
                if not first_tile:
                    contract(t - 1, 1 - par, expert(t - 1) % 2, 1)
                rows_in(t + 1, 1 - par, n + 1 if par else n)
                expand(t, par, s, loads, 1, first_tile)
                pe.wait_ge(v_w2, e + 1)
                if not first_pair:
                    pe.wait_ge(m_y, t - 1)
                contract(t, par, s, 0)

            def expert_pair(i, first_pair):
                for par in range(2):
                    t = 2 * i + par
                    if first_pair and par == 0:
                        expert_tile(0, 0, 0, 0, 0, True, True)
                        continue
                    e = expert(t)
                    with pe.If(e % 2 == 0):
                        expert_tile(t, par, i, e, 0, False, first_pair)
                    with pe.Else():
                        expert_tile(t, par, i, e, 1, False, first_pair)

            pairs = slot_pairs(pe)
            rows_in(0, 0, 0)
            expert_pair(0, True)
            with pe.Fori(1, SLOT_PAIRS) as i:
                with pe.If(i < pairs):
                    expert_pair(i, False)
            contract(2 * pairs - 1, 1, expert(2 * pairs - 1) % 2, 1)

            pe.wait_ge(m_y, 2 * pairs)
            pe.wait_ge(g_x, TB // 2)
            for b in range(B):
                values_of(1, b, s_bank[0][b // 2])
            turn_rows(1, 0)
            queries(1, 0, True, True)
            pe.wait_ge(p_kbd, 2 * DK * B)
            pe.wait_ge(v_vbd, 8)
            scores(1, 0, 0)
            scores(1, 0, 1)
            attention(1, 0, True, False)
            with pe.Fori(1, B - 1) as b:
                attention(1, b, False, False)
            attention(1, B - 1, False, True)
            pe.wait_ge(att[1]["v_y"], NT)

            def ff_up(t, par, first):
                for c in range(2):
                    if not first:
                        pe.wait_ge(f["v_h"], 2 * t - 1 + c)
                    for o, w in ((bank[c], gate_t), (bank[2 + c], up_t)):
                        for k in range(DK):
                            last = nc.tensor.matmul(o[:], x_qt[:, bass.ds(t, 1), k, :].rearrange("p o i -> p (o i)"),
                                                    w[:, k, 512 * c:512 * c + 512], start=(k == 0), stop=(k == DK - 1))
                    last.then_inc(f["t_gu"], 1)

            def ff_hidden(t, par, first):
                pe.wait_ge(f["hq"], t + 1)
                if not first:
                    pe.wait_ge(f["a_h"], t)
                o = t_bank[1][:].bitcast(BF16)
                for k in range(IK):
                    last = nc.tensor.transpose(o[:, P * k:P * k + P], h_q[:, par, k * P:k * P + P], ident_b[:])
                last.then_inc(f["t_h"], 1)

            def ff_down(t, par, first):
                pe.wait_ge(f["a_h"], t + 1)
                if not first:
                    pe.wait_ge(f["a_y"], t - 1)
                for k in range(IK):
                    last = nc.tensor.matmul(x_bank[par][:, 0:D], h_qt[:, par, k, :], down_t[:, k, :],
                                            start=(k == 0), stop=(k == IK - 1))
                last.then_inc(f["t_y"], 1)

            def ff_batch(b, first):
                pe.wait_ge(f["a_x"], b + 1)
                for i in range(TB):
                    t = TB * b + i
                    ff_up(t, i % 2, first and i == 0)
                    if first and i == 2:
                        ff_turn(B - 1)
                    if not (first and i < 2):
                        ff_hidden(t - 2, i % 2, first and i == 2)
                    if not (first and i < 3):
                        ff_down(t - 3, (i + 1) % 2, first)

            ff_batch(0, True)
            with pe.Fori(1, B) as b:
                ff_batch(b, False)
            for t in range(NT, NT + 3):
                if t < NT + 2:
                    ff_hidden(t - 2, t % 2, False)
                ff_down(t - 3, (t + 1) % 2, False)

        @block.scalar
        def _(act):
            def keys(l, kb):
                for m in range(DK):
                    act.wait_ge(t_k, DK * l + m + 1)
                    nc.scalar.activation(k_t[:, m, :], kb[m][:, 0:B * M], ACT.Identity,
                                         bias=vecs[:, (2, 10)[l] + m:(2, 10)[l] + m + 1]).then_inc(a_k, 1)

            act.wait_ge(v_ctx, 1)
            keys(0, x_bank)

            def turned_rows(l, n):
                for k in range(DK):
                    act.wait_ge(att[l]["t_xt"], DK * n + k + 1)
                    nc.scalar.copy(xn_t[:, k, :], t_bank[k][:]).then_inc(att[l]["a_xt"], 1)

            def queries(l, n):
                for m in range(DK):
                    act.wait_ge(att[l]["t_q"], DK * n + m + 1)
                    nc.scalar.activation(q_t[:, m, :], x_bank[m][:], ACT.Identity, bias=bq_s[:, l, m:m + 1],
                                         scale=QSCALE).then_inc(att[l]["a_q"], 1)

            def exps(l, n, i):
                act.wait_ge(att[l]["v_sub"], TB * n + i + 1)
                nc.scalar.activation(probs[:, i % 2, :], probs[:, i % 2, :], ACT.Exp).then_inc(att[l]["a_exp"], 1)

            def router_rows(b):
                for k in range(DK):
                    act.wait_ge(r_t, DK * b + k + 1)
                    nc.scalar.copy(xn_t[:, k, :], t_bank[k][:]).then_inc(r_e, 1)

            def ternary_chunk(n):
                act.wait_ge(t_bit, n + 1)
                half = flat((gate_t, up_t, down_t)[n // 2][:])[:, 1024 * (n % 2):1024 * (n % 2) + 1024]
                nc.scalar.copy(half, s_bank[0][n % 2][:].bitcast(BF16)).then_inc(a_bit, 1)

            def weight_abs(w):
                nc.scalar.activation(bit_q[:, w, :], bit_raw[:, w, :], ACT.Abs,
                                     accum_out=w_sum[:, w:w + 1]).then_inc(a_abs, 1)

            def ff_rows(b):
                act.wait_ge(f["t_x"], b + 1)
                nc.scalar.copy(x_qt[:, bass.ds(b * TB, TB), :, :].rearrange("p t k i -> p (t k i)"),
                               t_bank[0][:].bitcast(BF16)).then_inc(f["a_x"], 1)

            def attention(l, b, first_batch, last_batch):
                s = att[l]

                def turned(i):
                    if i >= 2:
                        act.wait_ge(s["t_o"], 2 * DK * b + DK)
                    for c in range(2):
                        act.wait_ge(s["t_pt"], 2 * (TB * b + i) + c + 1)
                        last = nc.scalar.copy(flat(probs_t[:, i % 2, 4 * c:4 * c + 4, :]), t_bank[c][:])
                    last.then_inc(s["a_pt"], 1)

                def output(half, k):
                    act.wait_ge(s["t_o"], 2 * DK * b + DK * half + k + 1)
                    nc.scalar.copy((o_hi if l == 0 else o_t)[:, k, 2 * P * half:2 * P * half + 2 * P],
                                   x_bank[k][:, 0:2 * P]).then_inc(s["a_o"], 1)

                def hidden(m):
                    act.wait_ge(s["t_h"], FK * b + m + 1)
                    nc.scalar.activation(h1_t[:, m, :], out_bank[0][m][:], ACT.Relu,
                                         bias=vecs[:, 4 + m:5 + m]).then_inc(s["a_h"], 1)
                    act.wait_ge(s["a_h"], 2 * FK * b + 2 * m + 1)
                    nc.scalar.copy(h1_hi[:, m, :], h1_t[:, m, :]).then_inc(s["a_h"], 1)

                turned(0)
                turned(1)
                if l == 0 and not first_batch:
                    router_rows(b - 1)
                exps(l, b, 2)
                output(0, 0)
                if not last_batch:
                    if l == 0 and not first_batch:
                        act.wait_ge(r_l, b)
                    turned_rows(l, b + 1)
                output(0, 1)
                exps(l, b, 3)
                if not last_batch:
                    queries(l, b + 1)
                elif l == 0:
                    ternary_chunk(0)
                    ternary_chunk(1)
                else:
                    nc.scalar.activation(carried[:, 10 + 2 * TB:11 + 2 * TB], carried[:, 2:3], ACT.Silu)
                turned(2)
                if l == 0 and last_batch:
                    ternary_chunk(2)
                    ternary_chunk(3)
                turned(3)
                if not last_batch:
                    exps(l, b + 1, 0)
                output(1, 0)
                output(1, 1)
                if l == 0 and last_batch:
                    ternary_chunk(4)
                    ternary_chunk(5)
                if l == 1 and not first_batch:
                    ff_rows(b - 1)
                if l == 0:
                    hidden(0)
                    hidden(1)
                if not last_batch:
                    exps(l, b + 1, 1)
                if l == 0:
                    hidden(2)
                    hidden(3)
                    if first_batch:
                        weight_abs(1)
                        weight_abs(2)

            turned_rows(0, 0)
            act.wait_ge(v_bq, 2)
            queries(0, 0)
            act.wait_ge(d_rout, 16 * 7)
            nc.scalar.activation(tg[:], gates[:], ACT.Tanh).then_inc(a_tanh, 1)
            exps(0, 0, 0)
            exps(0, 0, 1)
            act.wait_ge(d_bit, 48)
            weight_abs(0)
            attention(0, 0, True, False)
            with act.Fori(1, B - 1) as b:
                attention(0, b, False, False)
            attention(0, B - 1, False, True)
            router_rows(B - 1)

            act.wait_ge(r_v, 2)
            nc.scalar.activation(l_exp[:], r_tmp[:], ACT.Exp).then_inc(r_exp, 1)
            act.wait_ge(p_kbd, DK * B)
            keys(1, t_bank)

            def expert_rows(t, par):
                act.wait_ge(m_t, t + 1)
                nc.scalar.copy(flat(xs_t[:, par, :, :]), bank[6 + par][:, 0:D]).then_inc(m_xt, 1)

            def expert_gate(t, q, first_tile):
                act.wait_ge(m_up, 2 * t + q + 1)
                if not first_tile:
                    act.wait_ge(m_act, 2 * t + q - 1)
                nc.scalar.activation(sil[:, q, :], bank[q][:], ACT.Silu).then_inc(m_sil, 1)

            def expert_out(t, par):
                act.wait_ge(m_dn, t + 1)
                nc.scalar.copy(ys[:, par, :], bank[4 + par][:, 0:D]).then_inc(m_y, 1)
                act.wait_ge(m_y, t + 1)
                act.dma_start(slots_y[bass.ds(t * P, P), :], ys[:, par, :]).then_inc(m_st[par], 16)

            def upper_units(t, par, q):
                act.wait_ge(m_act, 2 * t + q + 1)
                nc.scalar.copy(act_hi[:, par, 4 * q:4 * q + 4, :],
                               act_t[:, par, 4 * q:4 * q + 4, :]).then_inc(m_hi, 1)

            def upper_weights(e, s):
                act.wait_ge(m_w2[s], 16 * (e // 2 + 1))
                nc.scalar.copy(ew2_hi[:, s, :, :], ew2[:, s, :, :]).then_inc(a_w2, 1)

            def expert_pair(i, first_pair):
                for par in range(2):
                    t = 2 * i + par
                    first_tile = first_pair and par == 0
                    expert_gate(t, 0, first_tile)
                    upper_units(t, par, 0)
                    if par and not first_pair:
                        act.wait_ge(m_st[0], 16 * i)
                        act.wait_ge(m_st[1], 16 * i)
                    if not first_tile:
                        expert_out(t - 1, 1 - par)
                    expert_rows(t + 1, 1 - par)
                    expert_gate(t, 1, first_tile)
                    upper_units(t, par, 1)
                    if first_tile:
                        upper_weights(1, 1)
                    else:
                        next_expert(act, t, upper_weights)

            pairs = slot_pairs(act)
            expert_rows(0, 0)
            upper_weights(0, 0)
            expert_pair(0, True)
            with act.Fori(1, SLOT_PAIRS) as i:
                with act.If(i < pairs):
                    expert_pair(i, False)
            expert_out(2 * pairs - 1, 1)

            turned_rows(1, 0)
            queries(1, 0)
            exps(1, 0, 0)
            exps(1, 0, 1)
            attention(1, 0, True, False)
            with act.Fori(1, B - 1) as b:
                attention(1, b, False, False)
            attention(1, B - 1, False, True)

            def ff_batch(b, first):
                act.wait_ge(f["unit"], 2 * b + 2)
                for i in range(TB):
                    t = TB * b + i
                    for c in range(2):
                        act.wait_ge(f["t_gu"], 2 * t + c + 1)
                        nc.scalar.copy(carried[:, 10 + 2 * i + c:11 + 2 * i + c], carried[:, 2:3])
                        nc.scalar.activation(sil_g[:, i % 2, 512 * c:512 * c + 512], bank[c][:], ACT.Silu,
                                             scale=x_unit[:, 0, bass.ds(t, 1)]).then_inc(f["a_sil"], 1)
                    if first and i == 2:
                        ff_rows(B - 1)
                    if not (first and i < 2):
                        ff_hidden(t - 2, i % 2, first)
                    if not (first and i < 3):
                        ff_out(t - 3, (i + 1) % TB, first)

            def ff_out(t, i, first):
                act.wait_ge(f["t_y"], t + 1)
                act.wait_ge(f["hunit"], t + 1)
                if not first:
                    act.wait_ge(f["p_y"], t - 1)
                nc.scalar.activation(y_f[:, i % 2, :], x_bank[i % 2][:, 0:D], ACT.Copy,
                                     scale=h_unit[:, i:i + 1]).then_inc(f["a_y"], 1)

            def ff_hidden(t, par, first):
                act.wait_ge(f["t_h"], t + 1)
                if not first:
                    act.wait_ge(f["t_y"], t - 1)
                nc.scalar.copy(flat(h_qt[:, par, :, :]), t_bank[1][:].bitcast(BF16)).then_inc(f["a_h"], 1)

            ff_batch(0, True)
            with act.Fori(1, B) as b:
                ff_batch(b, False)
            for t in range(NT, NT + 3):
                if t < NT + 2:
                    ff_hidden(t - 2, t % 2, False)
                ff_out(t - 3, (t + 1) % TB, False)

        @block.vector
        def _(dve):
            nc.vector.memset(carried[:, 0:1], 0.0).then_inc(v_zero, 1)
            nc.vector.memset(x_res[:, NT:NT + TB, :], 0.0).then_inc(v_zero, 1)
            nc.vector.memset(v_bd[:], 0.0).then_inc(v_zero, 1)

            def carry_wait():
                nc.vector.tensor_copy(carried[:, 1:2], carried[:, 0:1])

            def row(t):
                return x_res[:, bass.ds(t, 1), :].rearrange("p o d -> p (o d)")

            def row_stats(s, t0, tiles=range(TB)):
                for i in tiles:
                    last = nc.vector.bn_stats(stats[:, i, :], row(t0 + i))
                if TB - 1 in tiles:
                    last.then_inc(s["stats"], 1)

            def join_stats(s, n):
                dve.wait_ge(s["stats"], n)
                carry_wait()
                for i in range(TB):
                    last = nc.vector.bn_aggr(mv[:, i, :], stats[:, i, :])
                last.then_inc(s["aggr"], 1)

            def norm_stats(s, n, t0):
                carry_wait()
                row_stats(s, t0)
                join_stats(s, n)

            def norm_apply(s, n, t0, out):
                dve.wait_ge(s["aggr"], n)
                dve.wait_ge(s["rstd"], n)
                for i in range(TB):
                    last = nc.vector.tensor_scalar(out[:, i, :], row(t0 + i), mv[:, i, 0:1], rstd[:, i:i + 1],
                                                   ALU.subtract, ALU.mult)
                last.then_inc(s["xn"], 1)

            def layer_norm(s, n, t0, out):
                norm_stats(s, n, t0)
                norm_apply(s, n, t0, out)

            dve.wait_ge(t_ctx, 1)
            nc.vector.tensor_copy(vecs[:], t_bank[0][:, 0:12]).then_inc(v_ctx, 1)
            dve.wait_ge(t_ctx, 2)
            for c, (dst, src) in enumerate(((ctx_ta, x_bank[0]), (ctx_tb, x_bank[1]))):
                rows = (P, C - P)[c]
                for twice in range(2):
                    nc.vector.tensor_copy(dst[:, :, twice, :], src[0:rows, 0:B * M].rearrange(
                        "p (b s) -> p b s", b=B)).then_inc(v_ctx, 1)
            dve.wait_ge(v_ctx, 1)
            for l in range(2):
                nc.vector.tensor_scalar(bq_s[:, l, :], vecs[:, 8 * l:8 * l + 2], QSCALE, None,
                                        ALU.mult).then_inc(v_bq, 1)
            dve.wait_ge(d_x0, 16)
            layer_norm(ln["l0"], 1, 0, xn)

            def spread_values(l, c, values):
                dve.wait_ge(t_v, 2 * l + c + 1)
                for half in range(2):
                    lo = half * M
                    nc.vector.tensor_tensor(
                        v_pair[l][lo:lo + M, 2 * c:2 * c + 2, :, :],
                        values[lo:lo + M, :].rearrange("p (b j a) -> p b j a", b=2, j=PAIRS)[
                            :, :, :, half * HD:half * HD + HD],
                        bv[l][lo:lo + M, :].rearrange("p (j a) -> p j a", j=PAIRS)[
                            :, :, half * HD:half * HD + HD].unsqueeze(1).to_broadcast([M, 2, PAIRS, HD]),
                        ALU.add).then_inc(v_vbd, 1)

            def block_values(l, b):
                for half in range(2):
                    lo = half * M
                    for k in range(DK):
                        blocks = v_bd[lo:lo + M, 512 * k:512 * k + 640].rearrange("p (j a) -> p j a", a=P + 2 * HD)
                        last = nc.vector.tensor_copy(
                            blocks[:, :, half * HD:half * HD + HD],
                            v_pair[l][lo:lo + M, bass.ds(b, 1), 4 * k:4 * k + 4, :].rearrange("p o j a -> p (o j) a"))
                last.then_inc(att[l]["v_bd"], 1)


            def scores(l, n, i):
                s = att[l]
                g = TB * n + i
                dve.wait_ge(s["t_s"], g + 1)
                for m in range(DK):
                    last = nc.vector.tensor_reduce(s_max[:, i, HC * m:HC * m + HC],
                                                   s_bank[i % 2][m][:].rearrange("p (h s) -> p h s", h=HC),
                                                   AX, ALU.max)
                last.then_inc(s["v_max"], 1)
                dve.wait_ge(s["v_max"], g + 1)
                if i >= 2:
                    dve.wait_ge(s["t_pt"], 2 * g - 2)
                for m in range(DK):
                    last = nc.vector.tensor_tensor(
                        probs[:, i % 2, 512 * m:512 * m + 512].rearrange("p (h s) -> p h s", h=HC),
                        s_bank[i % 2][m][:].rearrange("p (h s) -> p h s", h=HC),
                        s_max[:, i, HC * m:HC * m + HC].unsqueeze(2).to_broadcast([P, HC, M]), ALU.subtract)
                last.then_inc(s["v_sub"], 1)

            def sums(l, n, i):
                s = att[l]
                g = TB * n + i
                dve.wait_ge(s["a_exp"], g + 1)
                nc.vector.tensor_reduce(p_sum[:, i, :], probs[:, i % 2, :].rearrange("p (h s) -> p h s", h=H), AX,
                                        ALU.add).then_inc(s["v_sum"], 1)
                dve.wait_ge(s["v_sum"], g + 1)
                nc.vector.reciprocal(p_rcp[:, i, :], p_sum[:, i, :]).then_inc(s["v_rcp"], 1)

            dve.wait_ge(d_bv, 16)
            spread_values(0, 0, s_bank[1][1])
            scores(0, 0, 0)
            dve.wait_ge(v_zero, 3)
            spread_values(0, 1, t_bank[1])
            sums(0, 0, 0)
            scores(0, 0, 1)
            sums(0, 0, 1)
            dve.wait_ge(v_vbd, 4)
            block_values(0, 0)
            dve.wait_ge(d_x, 16 * (B - 1))
            dve.wait_ge(att[0]["t_xt"], DK)
            layer_norm(ln["l0"], 2, TB, xn)
            dve.wait_ge(d_rout, 16 * 7)
            dve.wait_ge(a_tanh, 1)
            for l in range(2):
                nc.vector.tensor_scalar(bo[l][:], bo[l][:], tg[:, l:l + 1], None, ALU.mult).then_inc(v_bo, 1)
            def weight_scale(w):
                dve.wait_ge(t_abs, w + 1)
                nc.vector.tensor_scalar(w_mean[:, bass.ds(w, 1)], sum_out, 1.0 / (INNER * D),
                                        EPS, ALU.mult, ALU.max).then_inc(v_wm, 1)
                dve.wait_ge(v_wm, w + 1)
                nc.vector.reciprocal(w_inv[:, bass.ds(w, 1)], w_mean[:, bass.ds(w, 1)]).then_inc(v_tern, 1)

            def ternary(w):
                raw = bit_raw[:, bass.ds(w, 1), :].rearrange("p o a -> p (o a)")
                dve.wait_ge(v_tern, 3 * w + 1)
                nc.vector.tensor_scalar(raw, raw, w_inv[:, bass.ds(w, 1)], 1.0, ALU.mult, ALU.min).then_inc(v_tern, 1)
                dve.wait_ge(v_tern, 3 * w + 2)
                nc.vector.tensor_scalar(raw, raw, -1.0, ROUND, ALU.max, ALU.add).then_inc(v_tern, 1)

            def router_logits(b):
                dve.wait_ge(r_l, b + 1)
                nc.vector.tensor_tensor(logits[:, bass.ds(b * TB, TB), :],
                                        logit_out.rearrange("p (t e) -> p t e", t=TB),
                                        rb[:].unsqueeze(1).to_broadcast([P, TB, E]), ALU.add).then_inc(r_lg, 1)

            def row_scales(b):
                dve.wait_ge(ln["ff"]["xn"], b + 1)
                nc.vector.tensor_reduce(x_abs[:], xn2, AX, ALU.max, apply_absolute_value=True).then_inc(f["abs"], 1)
                dve.wait_ge(f["abs"], 2 * b + 1)
                nc.vector.tensor_scalar(x_abs[:], x_abs[:], 1.0 / 127.0, EPS / 127.0, ALU.mult,
                                        ALU.max).then_inc(f["abs"], 1)
                dve.wait_ge(f["abs"], 2 * b + 2)
                nc.vector.reciprocal(x_scale[:], x_abs[:]).then_inc(f["inv"], 1)
                for w in range(2):
                    nc.vector.tensor_scalar(x_unit[:, w, bass.ds(b * TB, TB)], x_abs[:], w_mean[:, w:w + 1], None,
                                            ALU.mult).then_inc(f["unit"], 1)

            def attention(l, b, first_batch, last_batch):
                s = att[l]
                second = ln["rt" if l == 0 else "ff"]
                phase = ln["l0" if l == 0 else "l1"]

                def next_values():
                    dve.wait_ge(s["t_o"], 2 * DK * b + 2 * DK)
                    block_values(l, b + 1)

                def lower_outputs(half, k):
                    dve.wait_ge(s["a_o"], 2 * DK * b + DK * half + k + 1)
                    cols = slice(2 * P * half, 2 * P * half + 2 * P)
                    nc.vector.tensor_tensor(o_lo[:, k, cols], x_bank[k][:, 0:2 * P], o_hi[:, k, cols].bitcast(F32),
                                            ALU.subtract).then_inc(v_olo, 1)

                def lower_hidden(m):
                    dve.wait_ge(s["a_h"], 2 * FK * b + 2 * m + 2)
                    nc.vector.tensor_tensor(h1_lo[:, m, :], h1_t[:, m, :], h1_hi[:, m, :].bitcast(F32),
                                            ALU.subtract).then_inc(v_hlo, 1)

                scores(l, b, 2)
                if last_batch:
                    scores(l, b, 3)
                if l == 1 and not (first_batch or last_batch):
                    norm_apply(second, b, TB * b - TB, xn2)
                sums(l, b, 2)
                if l == 0:
                    lower_outputs(0, 0)
                if not last_batch:
                    scores(l, b, 3)
                if l == 0:
                    lower_outputs(0, 1)
                if l == 0 and not last_batch:
                    weight_scale(b)
                if l == 0 and not first_batch:
                    router_logits(b - 1)
                if not last_batch:
                    row_stats(phase, TB * b + 2 * TB)
                sums(l, b, 3)
                if not last_batch:
                    join_stats(phase, b + 3)
                if l == 1 and last_batch:
                    norm_apply(second, b, TB * b - TB, xn2)
                if l == 1 and not first_batch:
                    row_scales(b - 1)
                if not last_batch:
                    scores(l, b + 1, 0)
                    if l == 0:
                        dve.wait_ge(s["t_xt"], DK * b + 2 * DK)
                        norm_apply(phase, b + 3, TB * b + 2 * TB, xn)
                    sums(l, b + 1, 0)
                if l == 0:
                    lower_outputs(1, 0)
                    lower_outputs(1, 1)
                if not last_batch:
                    scores(l, b + 1, 1)
                if l == 0:
                    lower_hidden(0)
                    lower_hidden(1)
                    if not last_batch:
                        sums(l, b + 1, 1)
                    lower_hidden(2)
                    lower_hidden(3)
                    if not last_batch:
                        next_values()
                        ternary(b)
                dve.wait_ge(s["p_xb"], b + 1)
                for i in range(TB):
                    if l == 1 and i == 2 and not last_batch:
                        sums(l, b + 1, 1)
                    g = TB * b + i
                    dve.wait_ge(s["t_y"], g + 1)
                    nc.vector.scalar_tensor_tensor(row(g), out_bank[l][i][:, 0:D], tg[:, l:l + 1], row(g), ALU.mult,
                                                   ALU.add).then_inc(s["v_y"], 1)
                    if last_batch:
                        dve.wait_ge(s["v_y"], g + 1)
                        row_stats(second, TB * b, (i,))
                if l == 1 and not last_batch:
                    next_values()
                if not last_batch:
                    dve.wait_ge(s["v_y"], TB * b + TB)
                if l == 1 and not last_batch:
                    dve.wait_ge(p_xm, b + 1)
                if last_batch:
                    join_stats(second, b + 1)
                else:
                    norm_stats(second, b + 1, TB * b)
                if l == 0:
                    if not first_batch:
                        dve.wait_ge(d_rows, 16 * b)
                    norm_apply(second, b + 1, TB * b, xn2)

            attention(0, 0, True, False)
            with dve.Fori(1, B - 1) as b:
                attention(0, b, False, False)
            attention(0, B - 1, False, True)
            router_logits(B - 1)
            nc.vector.tensor_scalar(wd_g[:], w_mean[:, 2:3], tg[:, 3:4], None, ALU.mult).then_inc(v_wd, 1)

            dve.wait_ge(r_lg, B)
            nc.vector.tensor_reduce(l_max[:], logits[:], AX, ALU.max).then_inc(r_v, 1)
            dve.wait_ge(r_v, 1)
            nc.vector.tensor_tensor(r_tmp[:], logits[:], l_max[:].unsqueeze(2).to_broadcast([P, NT, E]),
                                    ALU.subtract).then_inc(r_v, 1)
            nc.vector.tensor_tensor(onehot[:], logits[:], l_max[:].unsqueeze(2).to_broadcast([P, NT, E]),
                                    ALU.is_equal).then_inc(r_v, 1)
            dve.wait_ge(r_v, 3)
            nc.vector.scalar_tensor_tensor(count[:], onehot[:], -float(E),
                                           expert_no8[:].unsqueeze(1).to_broadcast([P, NT, E]), ALU.mult,
                                           ALU.add).then_inc(r_v, 1)
            dve.wait_ge(r_v, 4)
            nc.vector.tensor_reduce(first[:], count[:], AX, ALU.min).then_inc(r_v, 1)
            dve.wait_ge(r_v, 5)
            nc.vector.tensor_tensor(onehot[:], expert_no[:].unsqueeze(1).to_broadcast([P, NT, E]),
                                    first[:].unsqueeze(2).to_broadcast([P, NT, E]), ALU.is_equal).then_inc(r_hot, 1)
            dve.wait_ge(r_exp, 1)
            nc.vector.tensor_reduce(l_sum[:], l_exp[:], AX, ALU.add).then_inc(r_v, 1)
            dve.wait_ge(r_v, 6)
            nc.vector.reciprocal(l_sum[:], l_sum[:]).then_inc(r_v, 1)
            dve.wait_ge(r_v, 7)
            nc.vector.tensor_scalar(weight[:], l_sum[:], tg[:, 2:3], None, ALU.mult).then_inc(r_v, 1)
            dve.wait_ge(r_cnt, 1)
            nc.vector.tensor_copy(count[:], s_bank[1][1][:, 0:NT * E].rearrange("p (t e) -> p t e",
                                                                                t=NT)).then_inc(r_v, 1)
            dve.wait_ge(r_v, 9)
            for e in range(E):
                last = nc.vector.tensor_tensor_scan(upto[:, e, :], count[:, :, e], zeros[:, 0:NT], 0.0, ALU.add,
                                                     ALU.add)
            last.then_inc(r_v, 1)
            dve.wait_ge(r_v, 10)
            nc.vector.tensor_tensor(more[:], upto[:, :, NT - 1:NT].to_broadcast([P, E, NT]),
                                    tile_edge[:].unsqueeze(1).to_broadcast([P, E, NT]), ALU.is_gt).then_inc(r_v, 1)
            dve.wait_ge(r_v, 11)
            nc.vector.tensor_reduce(tiles_of[:], more[:], AX, ALU.add).then_inc(r_v, 1)
            dve.wait_ge(r_v, 12)
            nc.vector.tensor_scalar(tiles_of[:], tiles_of[:], 1.0, None, ALU.max).then_inc(r_v, 1)
            dve.wait_ge(r_v, 13)
            nc.vector.tensor_tensor_scan(tile_end[:], tiles_of[:], zeros[:, 0:E], 0.0, ALU.add,
                                         ALU.add).then_inc(r_v, 1)
            dve.wait_ge(r_v, 14)
            nc.vector.tensor_tensor(past[:], tile_end[:].unsqueeze(1).to_broadcast([P, SLOT_TILES, E]),
                                    slot_tile_no[:].unsqueeze(2).to_broadcast([P, SLOT_TILES, E]),
                                    ALU.is_le).then_inc(r_v, 1)
            nc.vector.tensor_tensor(slot_base[:], tile_end[:], tiles_of[:], ALU.subtract).then_inc(r_v, 1)
            nc.vector.tensor_copy(end_of[:], tile_end[:]).then_inc(r_exps, 1)
            dve.wait_ge(r_v, 16)
            nc.vector.tensor_reduce(expert_f[:], past[:, :, 0:E - 1], AX, ALU.add).then_inc(r_v, 1)
            dve.wait_ge(r_v, 17)
            nc.vector.tensor_copy(expert_of[:], expert_f[:]).then_inc(r_exps, 1)
            nc.vector.tensor_tensor(r_tmp[:], upto[:].rearrange("p e t -> p t e"), count[:],
                                    ALU.subtract).then_inc(r_v, 1)
            dve.wait_ge(r_v, 18)
            nc.vector.tensor_tensor(r_tmp[:], s_bank[1][0][:, 0:NT * E].rearrange("p (t e) -> p t e", t=NT), r_tmp[:],
                                    ALU.add).then_inc(r_v, 1)
            dve.wait_ge(r_v, 19)
            nc.vector.scalar_tensor_tensor(r_tmp[:], slot_base[:].unsqueeze(1).to_broadcast([P, NT, E]), float(P),
                                           r_tmp[:], ALU.mult, ALU.add).then_inc(r_v, 1)
            dve.wait_ge(r_v, 20)
            nc.vector.tensor_tensor(r_tmp[:], r_tmp[:], onehot[:], ALU.mult).then_inc(r_v, 1)
            dve.wait_ge(r_v, 21)
            nc.vector.tensor_reduce(pos_f[:], r_tmp[:], AX, ALU.add).then_inc(r_v, 1)
            dve.wait_ge(r_v, 22)
            nc.vector.tensor_tensor(above, pos_f[:].unsqueeze(2).to_broadcast([P, NT, READ_TILES + 1]),
                                    slot_edge[:].unsqueeze(1).to_broadcast([P, NT, READ_TILES + 1]),
                                    ALU.is_ge).then_inc(r_v, 1)
            dve.wait_ge(r_v, 23)
            nc.vector.tensor_reduce(n_above[:], above, AX, ALU.add).then_inc(r_v, 1)
            nc.vector.tensor_tensor(in_tile, above[:, :, 0:READ_TILES], above[:, :, 1:READ_TILES + 1],
                                    ALU.subtract).then_inc(r_v, 1)
            dve.wait_ge(r_v, 24)
            nc.vector.scalar_tensor_tensor(pos_lo[:], n_above[:], -float(P), pos_f[:], ALU.mult,
                                           ALU.add).then_inc(r_v, 1)
            dve.wait_ge(r_v, 25)
            nc.vector.tensor_tensor(ids[:, :, 0, :], in_tile,
                                    tile_edge[:].unsqueeze(2).to_broadcast([P, NT, READ_TILES]),
                                    ALU.mult).then_inc(r_id, 1)
            dve.wait_ge(r_v, 26)
            for b in range(B):
                nc.vector.tensor_tensor(in_slot[:, TB * b:TB * b + TB, :],
                                        pos_lo[:, TB * b:TB * b + TB].unsqueeze(2).to_broadcast([P, TB, P]),
                                        slot_no[:].unsqueeze(1).to_broadcast([P, TB, P]),
                                        ALU.is_equal).then_inc(r_slot, 1)
            nc.vector.tensor_copy(pos[:], pos_f[:]).then_inc(r_pos, 1)
            dve.wait_ge(r_inv, 1)
            nc.vector.tensor_reduce(token_f, x_bank[0][:, 0:2 * READ_TILES].rearrange("p (w k) -> p k w", w=2), AX,
                                    ALU.add).then_inc(r_v, 1)
            dve.wait_ge(r_v, 27)
            nc.vector.tensor_copy(token_of[:], token_f).then_inc(r_tok, 1)

            def lower_weights(e, s):
                dve.wait_ge(a_w2, e + 1)
                nc.vector.tensor_tensor(ew2_lo[:, s, :, :], ew2[:, s, :, :], ew2_hi[:, s, :, :].bitcast(F32),
                                        ALU.subtract).then_inc(v_w2, 1)

            def expert_tile(t, par):
                for q in range(2):
                    dve.wait_ge(m_sil, 2 * t + q + 1)
                    half = act_t[:, par, 4 * q:4 * q + 4, :]
                    nc.vector.tensor_tensor(flat(half), bank[2 + q][:], sil[:, q, :], ALU.mult).then_inc(m_act, 1)
                    dve.wait_ge(m_hi, 2 * t + q + 1)
                    nc.vector.tensor_tensor(act_lo[:, par, 4 * q:4 * q + 4, :], half,
                                            act_hi[:, par, 4 * q:4 * q + 4, :].bitcast(F32),
                                            ALU.subtract).then_inc(m_lo, 1)

            def expert_pair(i, first_pair):
                for par in range(2):
                    t = 2 * i + par
                    expert_tile(t, par)
                    if first_pair and par == 0:
                        lower_weights(1, 1)
                    else:
                        next_expert(dve, t, lower_weights)

            pairs = slot_pairs(dve)
            lower_weights(0, 0)
            expert_pair(0, True)
            with dve.Fori(1, SLOT_PAIRS) as i:
                with dve.If(i < pairs):
                    expert_pair(i, False)

            def add_experts(tiles):
                for t in tiles:
                    nc.vector.scalar_tensor_tensor(x_res[:, t, :], xn_all[:, t, :], weight[:, t:t + 1], x_res[:, t, :],
                                                   ALU.mult, ALU.add).then_inc(g_x, 1)

            for g in range(2):
                dve.wait_ge(g_y[g], 16 * len(GATHERS[g]))
                add_experts(GATHERS[g])
                dve.wait_ge(g_x, GATHERS[g].stop)
                row_stats(ln["l1"], 0, GATHERS[g])
            join_stats(ln["l1"], 1)
            norm_apply(ln["l1"], 1, 0, xn)
            for c in range(2):
                spread_values(1, c, s_bank[0][c])
            dve.wait_ge(g_y[2], 16 * TB)
            add_experts(GATHERS[2])
            dve.wait_ge(g_x, GATHERS[2].stop)
            norm_stats(ln["l1"], 2, TB)
            dve.wait_ge(v_vbd, 8)
            block_values(1, 0)
            scores(1, 0, 0)
            dve.wait_ge(att[1]["t_xt"], DK)
            norm_apply(ln["l1"], 2, TB, xn)
            sums(1, 0, 0)
            scores(1, 0, 1)
            dve.wait_ge(g_y[3], 16 * len(GATHERS[3]))
            add_experts(GATHERS[3][:TB])
            sums(1, 0, 1)
            add_experts(GATHERS[3][TB:])
            dve.wait_ge(g_x, NT)
            attention(1, 0, True, False)
            with dve.Fori(1, B - 1) as b:
                attention(1, b, False, False)
            attention(1, B - 1, False, True)

            def ff_hidden(t, i, first):
                par = i % 2
                one = slice(par, par + 1)
                if not first:
                    dve.wait_ge(f["hq"], t - 1)
                for c in range(2):
                    dve.wait_ge(f["a_sil"], 2 * t + c + 1)
                    nc.vector.scalar_tensor_tensor(h_f[:, par, 512 * c:512 * c + 512], bank[2 + c][:],
                                                   x_unit[:, 1, bass.ds(t, 1)], sil_g[:, par, 512 * c:512 * c + 512],
                                                   ALU.mult, ALU.mult).then_inc(f["v_h"], 1)
                dve.wait_ge(f["v_h"], 2 * t + 2)
                nc.vector.tensor_reduce(h_abs[:, one], h_f[:, par, :], AX, ALU.max,
                                        apply_absolute_value=True).then_inc(f["habs"], 1)
                dve.wait_ge(f["habs"], 2 * t + 1)
                nc.vector.tensor_scalar(h_abs[:, one], h_abs[:, one], 1.0 / 127.0, EPS / 127.0, ALU.mult,
                                        ALU.max).then_inc(f["habs"], 1)
                dve.wait_ge(f["habs"], 2 * t + 2)
                nc.vector.reciprocal(h_scale[:, one], h_abs[:, one]).then_inc(f["hinv"], 1)

            def ff_batch(b, first):
                for i in range(TB):
                    t = TB * b + i
                    ff_hidden(t, i, first and i < 2)
                    nc.vector.tensor_scalar(h_unit[:, i:i + 1], h_abs[:, i % 2:i % 2 + 1], wd_g[:, 0:1], None,
                                            ALU.mult).then_inc(f["hunit"], 1)
                    if first and i == 0:
                        norm_apply(ln["ff"], B, NT - TB, xn2)
                        row_scales(B - 1)

            dve.wait_ge(v_wd, 1)
            ff_batch(0, True)
            with dve.Fori(1, B) as b:
                ff_batch(b, False)


_INS = ["x", "ctx_768", "g_xattn", "g_ffn", "L0_xattn_Wq", "L0_xattn_bq", "L0_xattn_Wk", "L0_xattn_bk", "L0_xattn_Wv",
        "L0_xattn_bv", "L0_xattn_W1", "L0_xattn_b1", "L0_xattn_W2", "L0_xattn_b2", "L0_ffn_router_w",
        "L0_ffn_router_b", "L0_ffn_w1", "L0_ffn_w2", "L1_xattn_Wq", "L1_xattn_bq", "L1_xattn_Wk", "L1_xattn_bk",
        "L1_xattn_Wv", "L1_xattn_bv", "L1_xattn_Wo", "L1_xattn_bo", "L1_ffn_w_gate", "L1_ffn_w_up", "L1_ffn_w_down"]


def kernel(**inputs):
    import concourse.bacc as bacc
    from concourse.bass_utils import run_bass_kernel_spmd

    nc = bacc.Bacc("TRN2", target_bir_lowering=False, num_devices=1)
    arrays, inp = {}, {}
    for name in _INS:
        a = np.ascontiguousarray(inputs[name])
        arrays[f"in_{name}"] = a
        inp[name] = nc.dram_tensor(f"in_{name}", a.shape, mybir.dt.from_np(a.dtype), kind="ExternalInput").ap()
    out = nc.dram_tensor("out_rows", (B, N, D), F32, kind="ExternalOutput").ap()
    token_rows = nc.dram_tensor("token_rows", (NT * P, D), F32, kind="Internal").ap()
    slots_y = nc.dram_tensor("slots_y", (SLOT_TILES * P, D), F32, kind="Internal").ap()
    flamingo(nc, inp, out, token_rows, slots_y)
    r = run_bass_kernel_spmd(nc, [arrays], core_ids=[0])
    return r.results[0]["out_rows"]
```
